# Optimizing a Trainium2 kernel written in Bass

```python
import numpy as np
import jax
import jax.numpy as jnp

def _softmax(x, axis=-1):
    return jax.nn.softmax(x, axis=axis)

def _gelu(x):
    return jax.nn.gelu(x, approximate=True)

def _silu(x):
    return jax.nn.silu(x)

def _sigmoid(x):
    return jax.nn.sigmoid(x)

def _layernorm(x, axis=-1, eps=1e-05):
    m = jnp.mean(x, axis=axis, keepdims=True)
    v = jnp.var(x, axis=axis, keepdims=True)
    return (x - m) / jnp.sqrt(v + eps)

def _scatter_add(tgt, idx, src, axis=0):
    return tgt.at[idx].add(src)

def _segment_sum(src, seg, n):
    return jax.ops.segment_sum(src, seg, n)
kernel_name = 'mk_macaron_d1_jaxref_r4_99d15d'

def setup_inputs(seed: int=0):
    np.random.seed(seed)
    _w = jnp.asarray

    def _L0_attn_setup():
        import jax, jax.numpy as jnp
        import numpy as np
        HID = 256
        NH = 4
        DK = 64
        DV = 128
        C = 64
        EPS = 1e-05
        GLN = 16.0

        def _xavier(key, shape, gain=2 ** (-2.5)):
            fan_in, fan_out = shape
            lim = gain * np.sqrt(6.0 / (fan_in + fan_out))
            return jax.random.uniform(key, shape, jnp.float32, -lim, lim)

        def _chunk_simple_gla(q, k, v, g):
            B, H, N, dk = q.shape
            dv = v.shape[-1]
            nc = N // C
            scale = dk ** (-0.5)
            q = q.reshape(B, H, nc, C, dk) * scale
            k = k.reshape(B, H, nc, C, dk)
            v = v.reshape(B, H, nc, C, dv)
            g = g.reshape(B, H, nc, C)
            gc = jnp.cumsum(g, axis=-1)
            gt = gc[..., -1]
            dec = gc[..., :, None] - gc[..., None, :]
            mask = jnp.tril(jnp.ones((C, C), bool))
            A = jnp.einsum('bhntd,bhnsd->bhnts', q, k)
            A = A * jnp.where(mask, jnp.exp(jnp.where(mask, dec, 0.0)), 0.0)
            o_intra = jnp.einsum('bhnts,bhnsd->bhntd', A, v)
            qs = jnp.moveaxis(q, 2, 0)
            ks_ = jnp.moveaxis(k, 2, 0)
            vs = jnp.moveaxis(v, 2, 0)
            gcs = jnp.moveaxis(gc, 2, 0)
            gts = jnp.moveaxis(gt, 2, 0)
            S0 = jnp.zeros((B, H, dk, dv), q.dtype)

            def step(S, inp):
                qc, kc, vc, gcc, gtc = inp
                o_int = jnp.einsum('bhtd,bhde->bhte', qc * jnp.exp(gcc)[..., None], S)
                kd = kc * jnp.exp(gtc[..., None] - gcc)[..., None]
                S = jnp.exp(gtc)[..., None, None] * S + jnp.einsum('bhtd,bhte->bhde', kd, vc)
                return (S, o_int)
            _, o_inter = jax.lax.scan(step, S0, (qs, ks_, vs, gcs, gts))
            o = o_intra + jnp.moveaxis(o_inter, 0, 2)
            return o.reshape(B, H, N, dv)
        key = jax.random.key(seed)
        ks = jax.random.split(key, 8)
        x = jax.random.normal(ks[0], (4, 512, HID), jnp.float32)
        Wq = _xavier(ks[1], (HID, NH * DK))
        Wk = _xavier(ks[2], (HID, NH * DK))
        Wv = _xavier(ks[3], (HID, NH * DV))
        Wg = _xavier(ks[4], (HID, NH * DV))
        Wgk = _xavier(ks[5], (HID, NH))
        bgk = jnp.zeros((NH,), jnp.float32)
        Wo = _xavier(ks[6], (NH * DV, HID))
        gnorm_w = jnp.ones((DV,), jnp.float32)
        return {'x': x, 'Wq': Wq, 'Wk': Wk, 'Wv': Wv, 'Wg': Wg, 'Wgk': Wgk, 'bgk': bgk, 'Wo': Wo, 'gnorm_w': gnorm_w}
    _L0_attn_in = _L0_attn_setup()

    def _L0_ffn_setup():
        import jax, jax.numpy as jnp
        import numpy as np
        D = 256
        H = 512
        E = 8
        TOP_K = 2
        N_SHARED = 1
        B, S = (2, 256)
        key = jax.random.key(seed)
        ks = jax.random.split(key, 12)
        sc = 0.02
        return {'hidden': jax.random.normal(ks[0], (B, S, D), jnp.float32), 'router_w': jax.random.normal(ks[1], (D, E), jnp.float32) * sc, 'router_b': jnp.zeros((E,), jnp.float32), 'sw1': jax.random.normal(ks[2], (D, H), jnp.float32) * sc, 'sb1': jnp.zeros((H,), jnp.float32), 'sw2': jax.random.normal(ks[3], (H, D), jnp.float32) * sc, 'sb2': jnp.zeros((D,), jnp.float32), 'rw1': jax.random.normal(ks[4], (E, D, H), jnp.float32) * sc, 'rb1': jnp.zeros((E, H), jnp.float32), 'rw2': jax.random.normal(ks[5], (E, H, D), jnp.float32) * sc, 'rb2': jnp.zeros((E, D), jnp.float32)}
    _L0_ffn_in = _L0_ffn_setup()
    _d = {'L0_attn_x': _L0_attn_in['x'], 'L0_attn_Wq': _L0_attn_in['Wq'], 'L0_attn_Wk': _L0_attn_in['Wk'], 'L0_attn_Wv': _L0_attn_in['Wv'], 'L0_attn_Wg': _L0_attn_in['Wg'], 'L0_attn_Wgk': _L0_attn_in['Wgk'], 'L0_attn_bgk': _L0_attn_in['bgk'], 'L0_attn_Wo': _L0_attn_in['Wo'], 'L0_attn_gnorm_w': _L0_attn_in['gnorm_w'], 'L0_ffn_router_w': _L0_ffn_in['router_w'], 'L0_ffn_router_b': _L0_ffn_in['router_b'], 'L0_ffn_sw1': _L0_ffn_in['sw1'], 'L0_ffn_sb1': _L0_ffn_in['sb1'], 'L0_ffn_sw2': _L0_ffn_in['sw2'], 'L0_ffn_sb2': _L0_ffn_in['sb2'], 'L0_ffn_rw1': _L0_ffn_in['rw1'], 'L0_ffn_rb1': _L0_ffn_in['rb1'], 'L0_ffn_rw2': _L0_ffn_in['rw2'], 'L0_ffn_rb2': _L0_ffn_in['rb2']}
    _x0 = _d['L0_attn_x']
    _d['L0_attn_x'] = jax.random.normal(jax.random.fold_in(jax.random.key(seed), 1), (8, 512, 256), dtype=_x0.dtype)
    del _x0
    return _d

def reference(L0_attn_x, L0_attn_Wq, L0_attn_Wk, L0_attn_Wv, L0_attn_Wg, L0_attn_Wgk, L0_attn_bgk, L0_attn_Wo, L0_attn_gnorm_w, L0_ffn_router_w, L0_ffn_router_b, L0_ffn_sw1, L0_ffn_sb1, L0_ffn_sw2, L0_ffn_sb2, L0_ffn_rw1, L0_ffn_rb1, L0_ffn_rw2, L0_ffn_rb2):

    def _L0_attn_ref(x, Wq, Wk, Wv, Wg, Wgk, bgk, Wo, gnorm_w):
        import jax, jax.numpy as jnp
        import numpy as np
        HID = 256
        NH = 4
        DK = 64
        DV = 128
        C = 64
        EPS = 1e-05
        GLN = 16.0

        def _xavier(key, shape, gain=2 ** (-2.5)):
            fan_in, fan_out = shape
            lim = gain * np.sqrt(6.0 / (fan_in + fan_out))
            return jax.random.uniform(key, shape, jnp.float32, -lim, lim)

        def _chunk_simple_gla(q, k, v, g):
            B, H, N, dk = q.shape
            dv = v.shape[-1]
            nc = N // C
            scale = dk ** (-0.5)
            q = q.reshape(B, H, nc, C, dk) * scale
            k = k.reshape(B, H, nc, C, dk)
            v = v.reshape(B, H, nc, C, dv)
            g = g.reshape(B, H, nc, C)
            gc = jnp.cumsum(g, axis=-1)
            gt = gc[..., -1]
            dec = gc[..., :, None] - gc[..., None, :]
            mask = jnp.tril(jnp.ones((C, C), bool))
            A = jnp.einsum('bhntd,bhnsd->bhnts', q, k)
            A = A * jnp.where(mask, jnp.exp(jnp.where(mask, dec, 0.0)), 0.0)
            o_intra = jnp.einsum('bhnts,bhnsd->bhntd', A, v)
            qs = jnp.moveaxis(q, 2, 0)
            ks_ = jnp.moveaxis(k, 2, 0)
            vs = jnp.moveaxis(v, 2, 0)
            gcs = jnp.moveaxis(gc, 2, 0)
            gts = jnp.moveaxis(gt, 2, 0)
            S0 = jnp.zeros((B, H, dk, dv), q.dtype)

            def step(S, inp):
                qc, kc, vc, gcc, gtc = inp
                o_int = jnp.einsum('bhtd,bhde->bhte', qc * jnp.exp(gcc)[..., None], S)
                kd = kc * jnp.exp(gtc[..., None] - gcc)[..., None]
                S = jnp.exp(gtc)[..., None, None] * S + jnp.einsum('bhtd,bhte->bhde', kd, vc)
                return (S, o_int)
            _, o_inter = jax.lax.scan(step, S0, (qs, ks_, vs, gcs, gts))
            o = o_intra + jnp.moveaxis(o_inter, 0, 2)
            return o.reshape(B, H, N, dv)
        B, N, _ = x.shape
        q = (x @ Wq).reshape(B, N, NH, DK).transpose(0, 2, 1, 3)
        k = (x @ Wk).reshape(B, N, NH, DK).transpose(0, 2, 1, 3)
        v = (x @ Wv).reshape(B, N, NH, DV).transpose(0, 2, 1, 3)
        gk = (x @ Wgk + bgk).transpose(0, 2, 1)
        gk = jax.nn.log_sigmoid(gk) / GLN
        o = _chunk_simple_gla(q, k, v, gk)
        o = o.transpose(0, 2, 1, 3)
        g = (x @ Wg).reshape(B, N, NH, DV)
        on = o * jax.lax.rsqrt(jnp.mean(o * o, axis=-1, keepdims=True) + EPS) * gnorm_w
        o = on * (g * jax.nn.sigmoid(g))
        o = o.reshape(B, N, NH * DV)
        return o @ Wo

    def _L0_ffn_ref(hidden, router_w, router_b, sw1, sb1, sw2, sb2, rw1, rb1, rw2, rb2):
        import jax, jax.numpy as jnp
        import numpy as np
        D = 256
        H = 512
        E = 8
        TOP_K = 2
        N_SHARED = 1
        B, S = (2, 256)
        b, s, d = hidden.shape
        T = b * s
        flat = hidden.reshape(T, d)
        router_logits = flat @ router_w + router_b
        router_probs = jax.nn.softmax(router_logits, axis=-1)
        topk_probs, topk_idx = jax.lax.top_k(router_probs, TOP_K)
        weights = jnp.zeros_like(router_probs).at[jnp.arange(T)[:, None], topk_idx].add(topk_probs)
        sh = jax.nn.gelu(flat @ sw1 + sb1, approximate=False)
        shared_out = (sh @ sw2 + sb2) / N_SHARED
        h1 = jax.nn.gelu(jnp.einsum('td,edh->teh', flat, rw1) + rb1[None], approximate=False)
        expert_out = jnp.einsum('teh,ehd->ted', h1, rw2) + rb2[None]
        mixed = jnp.einsum('ted,te->td', expert_out, weights)
        return (shared_out + mixed).reshape(b, s, d)
    x = L0_attn_x
    x = x + 0.5 * _L0_ffn_ref(_layernorm(x, axis=-1), L0_ffn_router_w, L0_ffn_router_b, L0_ffn_sw1, L0_ffn_sb1, L0_ffn_sw2, L0_ffn_sb2, L0_ffn_rw1, L0_ffn_rb1, L0_ffn_rw2, L0_ffn_rb2)
    x = x + _L0_attn_ref(_layernorm(x, axis=-1), L0_attn_Wq, L0_attn_Wk, L0_attn_Wv, L0_attn_Wg, L0_attn_Wgk, L0_attn_bgk, L0_attn_Wo, L0_attn_gnorm_w)
    x = x + 0.5 * _L0_ffn_ref(_layernorm(x, axis=-1), L0_ffn_router_w, L0_ffn_router_b, L0_ffn_sw1, L0_ffn_sb1, L0_ffn_sw2, L0_ffn_sb2, L0_ffn_rw1, L0_ffn_rb1, L0_ffn_rw2, L0_ffn_rb2)
    return x

_drawn_inputs = setup_inputs


def setup_inputs(seed=0):
    import zlib

    import numpy as np

    out = dict(_drawn_inputs(seed))
    spreads = {'L0_attn_bgk': (0.0, 0.8),
     'L0_attn_gnorm_w': (1.0, 0.6),
     'L0_ffn_router_b': (0.0, 0.613),
     'L0_ffn_sb1': (0.0, 0.334),
     'L0_ffn_sb2': (0.0, 0.1),
     'L0_ffn_rb1': (0.0, 0.8),
     'L0_ffn_rb2': (0.0, 0.319)}
    factors = {'L0_attn_Wq': 3.759,
     'L0_attn_Wk': 3.733,
     'L0_attn_Wv': 3.744,
     'L0_attn_Wg': 3.745,
     'L0_attn_Wgk': 8.0,
     'L0_attn_Wo': 3.741,
     'L0_ffn_rw1': 2.929,
     'L0_ffn_rw2': 2.715}
    for name, (base, spread) in spreads.items():
        noise = np.random.default_rng([zlib.crc32(name.encode()), seed]).standard_normal(out[name].shape)
        drawn = base * np.exp(spread * noise) if base else spread * noise
        out[name] = jnp.asarray(drawn.astype(out[name].dtype))
    for name, factor in factors.items():
        out[name] = (out[name] * factor).astype(out[name].dtype)
    return out
```

```python
from contextlib import ExitStack

import concourse.bass as bass
from concourse import mybir

P = 128
F32 = mybir.dt.float32
F32R = mybir.dt.float32r
ALU = mybir.AluOpType
ACT = mybir.ActivationFunctionType
AX_X = mybir.AxisListType.X

T = 4096
D = 256
TILES = T // P
GT = 4
G = TILES // GT
GN = GT * P
KD = D // P
H = 512
KH = H // P
E = 8
NX = E + 1
EPS = 1e-5
B = 8
NH, DK, DV = 4, 64, 128
WALL = 2 * NH * DK + 2 * NH * DV
GLN = 16.0
NEVER = -1e4


def wait_apart(eng, k, sem, value):
    eng.wait_ge(sem, value)
    eng.sem_inc(k.passed, 1)


class Core:
    pass


def constants(nc, k, dram):
    with ExitStack() as ctx:
        x_in = ctx.enter_context(nc.semaphore("x_in"))
        small_in = ctx.enter_context(nc.semaphore("small_in"))
        zeroed = ctx.enter_context(nc.semaphore("zeroed"))
        built = ctx.enter_context(nc.semaphore("built"))
        turned = ctx.enter_context(nc.semaphore("turned"))
        b1_rows = ctx.enter_context(nc.sbuf_tensor("b1_rows", [NX * KH, P], F32))
        ps = ctx.enter_context(nc.psum_tensor("const_ps", [P, 512], F32))
        block = ctx.enter_context(nc.Block())
        x_rows = dram["x"].rearrange("b n d -> (b n) d").rearrange("(t p) d -> p t d", p=P)

        @block.sync
        def _(sp):
            for g in range(4):
                sp.dma_start(k.x[:, 8 * g:8 * g + 8, :], x_rows[:, 8 * g:8 * g + 8, :]).then_inc(x_in, 16)
            sp.wait_ge(x_in, 64)

        @block.scalar
        def _(act):
            act.dma_start(b1_rows[0:KH, :], dram["sb1"].rearrange("(c p) -> c p", p=P)).then_inc(small_in, 16)
            act.dma_start(b1_rows[KH:NX * KH, :],
                          dram["rb1"].rearrange("e (c p) -> (e c) p", p=P)).then_inc(small_in, 16)
            act.dma_start(k.router_w[:, :, :], dram["router_w"].rearrange("(k p) e -> p k e", p=P)).then_inc(small_in, 16)
            act.dma_start(k.router_b[:, :], dram["router_b"].rearrange("(o e) -> o e", o=1).to_broadcast([P, E])
                          ).then_inc(small_in, 16)
            act.wait_ge(zeroed, 4)
            for t in range(GT):
                act.dma_start(k.b2_blocks[32 * t:32 * t + 1, t, :],
                              dram["sb2"].rearrange("(o d) -> o d", o=1)).then_inc(small_in, 16)
                act.dma_start(k.b2_blocks[32 * t + 1:32 * t + NX, t, :], dram["rb2"]).then_inc(small_in, 16)
            act.wait_ge(small_in, 16 * (4 + 2 * GT))

        @block.gpsimd
        def _(pool):
            pool.memset(k.ident[:, :], 0.0).then_inc(zeroed, 1)
            pool.memset(k.neg_half[:, :], -0.5).then_inc(zeroed, 1)
            pool.memset(k.b2_blocks[:, :, :], 0.0).then_inc(zeroed, 1)
            pool.memset(k.gate_pad[:, :, :, :], 0.0).then_inc(zeroed, 1)
            pool.wait_ge(zeroed, 4)
            pool.affine_select(out=k.ident[:, :], in_=k.ident[:, :], compare_op=ALU.not_equal, fill=1.0,
                               base=0, pattern=[[-1, P]], channel_multiplier=1).then_inc(built, 1)

        @block.tensor
        def _(pe):
            pe.wait_ge(built, 1)
            pe.wait_ge(small_in, 16 * (4 + 2 * GT))
            pe.transpose(ps[:, 0:NX * KH], b1_rows[:, :], k.ident[0:NX * KH, 0:NX * KH]).then_inc(turned, 1)

        @block.vector
        def _(dve):
            dve.wait_ge(turned, 1)
            dve.tensor_copy(k.b1[:, :, :], ps[:, 0:NX * KH].rearrange("p (x c) -> p x c", x=NX)).then_inc(built, 1)


def normalise(nc, k, name, after_logits=None):
    with ExitStack() as ctx:
        def sem(n):
            return ctx.enter_context(nc.semaphore(f"{name}_{n}"))

        def sb(n, shape, dt=F32):
            return ctx.enter_context(nc.sbuf_tensor(f"{name}_{n}", shape, dt))

        stats = sb("stats", [P, 2, GT, 6])
        mean_var = sb("mean_var", [P, 2, GT, 2])
        var_eps = sb("var_eps", [P, 2, GT])
        rstd = sb("rstd", [P, 2, GT])
        xn = sb("xn", [P, 2, GT, D])
        xT32 = sb("xT32", [P, 2, KD, GN])
        logits = sb("logits", [P, TILES, E])
        top = sb("top", [P, TILES])
        probs = sb("probs", [P, TILES, E])
        total = sb("total", [P, TILES])
        beats = sb("beats", [P, E, TILES, E])
        rank = sb("rank", [P, TILES, E])
        gateT = sb("gateT", [P, 2, P])
        turn_ps = ctx.enter_context(nc.psum_tensor(f"{name}_turn_ps", [P, 2, KD, 512], F32))
        logit_ps = ctx.enter_context(nc.psum_tensor(f"{name}_logit_ps", [P, 512], F32))
        bias_ps = ctx.enter_context(nc.psum_tensor(f"{name}_bias_ps", [P, 2, 512], F32))

        stats_done, agg_done, rstd_done, eps_done = sem("stats_done"), sem("agg_done"), sem("rstd_done"), sem("eps_done")
        xn_done, turned, copied = sem("xn_done"), sem("turned"), sem("copied")
        hi_done, lo_done, logits_done = sem("hi_done"), sem("lo_done"), sem("logits_done")
        chain, exp_in, exp_out, diag_zero = sem("chain"), sem("exp_in"), sem("exp_out"), sem("diag_zero")
        gate_turned, gate_copied, bias_done, bias_added = sem("gate_turned"), sem("gate_copied"), sem("bias_done"), sem("bias_added")
        gate_staged = sem("gate_staged")
        block = ctx.enter_context(nc.Block())

        @block.gpsimd
        def _(pool):
            pool.memset(beats[:, :, :, :], 0.0).then_inc(diag_zero, 1)

            def rsqrt(g, p):
                wait_apart(pool, k, agg_done, g + 1)
                pool.tensor_scalar(var_eps[:, p, :], mean_var[:, p, :, 1], EPS, None, ALU.add).then_inc(eps_done, 1)
                pool.wait_ge(eps_done, g + 1)
                pool.tensor_tensor(rstd[:, p, :], var_eps[:, p, :], k.neg_half[:, 0:GT], ALU.pow).then_inc(rstd_done, 1)

            with pool.Fori(0, G // 2) as j:
                rsqrt(2 * j, 0)
                rsqrt(2 * j + 1, 1)

        @block.vector
        def _(dve):
            def statistics(g, p):
                for t in range(GT):
                    last = dve.bn_stats(stats[:, p, t, :], k.x[:, GT * g + t, :])
                last.then_inc(stats_done, 1)
                wait_apart(dve, k, stats_done, g + 1)
                for t in range(GT):
                    last = dve.bn_aggr(mean_var[:, p, t, :], stats[:, p, t, :])
                last.then_inc(agg_done, 1)

            def scale(g, p, reuse):
                if reuse:
                    dve.wait_ge(turned, g - 1)
                dve.wait_ge(rstd_done, g + 1)
                for t in range(GT):
                    last = dve.tensor_scalar(xn[:, p, t, :], k.x[:, GT * g + t, :], mean_var[:, p, t, 0:1],
                                             rstd[:, p, t:t + 1], ALU.subtract, ALU.mult)
                last.then_inc(xn_done, 1)

            def split(g, p):
                dve.wait_ge(copied, g + 1)
                hi = k.xT_hi[:, :, bass.ds(g * GN, GN)]
                dve.tensor_copy(hi, xT32[:, p, :, :]).then_inc(hi_done, 1)
                dve.wait_ge(hi_done, g + 1)
                dve.tensor_tensor(k.xT_lo[:, :, bass.ds(g * GN, GN)], xT32[:, p, :, :], hi.bitcast(F32),
                                  ALU.subtract).then_inc(lo_done, 1)

            def pair(g, reuse):
                statistics(g + 1, 1)
                scale(g + 1, 1, reuse)
                split(g, 0)
                statistics(g + 2, 0)
                scale(g + 2, 0, True)
                split(g + 1, 1)

            statistics(0, 0)
            scale(0, 0, False)
            pair(0, False)
            with dve.Fori(1, G // 2 - 1) as j:
                pair(2 * j, True)
            statistics(G - 1, 1)
            scale(G - 1, 1, True)
            split(G - 2, 0)
            split(G - 1, 1)

            links = [0]

            def link(ins):
                links[0] += 1
                ins.then_inc(chain, 1)
                dve.wait_ge(chain, links[0])

            dve.wait_ge(logits_done, G)
            link(dve.tensor_tensor(logits[:, :, :], logit_ps[:, 0:TILES * E].rearrange("p (t e) -> p t e", e=E),
                                   k.router_b[:, :].unsqueeze(1).to_broadcast([P, TILES, E]), ALU.add))
            link(dve.tensor_reduce(top[:, :], logits[:, :, :], AX_X, ALU.max))
            dve.tensor_tensor(probs[:, :, :], logits[:, :, :], top[:, :].unsqueeze(2).to_broadcast([P, TILES, E]),
                              ALU.subtract).then_inc(exp_in, 1)
            dve.wait_ge(diag_zero, 1)
            for j in range(E):
                rival = logits[:, :, j:j + 1]
                if j:
                    last = dve.tensor_tensor(beats[:, j, :, 0:j], rival.to_broadcast([P, TILES, j]),
                                             logits[:, :, 0:j], ALU.is_gt)
                if j < E - 1:
                    last = dve.tensor_tensor(beats[:, j, :, j + 1:E], rival.to_broadcast([P, TILES, E - 1 - j]),
                                             logits[:, :, j + 1:E], ALU.is_ge)
            link(last)
            link(dve.tensor_reduce(rank[:, :, :], beats[:, :, :, :].rearrange("p j t e -> p t e j"), AX_X, ALU.add))
            link(dve.tensor_scalar(rank[:, :, :], rank[:, :, :], 2.0, 0.5, ALU.is_lt, ALU.mult))
            dve.wait_ge(exp_out, 1)
            link(dve.tensor_reduce(total[:, :], probs[:, :, :], AX_X, ALU.add))
            link(dve.reciprocal(total[:, :], total[:, :]))
            link(dve.tensor_tensor(probs[:, :, :], probs[:, :, :], total[:, :].unsqueeze(2).to_broadcast([P, TILES, E]),
                                   ALU.mult))
            link(dve.tensor_tensor(k.gate[:, :, 1:NX], probs[:, :, :], rank[:, :, :], ALU.mult))
            link(dve.memset(k.gate[:, :, 0:1], 0.5))

            def stage(g, p, reuse):
                if reuse:
                    dve.wait_ge(gate_turned, g - 1)
                dve.tensor_copy(k.gate_pad[:, p, :, 0:NX], k.gate[:, bass.ds(GT * g, GT), :]).then_inc(gate_staged, 1)

            def turn_copy(g, p, reuse):
                dve.wait_ge(gate_turned, g + 1)
                if reuse:
                    dve.wait_ge(bias_done, g - 1)
                dve.tensor_copy(gateT[:, p, :], turn_ps[:, p, 0, 0:P]).then_inc(gate_copied, 1)

            def add_bias(g):
                dve.wait_ge(bias_done, g + 1)
                xg = k.x[:, bass.ds(GT * g, GT), :]
                dve.tensor_tensor(xg, bias_ps[:, :, :].rearrange("p a (b d) -> p (a b) d", b=2), xg,
                                  ALU.add).then_inc(bias_added, 1)

            stage(0, 0, False)
            stage(1, 1, False)
            for g in range(2):
                turn_copy(g, g, False)
                add_bias(g)
            with dve.Fori(1, G // 2) as j:
                stage(2 * j, 0, True)
                stage(2 * j + 1, 1, True)
                turn_copy(2 * j, 0, True)
                add_bias(2 * j)
                turn_copy(2 * j + 1, 1, True)
                add_bias(2 * j + 1)

        @block.tensor
        def _(pe):
            def turn(g, p, reuse):
                pe.wait_ge(xn_done, g + 1)
                if reuse:
                    pe.wait_ge(copied, g - 1)
                for kd in range(KD):
                    for t in range(GT):
                        last = pe.transpose(turn_ps[:, p, kd, t * P:(t + 1) * P], xn[:, p, t, kd * P:(kd + 1) * P],
                                            k.ident[:, :])
                last.then_inc(turned, 1)

            def route(g, p):
                pe.wait_ge(copied, g + 1)
                for t in range(GT):
                    for kd in range(KD):
                        last = pe.matmul(logit_ps[:, bass.ds((GT * g + t) * E, E)], xT32[:, p, kd, t * P:(t + 1) * P],
                                         k.router_w[:, kd, :], start=(kd == 0), stop=(kd == KD - 1))
                last.then_inc(logits_done, 1)

            turn(0, 0, False)
            turn(1, 1, False)
            route(0, 0)
            route(1, 1)
            with pe.Fori(1, G // 2) as j:
                turn(2 * j, 0, True)
                turn(2 * j + 1, 1, True)
                route(2 * j, 0)
                route(2 * j + 1, 1)

            def gate_turn(g, p, reuse):
                pe.wait_ge(gate_staged, g + 1)
                if reuse:
                    pe.wait_ge(gate_copied, g - 1)
                pe.transpose(turn_ps[:, p, 0, 0:P], k.gate_pad[:, p, :, :].rearrange("p t e -> p (t e)"),
                             k.ident[:, :]).then_inc(gate_turned, 1)

            def gate_bias(g, p, reuse):
                pe.wait_ge(gate_copied, g + 1)
                if reuse:
                    pe.wait_ge(bias_added, g)
                for half in range(2):
                    last = pe.matmul(bias_ps[:, half, :], gateT[:, p, :],
                                     k.b2_blocks[:, 2 * half:2 * half + 2, :].rearrange("p t d -> p (t d)"),
                                     start=True, stop=True)
                last.then_inc(bias_done, 1)

            gate_turn(0, 0, False)
            gate_turn(1, 1, False)
            gate_bias(0, 0, False)
            gate_bias(1, 1, True)
            with pe.Fori(1, G // 2) as j:
                gate_turn(2 * j, 0, True)
                gate_turn(2 * j + 1, 1, True)
                gate_bias(2 * j, 0, True)
                gate_bias(2 * j + 1, 1, True)

        @block.scalar
        def _(act):
            def copy(g, p, reuse):
                act.wait_ge(turned, g + 1)
                if reuse:
                    act.wait_ge(logits_done, g - 1)
                    act.wait_ge(lo_done, g - 1)
                for kd in range(KD):
                    last = act.activation(xT32[:, p, kd, :], turn_ps[:, p, kd, :], ACT.Copy)
                last.then_inc(copied, 1)

            copy(0, 0, False)
            copy(1, 1, False)
            with act.Fori(1, G // 2) as j:
                copy(2 * j, 0, True)
                copy(2 * j + 1, 1, True)
            act.wait_ge(exp_in, 1)
            act.activation(probs[:, :, :], probs[:, :, :], ACT.Exp).then_inc(exp_out, 1)


def experts(nc, k, dram, name):
    with ExitStack() as ctx:
        def sem(n):
            return ctx.enter_context(nc.semaphore(f"{name}_{n}"))

        def sb(n, shape, dt=F32):
            return ctx.enter_context(nc.sbuf_tensor(f"{name}_{n}", shape, dt))

        w1_in = sb("w1_in", [P, KD, H])
        w2_in = sb("w2_in", [P, KH, D])
        w1_hi, w1_lo = sb("w1_hi", [P, KD, H], F32R), sb("w1_lo", [P, KD, H], F32R)
        w2_hi, w2_lo = sb("w2_hi", [P, KH, D], F32R), sb("w2_lo", [P, KH, D], F32R)
        h32 = sb("h32", [P, KH, GN])
        h_hi, h_lo = sb("h_hi", [P, KH, GN], F32R), sb("h_lo", [P, KH, GN], F32R)
        hid_ps = ctx.enter_context(nc.psum_tensor(f"{name}_hid_ps", [P, KH, GN], F32))
        out_ps = ctx.enter_context(nc.psum_tensor(f"{name}_out_ps", [P, GT, 512], F32))

        w1_loaded, w2_loaded = sem("w1_loaded"), sem("w2_loaded")
        w1_hi_done, w1_split, w2_hi_done, w2_split = sem("w1_hi_done"), sem("w1_split"), sem("w2_hi_done"), sem("w2_split")
        hid_done, gelu_done, h_hi_done, h_split = sem("hid_done"), sem("gelu_done"), sem("h_hi_done"), sem("h_split")
        chunk_used, out_done, out_added = sem("chunk_used"), sem("out_done"), sem("out_added")
        block = ctx.enter_context(nc.Block())
        w1_dram = dram["rw1"].rearrange("e (k p) h -> e p k h", p=P)
        w2_dram = dram["rw2"].rearrange("e (k p) d -> e p k d", p=P)

        @block.sync
        def _(sp):
            sp.dma_start(w1_in[:, :, :], dram["sw1"].rearrange("(k p) h -> p k h", p=P)).then_inc(w1_loaded, 16)
            sp.dma_start(w2_in[:, :, :], dram["sw2"].rearrange("(k p) d -> p k d", p=P)).then_inc(w2_loaded, 16)
            with sp.Fori(0, E) as e:
                sp.wait_ge(w1_split, e + 1)
                sp.dma_start(w1_in[:, :, :], w1_dram[bass.ds(e, 1)].rearrange("o p k h -> p (o k) h")).then_inc(w1_loaded, 16)
                sp.wait_ge(w2_split, e + 1)
                sp.dma_start(w2_in[:, :, :], w2_dram[bass.ds(e, 1)].rearrange("o p k d -> p (o k) d")).then_inc(w2_loaded, 16)

        @block.scalar
        def _(act):
            def w1_high(e, reuse):
                act.wait_ge(w1_loaded, 16 * e + 16)
                if reuse:
                    act.wait_ge(hid_done, KH * G * e)
                act.activation(w1_hi[:, :, :], w1_in[:, :, :], ACT.Copy).then_inc(w1_hi_done, 1)

            def w2_high(e, reuse):
                act.wait_ge(w2_loaded, 16 * e + 16)
                if reuse:
                    act.wait_ge(out_done, GT * G * e)
                act.activation(w2_hi[:, :, :], w2_in[:, :, :], ACT.Copy).then_inc(w2_hi_done, 1)

            def hidden(e, i, reuse):
                for c in range(KH):
                    if reuse:
                        act.wait_ge(h_split, KH * (i - 1) + c + 1)
                    wait_apart(act, k, hid_done, KH * i + c + 1)
                    act.activation(h32[:, c, :], hid_ps[:, c, :], ACT.Gelu,
                                   bias=k.b1[:, e, c:c + 1] if isinstance(e, int) else k.b1[:, bass.ds(e, 1), c]
                                   ).then_inc(gelu_done, 1)
                for c in range(KH):
                    act.wait_ge(gelu_done, KH * i + c + 1)
                    if reuse and c < KH - 1:
                        act.wait_ge(chunk_used, (KH - 1) * (i - 1) + c + 1)
                    elif reuse:
                        act.wait_ge(out_done, GT * i)
                    act.activation(h_hi[:, c, :], h32[:, c, :], ACT.Copy).then_inc(h_hi_done, 1)

            w1_high(0, False)
            w2_high(0, False)
            hidden(0, 0, False)
            with act.Fori(1, G) as g:
                hidden(0, g, True)
            with act.Fori(1, NX) as e:
                w1_high(e, True)
                hidden(e, G * e, True)
                w2_high(e, True)
                with act.Fori(1, G) as g:
                    hidden(e, G * e + g, True)

        @block.vector
        def _(dve):
            def w1_low(e):
                dve.wait_ge(w1_hi_done, e + 1)
                dve.tensor_tensor(w1_lo[:, :, :], w1_in[:, :, :], w1_hi[:, :, :].bitcast(F32),
                                  ALU.subtract).then_inc(w1_split, 1)

            def w2_low(e):
                dve.wait_ge(w2_hi_done, e + 1)
                dve.tensor_tensor(w2_lo[:, :, :], w2_in[:, :, :], w2_hi[:, :, :].bitcast(F32),
                                  ALU.subtract).then_inc(w2_split, 1)

            def low(i):
                for c in range(KH):
                    dve.wait_ge(h_hi_done, KH * i + c + 1)
                    dve.tensor_tensor(h_lo[:, c, :], h32[:, c, :], h_hi[:, c, :].bitcast(F32),
                                      ALU.subtract).then_inc(h_split, 1)

            def add(e, g, i):
                for t in range(GT):
                    dve.wait_ge(out_done, GT * i + t + 1)
                    xt = k.x[:, GT * g + t, :]
                    dve.scalar_tensor_tensor(out=xt, in0=out_ps[:, t, 0:D], scalar=k.gate[:, GT * g + t, bass.ds(e, 1)],
                                             in1=xt, op0=ALU.mult, op1=ALU.add).then_inc(out_added, 1)

            w1_low(0)
            w2_low(0)
            low(0)
            with dve.Fori(1, G) as g:
                low(g)
                add(0, g - 1, g - 1)
            with dve.Fori(1, NX) as e:
                w1_low(e)
                low(G * e)
                add(e - 1, G - 1, G * e - 1)
                w2_low(e)
                with dve.Fori(1, G) as g:
                    low(G * e + g)
                    add(e, g - 1, G * e + g - 1)
            add(E, G - 1, NX * G - 1)

        @block.tensor
        def _(pe):
            def first(g, i, reuse):
                for c in range(KH):
                    if reuse:
                        pe.wait_ge(gelu_done, KH * (i - 1) + c + 1)
                    passes = [(w, x, kd) for kd in range(KD)
                              for w, x in ((w1_hi, k.xT_hi), (w1_hi, k.xT_lo), (w1_lo, k.xT_hi))]
                    for n, (w, x, kd) in enumerate(passes):
                        last = pe.matmul(hid_ps[:, c, :], w[:, kd, c * P:(c + 1) * P], x[:, kd, bass.ds(g * GN, GN)],
                                         start=(n == 0), stop=(n == len(passes) - 1))
                    last.then_inc(hid_done, 1)

            def second(i, reuse):
                for c in range(KH):
                    pe.wait_ge(h_split, KH * i + c + 1)
                    for t in range(GT):
                        if reuse and c == 0:
                            pe.wait_ge(out_added, GT * (i - 1) + t + 1)
                        for n, (h, w) in enumerate(((h_hi, w2_hi), (h_hi, w2_lo), (h_lo, w2_hi))):
                            last = pe.matmul(out_ps[:, t, 0:D], h[:, c, t * P:(t + 1) * P], w[:, c, :],
                                             start=(c == 0 and n == 0), stop=(c == KH - 1 and n == 2))
                        if c == KH - 1:
                            last.then_inc(out_done, 1)
                    if c < KH - 1:
                        last.then_inc(chunk_used, 1)

            pe.wait_ge(w1_split, 1)
            first(0, 0, False)
            pe.wait_ge(w2_split, 1)
            first(1, 1, True)
            second(0, False)
            with pe.Fori(2, G) as g:
                first(g, g, True)
                second(g - 1, True)
            with pe.Fori(1, NX) as e:
                pe.wait_ge(w1_split, e + 1)
                first(0, G * e, True)
                second(G * e - 1, True)
                first(1, G * e + 1, True)
                pe.wait_ge(w2_split, e + 1)
                second(G * e, True)
                with pe.Fori(2, G) as g:
                    first(g, G * e + g, True)
                    second(G * e + g - 1, True)
            second(NX * G - 1, True)


def attention(nc, k, dram):
    with ExitStack() as ctx:
        def sem(n):
            return ctx.enter_context(nc.semaphore(f"attn_{n}"))

        def sb(n, shape, dt=F32):
            return ctx.enter_context(nc.sbuf_tensor(f"attn_{n}", shape, dt))

        def bank(n):
            return ctx.enter_context(nc.psum_tensor(f"attn_{n}_ps", [P, 512], F32))

        w_in = sb("w_in", [P, KD, WALL])
        w_hi, w_lo = sb("w_hi", [P, KD, WALL], F32R), sb("w_lo", [P, KD, WALL], F32R)
        wo_in, wo_scaled = sb("wo_in", [P, NH, D]), sb("wo_scaled", [P, NH, D])
        wo_hi, wo_lo = sb("wo_hi", [P, NH, D], F32R), sb("wo_lo", [P, NH, D], F32R)
        gnorm = sb("gnorm", [P, 1])
        wgk = sb("wgk", [P, KD, NH])
        bgk = sb("bgk", [P, NH])
        ones = sb("ones", [P, P])
        upto = sb("upto", [P, P])
        causal = sb("causal", [P, P])
        stats = sb("stats", [P, GT, 6])
        mean_var = sb("mean_var", [P, GT, 2])
        var_eps = sb("var_eps", [P, GT])
        rstd = sb("rstd", [P, GT])
        xn = sb("xn", [P, GT, D])
        xT32 = sb("xT32", [P, KD, GN])
        xT_hi, xT_lo = sb("xT_hi", [P, KD, GN], F32R), sb("xT_lo", [P, KD, GN], F32R)
        z = sb("z", [P, GT, NH])
        z_min = sb("z_min", [P, GT, NH])
        z_abs = sb("z_abs", [P, GT, NH])
        z_exp = sb("z_exp", [P, GT, NH])
        z_log = sb("z_log", [P, GT, NH])
        decay = sb("decay", [P, GT, NH])
        kT = sb("kT", [P, 2, GN])
        q_pad = sb("q_pad", [P, 2, 2, GN])
        steps = sb("steps", [P, 2, NH, P])
        cum = sb("cum", [P, NH, P])
        cum_exp = sb("cum_exp", [P, 2, NH, P])
        cum_col = sb("cum_col", [P, NH])
        gap = sb("gap", [P, NH, P])
        gap_exp = sb("gap_exp", [P, NH, P])
        k_gap = sb("k_gap", [P, NH])
        k_fac = sb("k_fac", [P, NH])
        q_dec = sb("q_dec", [P, 2, 2, P])
        k_dec = sb("k_dec", [P, 2, NH, DK])
        v32 = sb("v32", [P, 2, NH * DV])
        score = sb("score", [P, 2, NH, P])
        tanh_g = sb("tanh_g", [P, NH * DV])
        gate = sb("gate", [P, 2, NH * DV])
        state = sb("state", [P, 2, 2, DV])
        o32 = sb("o32", [P, NH * DV])
        o_sq = sb("o_sq", [P, NH, DV])
        o_sum = sb("o_sum", [P, NH])
        o_mean = sb("o_mean", [P, NH])
        o_rstd = sb("o_rstd", [P, NH])
        o_gated = sb("o_gated", [P, NH * DV])
        oT_hi, oT_lo = sb("oT_hi", [P, NH * P], F32R), sb("oT_lo", [P, NH * P], F32R)
        cum_ps, score_ps, v_ps, g_ps = bank("cum"), bank("score"), bank("v"), bank("g")
        o_ps, s_ps, y_ps, k_ps = bank("o"), bank("s"), bank("y"), bank("k")
        COL, GK = NH * DK, NH * DK + 16

        loaded, w_hi_done, w_ready = sem("loaded"), sem("w_hi_done"), sem("w_ready")
        const_made, const_ready, wo_scaled_done = sem("const_made"), sem("const_ready"), sem("wo_scaled_done")
        stats_done, agg_done, eps_done, rstd_done = sem("stats_done"), sem("agg_done"), sem("eps_done"), sem("rstd_done")
        xn_done, turned, copied, hi_done, split_done = (sem("xn_done"), sem("turned"), sem("copied"), sem("hi_done"),
                                                        sem("split_done"))
        gk_done, z_done, z_abs_done, z_exp_done, z_log_done, z_min_done, log_sig_done, decay_done = (
            sem("gk_done"), sem("z_done"), sem("z_abs_done"), sem("z_exp_done"), sem("z_log_done"), sem("z_min_done"),
            sem("log_sig_done"), sem("decay_done"))
        qk_done, qk_copied = sem("qk_done"), sem("qk_copied")
        steps_done, k_done, score_done, cum_done, v_done, g_done = (
            sem("steps_done"), sem("k_done"), sem("score_done"), sem("cum_done"), sem("v_done"), sem("g_done"))
        cum_copied, cum_exp_done, col_copied, gap_done, gap_exp_done = (
            sem("cum_copied"), sem("cum_exp_done"), sem("col_copied"), sem("gap_done"), sem("gap_exp_done"))
        k_gap_done, k_fac_done, v_copied, tanh_done = sem("k_gap_done"), sem("k_fac_done"), sem("v_copied"), sem("tanh_done")
        q_dec_done, k_dec_done, masked, gated = sem("q_dec_done"), sem("k_dec_done"), sem("masked"), sem("gated")
        s_done, o_done, state_done = sem("s_done"), sem("o_done"), sem("state_done")
        o_copied, sq_done, sum_done, mean_done, o_rstd_done, o_gated_done = (
            sem("o_copied"), sem("sq_done"), sem("sum_done"), sem("mean_done"), sem("o_rstd_done"), sem("o_gated_done"))
        oT_done, oT_hi_done, oT_split, y_done, y_added = (
            sem("oT_done"), sem("oT_hi_done"), sem("oT_split"), sem("y_done"), sem("y_added"))
        block = ctx.enter_context(nc.Block())

        def states(b, c):
            return (GT - 1) * b + min(c + 1, GT - 1)

        def schedule(eng, slot, drain):
            for c in range(GT):
                slot(0, c, True)
            with eng.Fori(1, B - 1) as b:
                for c in range(GT):
                    slot(b, c, True)
            for c in range(GT):
                slot(B - 1, c, False)
            drain()

        def before(b, c, back):
            if c >= back:
                return b, c - back
            if isinstance(b, int) and b == 0:
                return None
            return b - 1, c - back + GT

        @block.sync
        def _(sp):
            for n, (name, width) in enumerate((("Wq", 256), ("Wk", 256), ("Wv", 512), ("Wg", 512))):
                at = (0, 256, 512, 1024)[n]
                sp.dma_start(w_in[:, :, at:at + width], dram[name].rearrange("(k p) n -> p k n", p=P)).then_inc(loaded, 16)
            sp.dma_start(wo_in[:, :, :], dram["Wo"].rearrange("(h p) d -> p h d", p=P)).then_inc(loaded, 16)
            sp.dma_start(gnorm[:, :], dram["gnorm_w"].rearrange("(p o) -> p o", o=1)).then_inc(loaded, 16)
            sp.dma_start(wgk[:, :, :], dram["Wgk"].rearrange("(k p) h -> p k h", p=P)).then_inc(loaded, 16)
            sp.dma_start(bgk[:, :], dram["bgk"].rearrange("(o h) -> o h", o=1).to_broadcast([P, NH])).then_inc(loaded, 16)
            sp.wait_ge(loaded, 128)

        @block.gpsimd
        def _(pool):
            pool.memset(ones[:, :], 1.0).then_inc(const_made, 1)
            pool.memset(causal[:, :], 0.0).then_inc(const_made, 1)
            pool.memset(q_pad[:, :, :, :], 0.0).then_inc(const_made, 1)
            pool.memset(state[:, :, :, :], 0.0).then_inc(const_made, 1)
            pool.wait_ge(const_made, 4)
            pool.affine_select(out=upto[:, :], in_=ones[:, :], compare_op=ALU.is_ge, fill=0.0, base=0,
                               pattern=[[1, P]], channel_multiplier=-1).then_inc(const_ready, 1)
            pool.affine_select(out=causal[:, :], in_=causal[:, :], compare_op=ALU.is_ge, fill=NEVER, base=0,
                               pattern=[[1, P]], channel_multiplier=-1).then_inc(const_ready, 1)
            pool.wait_ge(const_ready, 2)

            def norm_rsqrt(b):
                wait_apart(pool, k, agg_done, b + 1)
                pool.tensor_scalar(var_eps[:, :], mean_var[:, :, 1], EPS, None, ALU.add).then_inc(eps_done, 1)
                pool.wait_ge(eps_done, b + 1)
                pool.tensor_tensor(rstd[:, :], var_eps[:, :], k.neg_half[:, 0:GT], ALU.pow).then_inc(rstd_done, 1)

            def spread(b, c):
                n = GT * b + c
                if c == 0:
                    pool.wait_ge(decay_done, b + 1)
                if before(b, c, 2):
                    pool.wait_ge(cum_done, n - 1)
                pool.tensor_tensor(steps[:, c % 2, :, :], upto[:, :].unsqueeze(1).to_broadcast([P, NH, P]),
                                   decay[:, c, :].unsqueeze(2).to_broadcast([P, NH, P]), ALU.mult).then_inc(steps_done, 1)

            def out_rsqrt(b, c):
                n = GT * b + c
                wait_apart(pool, k, sum_done, n + 1)
                pool.tensor_scalar(o_mean[:, :], o_sum[:, :], 1.0 / DV, EPS, ALU.mult, ALU.add).then_inc(mean_done, 1)
                pool.wait_ge(mean_done, n + 1)
                pool.tensor_tensor(o_rstd[:, :], o_mean[:, :], k.neg_half[:, 0:NH], ALU.pow).then_inc(o_rstd_done, 1)

            def slot(b, c, more):
                if before(b, c, 2):
                    out_rsqrt(*before(b, c, 2))
                if c == 0:
                    spread(b, 0)
                if c == 2 and more:
                    norm_rsqrt(b + 1)
                if c < GT - 1:
                    spread(b, c + 1)

            def drain():
                out_rsqrt(B - 1, GT - 2)
                out_rsqrt(B - 1, GT - 1)

            norm_rsqrt(0)
            schedule(pool, slot, drain)

        @block.vector
        def _(dve):
            def statistics(b):
                for t in range(GT):
                    last = dve.bn_stats(stats[:, t, :], k.x[:, GT * b + t, :])
                last.then_inc(stats_done, 1)
                wait_apart(dve, k, stats_done, b + 1)
                for t in range(GT):
                    last = dve.bn_aggr(mean_var[:, t, :], stats[:, t, :])
                last.then_inc(agg_done, 1)

            def scale(b, reuse):
                if reuse:
                    dve.wait_ge(turned, b)
                dve.wait_ge(rstd_done, b + 1)
                for t in range(GT):
                    last = dve.tensor_scalar(xn[:, t, :], k.x[:, GT * b + t, :], mean_var[:, t, 0:1], rstd[:, t:t + 1],
                                             ALU.subtract, ALU.mult)
                last.then_inc(xn_done, 1)

            def split(b):
                dve.wait_ge(copied, b + 1)
                if before(b, 0, 1):
                    dve.wait_ge(g_done, GT * b)
                dve.tensor_copy(xT_hi[:, :, :], xT32[:, :, :]).then_inc(hi_done, 1)
                dve.wait_ge(hi_done, b + 1)
                dve.tensor_tensor(xT_lo[:, :, :], xT32[:, :, :], xT_hi[:, :, :].bitcast(F32), ALU.subtract).then_inc(split_done, 1)

            def logit(b):
                dve.wait_ge(gk_done, b + 1)
                dve.tensor_tensor(z[:, :, :], k_ps[:, GK:GK + GT * NH].rearrange("p (t h) -> p t h", h=NH),
                                  bgk[:, :].unsqueeze(1).to_broadcast([P, GT, NH]), ALU.add).then_inc(z_done, 1)
                dve.wait_ge(z_done, b + 1)
                dve.scalar_tensor_tensor(out=z_abs[:, :, :], in0=z[:, :, :], scalar=-1.0, in1=z[:, :, :],
                                         op0=ALU.mult, op1=ALU.min).then_inc(z_abs_done, 1)
                dve.tensor_scalar(z_min[:, :, :], z[:, :, :], 0.0, None, ALU.min).then_inc(z_min_done, 1)

            def log_sigmoid(b):
                dve.wait_ge(z_log_done, b + 1)
                dve.wait_ge(z_min_done, b + 1)
                if before(b, 0, 1):
                    dve.wait_ge(steps_done, GT * b)
                dve.tensor_tensor(z_min[:, :, :], z_min[:, :, :], z_log[:, :, :], ALU.subtract).then_inc(log_sig_done, 1)
                dve.wait_ge(log_sig_done, b + 1)
                dve.tensor_scalar(decay[:, :, :], z_min[:, :, :], 1.0 / GLN, None, ALU.mult).then_inc(decay_done, 1)

            def gaps(b, c):
                n = GT * b + c
                dve.wait_ge(cum_done, n + 1)
                dve.tensor_copy(cum_col[:, :], k_ps[:, COL:COL + NH]).then_inc(col_copied, 1)
                dve.wait_ge(col_copied, n + 1)
                dve.wait_ge(cum_copied, n + 1)
                if before(b, c, 1):
                    dve.wait_ge(k_fac_done, n)
                    dve.wait_ge(gap_exp_done, n)
                dve.tensor_tensor(k_gap[:, :], cum[:, :, P - 1], cum_col[:, :], ALU.subtract).then_inc(k_gap_done, 1)
                for h in range(NH):
                    last = dve.scalar_tensor_tensor(out=gap[:, h, :], in0=cum[:, h, :], scalar=cum_col[:, h:h + 1],
                                                    in1=causal[:, :], op0=ALU.subtract, op1=ALU.min)
                last.then_inc(gap_done, 1)

            def decayed(b, c):
                n = GT * b + c
                dve.wait_ge(cum_exp_done, n + 1)
                if c == 0:
                    dve.wait_ge(qk_copied, 4 * (b + 1))
                if before(b, c, 2):
                    dve.wait_ge(o_done, n - 1)
                for i in range(2):
                    rows = slice(DK * i, DK * i + DK)
                    last = dve.tensor_tensor(q_dec[rows, c % 2, :, :], q_pad[rows, :, i, c * P:(c + 1) * P],
                                             cum_exp[rows, c % 2, i:NH:2, :], ALU.mult)
                last.then_inc(q_dec_done, 1)
                dve.wait_ge(k_done, n + 1)
                dve.wait_ge(k_fac_done, n + 1)
                dve.tensor_tensor(k_dec[:, c % 2, :, :], k_ps[:, 0:NH * DK].rearrange("p (h d) -> p h d", h=NH),
                                  k_fac[:, :].unsqueeze(2).to_broadcast([P, NH, DK]), ALU.mult).then_inc(k_dec_done, 1)

            def mask(b, c):
                n = GT * b + c
                dve.wait_ge(score_done, n + 1)
                dve.wait_ge(gap_exp_done, n + 1)
                dve.tensor_tensor(score[:, c % 2, :, :], score_ps[:, :].rearrange("p (h t) -> p h t", h=NH),
                                  gap_exp[:, :, :], ALU.mult).then_inc(masked, 1)

            def swish(b, c):
                n = GT * b + c
                dve.wait_ge(tanh_done, n + 1)
                if before(b, c, 2):
                    dve.wait_ge(o_gated_done, n - 1)
                dve.scalar_tensor_tensor(out=gate[:, c % 2, :], in0=tanh_g[:, :], scalar=1.0, in1=g_ps[:, :],
                                         op0=ALU.add, op1=ALU.mult).then_inc(gated, 1)

            def update(b, c):
                n = GT * b + c
                dve.wait_ge(o_done, n + 1)
                if before(b, c, 1):
                    dve.wait_ge(state_done, states(*before(b, c, 1)))
                new = s_ps[:, :].rearrange("p (a i d) -> p a i d", a=2, i=2)
                for i in range(2):
                    rows = slice(DK * i, DK * i + DK)
                    if c == 0:
                        last = dve.tensor_copy(state[rows, :, i, :], new[rows, :, i, :])
                        continue
                    for a in range(2):
                        last = dve.scalar_tensor_tensor(out=state[rows, a, i, :], in0=state[rows, a, i, :],
                                                        scalar=cum_exp[rows, c % 2, 2 * a + i, P - 1:P],
                                                        in1=new[rows, a, i, :], op0=ALU.mult, op1=ALU.add)
                last.then_inc(state_done, 1)

            def square_sum(b, c):
                n = GT * b + c
                dve.wait_ge(sq_done, n + 1)
                if before(b, c, 1):
                    dve.wait_ge(mean_done, n)
                dve.tensor_reduce(o_sum[:, :], o_sq[:, :, :], AX_X, ALU.add).then_inc(sum_done, 1)

            def gate_out(b, c):
                n = GT * b + c
                dve.wait_ge(o_rstd_done, n + 1)
                if before(b, c, 1):
                    dve.wait_ge(oT_done, n)
                for h in range(NH):
                    cols = slice(h * DV, (h + 1) * DV)
                    last = dve.scalar_tensor_tensor(out=o_gated[:, cols], in0=o32[:, cols], scalar=o_rstd[:, h:h + 1],
                                                    in1=gate[:, c % 2, cols], op0=ALU.mult, op1=ALU.mult)
                last.then_inc(o_gated_done, 1)

            def out_low(b, c):
                n = GT * b + c
                dve.wait_ge(oT_hi_done, n + 1)
                dve.tensor_tensor(oT_lo[:, :], y_ps[:, :], oT_hi[:, :].bitcast(F32), ALU.subtract).then_inc(oT_split, 1)

            def add_out(b, c):
                n = GT * b + c
                dve.wait_ge(y_done, n + 1)
                xt = k.x[:, n, :]
                dve.tensor_tensor(xt, y_ps[:, 0:D], xt, ALU.add).then_inc(y_added, 1)

            def slot(b, c, more):
                mid, tail = before(b, c, 1), before(b, c, 2)
                if tail:
                    square_sum(*tail)
                if c == 0:
                    if tail:
                        gate_out(*tail)
                    split(b)
                    logit(b)
                    if tail:
                        out_low(*tail)
                    log_sigmoid(b)
                    if tail:
                        add_out(*tail)
                gaps(b, c)
                if tail and c:
                    gate_out(*tail)
                decayed(b, c)
                mask(b, c)
                swish(b, c)
                if tail and c:
                    out_low(*tail)
                if mid and c:
                    update(*mid)
                if tail and c:
                    add_out(*tail)
                if c == 2 and more:
                    statistics(b + 1)
                if c == 3 and more:
                    scale(b + 1, True)

            def drain():
                for c in (GT - 2, GT - 1):
                    square_sum(B - 1, c)
                    gate_out(B - 1, c)
                    out_low(B - 1, c)
                    add_out(B - 1, c)

            dve.wait_ge(loaded, 128)
            for h in range(NH):
                last = dve.tensor_scalar(wo_scaled[:, h, :], wo_in[:, h, :], gnorm[:, 0:1], 0.5, ALU.mult, ALU.mult)
            last.then_inc(wo_scaled_done, 1)
            dve.wait_ge(w_hi_done, 1)
            dve.tensor_tensor(w_lo[:, :, :], w_in[:, :, :], w_hi[:, :, :].bitcast(F32), ALU.subtract).then_inc(w_ready, 1)
            dve.wait_ge(w_hi_done, 2)
            dve.tensor_tensor(wo_lo[:, :, :], wo_scaled[:, :, :], wo_hi[:, :, :].bitcast(F32), ALU.subtract).then_inc(w_ready, 1)
            dve.wait_ge(const_ready, 2)
            statistics(0)
            scale(0, False)
            schedule(dve, slot, drain)

        @block.scalar
        def _(act):
            def copy(b):
                act.wait_ge(turned, b + 1)
                if before(b, 0, 1):
                    act.wait_ge(gk_done, b)
                    act.wait_ge(split_done, b)
                act.activation(xT32[:, 0, :], v_ps[:, :], ACT.Copy)
                act.activation(xT32[:, 1, :], g_ps[:, :], ACT.Copy).then_inc(copied, 1)

            def log1p_exp(b):
                act.wait_ge(z_abs_done, b + 1)
                act.activation(z_exp[:, :, :], z_abs[:, :, :], ACT.Exp).then_inc(z_exp_done, 1)
                act.wait_ge(z_exp_done, b + 1)
                act.activation(z_log[:, :, :], z_exp[:, :, :], ACT.Ln, bias=1.0).then_inc(z_log_done, 1)

            def qk_copy(b):
                if before(b, 0, 1):
                    act.wait_ge(score_done, GT * b)
                    act.wait_ge(q_dec_done, GT * b)
                else:
                    act.wait_ge(const_ready, 2)
                for a, ps in enumerate((cum_ps, score_ps)):
                    act.wait_ge(qk_done, 4 * b + a + 1)
                    act.activation(kT[:, a, :], ps[:, :], ACT.Copy).then_inc(qk_copied, 1)
                for a, ps in enumerate((v_ps, g_ps)):
                    act.wait_ge(qk_done, 4 * b + a + 3)
                    act.activation(q_pad[0:DK, a, 0, :], ps[0:DK, :], ACT.Copy, scale=DK ** -0.5)
                    act.activation(q_pad[DK:P, a, 1, :], ps[DK:P, :], ACT.Copy, scale=DK ** -0.5).then_inc(qk_copied, 1)

            def front(b, c):
                n = GT * b + c
                act.wait_ge(cum_done, n + 1)
                if before(b, c, 1):
                    act.wait_ge(gap_done, n)
                act.activation(cum[:, :, :], cum_ps[:, :].rearrange("p (h t) -> p h t", h=NH), ACT.Copy).then_inc(cum_copied, 1)
                act.wait_ge(cum_copied, n + 1)
                if before(b, c, 2):
                    act.wait_ge(state_done, states(*before(b, c, 2)))
                    act.wait_ge(q_dec_done, n - 1)
                act.activation(cum_exp[:, c % 2, :, :], cum[:, :, :], ACT.Exp).then_inc(cum_exp_done, 1)
                act.wait_ge(k_gap_done, n + 1)
                if before(b, c, 1):
                    act.wait_ge(k_dec_done, n)
                act.activation(k_fac[:, :], k_gap[:, :], ACT.Exp).then_inc(k_fac_done, 1)
                act.wait_ge(v_done, n + 1)
                if before(b, c, 2):
                    act.wait_ge(o_done, n - 1)
                act.activation(v32[:, c % 2, :], v_ps[:, :], ACT.Copy).then_inc(v_copied, 1)
                act.wait_ge(gap_done, n + 1)
                if before(b, c, 1):
                    act.wait_ge(masked, n)
                act.activation(gap_exp[:, :, :], gap[:, :, :], ACT.Exp).then_inc(gap_exp_done, 1)
                act.wait_ge(g_done, n + 1)
                if before(b, c, 1):
                    act.wait_ge(gated, n)
                act.activation(tanh_g[:, :], g_ps[:, :], ACT.Tanh, scale=0.5).then_inc(tanh_done, 1)

            def out_copy(b, c):
                n = GT * b + c
                act.wait_ge(o_done, n + 1)
                if before(b, c, 1):
                    act.wait_ge(o_gated_done, n)
                    act.wait_ge(sum_done, n)
                act.activation(o32[:, :], o_ps[:, :], ACT.Copy).then_inc(o_copied, 1)
                act.wait_ge(o_copied, n + 1)
                act.activation(o_sq[:, :, :].rearrange("p h d -> p (h d)"), o32[:, :], ACT.Square).then_inc(sq_done, 1)

            def out_high(b, c):
                n = GT * b + c
                act.wait_ge(oT_done, n + 1)
                if before(b, c, 1):
                    act.wait_ge(y_done, n)
                act.activation(oT_hi[:, :], y_ps[:, :], ACT.Copy).then_inc(oT_hi_done, 1)

            def slot(b, c, more):
                tail = before(b, c, 2)
                if tail:
                    out_copy(*tail)
                if c == 0:
                    copy(b)
                    if tail:
                        out_high(*tail)
                    log1p_exp(b)
                    qk_copy(b)
                front(b, c)
                if tail and c:
                    out_high(*tail)

            def drain():
                for c in (GT - 2, GT - 1):
                    out_copy(B - 1, c)
                    out_high(B - 1, c)

            act.wait_ge(loaded, 128)
            act.activation(w_hi[:, :, :], w_in[:, :, :], ACT.Copy).then_inc(w_hi_done, 1)
            act.wait_ge(wo_scaled_done, 1)
            act.activation(wo_hi[:, :, :], wo_scaled[:, :, :], ACT.Copy).then_inc(w_hi_done, 1)
            schedule(act, slot, drain)

        @block.tensor
        def _(pe):
            def product(out, pairs):
                for i, (w, x) in enumerate(pairs):
                    last = pe.matmul(out, w, x, start=(i == 0), stop=(i == len(pairs) - 1))
                return last

            def turn(b):
                pe.wait_ge(xn_done, b + 1)
                if before(b, 0, 1):
                    pe.wait_ge(v_copied, GT * b)
                    pe.wait_ge(gated, GT * b)
                for kd, ps in enumerate((v_ps, g_ps)):
                    for t in range(GT):
                        last = pe.transpose(ps[:, t * P:(t + 1) * P], xn[:, t, kd * P:(kd + 1) * P], k.ident[:, :])
                last.then_inc(turned, 1)

            def decay_logits(b):
                pe.wait_ge(copied, b + 1)
                if before(b, 0, 1):
                    pe.wait_ge(k_dec_done, GT * b)
                for t in range(GT):
                    last = product(k_ps[:, GK + NH * t:GK + NH * (t + 1)],
                                   [(xT32[:, kd, t * P:(t + 1) * P], wgk[:, kd, :]) for kd in range(KD)])
                last.then_inc(gk_done, 1)

            def qk(b):
                pe.wait_ge(split_done, b + 1)
                if before(b, 0, 1):
                    pe.wait_ge(cum_copied, GT * b)
                    pe.wait_ge(masked, GT * b)
                for ps, at in ((cum_ps, 256), (score_ps, 384), (v_ps, 0), (g_ps, 128)):
                    product(ps[:, :], [(w[:, kd, at:at + P], x[:, kd, :]) for kd in range(KD)
                                       for w, x in ((w_hi, xT_hi), (w_hi, xT_lo), (w_lo, xT_hi))]).then_inc(qk_done, 1)

            def rows(out, b, c, at, width):
                toks = slice(c * P, (c + 1) * P)
                return product(out, [(x[:, kd, toks], w[:, kd, at:at + width]) for kd in range(KD)
                                     for x, w in ((xT_hi, w_hi), (xT_hi, w_lo), (xT_lo, w_hi))])

            def front(b, c):
                n = GT * b + c
                if before(b, c, 1):
                    pe.wait_ge(k_dec_done, n)
                if c == 0:
                    pe.wait_ge(z_done, b + 1)
                rows(k_ps[:, 0:NH * DK], b, c, 256, 256).then_inc(k_done, 1)
                if c == 0:
                    pe.wait_ge(qk_copied, 4 * (b + 1))
                else:
                    pe.wait_ge(masked, n)
                for a in range(2):
                    last = product(score_ps[:, 256 * a:256 * a + 256],
                                   [(kT[:, a, c * P:(c + 1) * P], q_pad[:, a, :, c * P:(c + 1) * P])])
                last.then_inc(score_done, 1)
                if c:
                    pe.wait_ge(v_copied, n)
                rows(v_ps[:, :], b, c, 512, 512).then_inc(v_done, 1)
                pe.wait_ge(steps_done, n + 1)
                if c:
                    pe.wait_ge(cum_copied, n)
                product(k_ps[:, COL:COL + NH], [(upto[:, :], decay[:, c, :])])
                product(cum_ps[:, :], [(ones[:, :], steps[:, c % 2, :, :].rearrange("p h t -> p (h t)"))]).then_inc(cum_done, 1)
                if c:
                    pe.wait_ge(gated, n)
                rows(g_ps[:, :], b, c, 1024, 512).then_inc(g_done, 1)

            def mid(b, c):
                n = GT * b + c
                pe.wait_ge(v_copied, n + 1)
                pe.wait_ge(k_dec_done, n + 1)
                pe.wait_ge(masked, n + 1)
                if before(b, c, 1):
                    pe.wait_ge(state_done, states(*before(b, c, 1)))
                    pe.wait_ge(o_copied, n)
                if c < GT - 1:
                    for a in range(2):
                        last = product(s_ps[:, 256 * a:256 * a + 256],
                                       [(k_dec[:, c % 2, 2 * a:2 * a + 2, :].rearrange("p h d -> p (h d)"),
                                         v32[:, c % 2, 256 * a:256 * a + 256])])
                    last.then_inc(s_done, 1)
                for a in range(2):
                    if c:
                        pe.matmul(o_ps[:, 256 * a:256 * a + 256], q_dec[:, c % 2, a, :],
                                  state[:, a, :, :].rearrange("p i d -> p (i d)"), start=True, stop=True,
                                  skip_group_check=True)
                    for h in (2 * a, 2 * a + 1):
                        cols = slice(h * DV, (h + 1) * DV)
                        last = pe.matmul(o_ps[:, cols], score[:, c % 2, h, :], v32[:, c % 2, cols],
                                         start=(c == 0), stop=True, skip_group_check=True)
                last.then_inc(o_done, 1)

            def turn_out(b, c):
                n = GT * b + c
                pe.wait_ge(o_gated_done, n + 1)
                if before(b, c, 1):
                    pe.wait_ge(y_added, n)
                for h in range(NH):
                    last = pe.transpose(y_ps[:, h * P:(h + 1) * P], o_gated[:, h * DV:(h + 1) * DV], k.ident[:, :])
                last.then_inc(oT_done, 1)

            def project(b, c):
                pe.wait_ge(oT_split, GT * b + c + 1)
                product(y_ps[:, 0:D], [(o[:, h * P:(h + 1) * P], w[:, h, :]) for h in range(NH)
                                       for o, w in ((oT_hi, wo_hi), (oT_hi, wo_lo), (oT_lo, wo_hi))]).then_inc(y_done, 1)

            def slot(b, c, more):
                m, tail = before(b, c, 1), before(b, c, 2)
                if c == 0:
                    turn(b)
                    if m:
                        mid(*m)
                        turn_out(*tail)
                    decay_logits(b)
                    if m:
                        project(*tail)
                    qk(b)
                    front(b, 0)
                    return
                front(b, c)
                if tail:
                    turn_out(*tail)
                mid(*m)
                if tail:
                    project(*tail)

            def drain():
                mid(B - 1, GT - 1)
                for c in (GT - 2, GT - 1):
                    turn_out(B - 1, c)
                    project(B - 1, c)

            pe.wait_ge(w_ready, 2)
            pe.wait_ge(const_ready, 2)
            schedule(pe, slot, drain)


def store(nc, k, dram):
    with ExitStack() as ctx:
        stored = ctx.enter_context(nc.semaphore("stored"))
        block = ctx.enter_context(nc.Block())
        rows = dram["out"].rearrange("b n d -> (b n) d").rearrange("(t p) d -> p t d", p=P)

        @block.sync
        def _(sp):
            for g in range(4):
                sp.dma_start(rows[:, 8 * g:8 * g + 8, :], k.x[:, 8 * g:8 * g + 8, :]).then_inc(stored, 16)
            sp.wait_ge(stored, 64)


def macaron(nc, dram, parts=("ffn1", "attn", "ffn2")):
    k = Core()
    with ExitStack() as ctx:
        def sb(n, shape, dt=F32):
            return ctx.enter_context(nc.sbuf_tensor(n, shape, dt))

        k.x = sb("x", [P, TILES, D])
        k.ident = sb("ident", [P, P])
        k.neg_half = sb("neg_half", [P, GT])
        k.router_w = sb("router_w", [P, KD, E])
        k.router_b = sb("router_b", [P, E])
        k.b1 = sb("b1", [P, NX, KH])
        k.b2_blocks = sb("b2_blocks", [P, GT, D])
        k.gate = sb("gate", [P, TILES, NX])
        k.gate_pad = sb("gate_pad", [P, 2, GT, 32])
        k.passed = ctx.enter_context(nc.semaphore("passed"))
        constants(nc, k, dram)
        for part in parts:
            if part == "attn":
                attention(nc, k, dram)
                continue
            with ExitStack() as phase:
                k.xT_hi = phase.enter_context(nc.sbuf_tensor(f"{part}_xT_hi", [P, KD, T], F32R))
                k.xT_lo = phase.enter_context(nc.sbuf_tensor(f"{part}_xT_lo", [P, KD, T], F32R))
                normalise(nc, k, f"{part}_norm")
                experts(nc, k, dram, f"{part}_experts")
        store(nc, k, dram)


_INS = {"L0_attn_x": "x", "L0_attn_Wq": "Wq", "L0_attn_Wk": "Wk", "L0_attn_Wv": "Wv", "L0_attn_Wg": "Wg",
        "L0_attn_Wgk": "Wgk", "L0_attn_bgk": "bgk", "L0_attn_Wo": "Wo", "L0_attn_gnorm_w": "gnorm_w",
        "L0_ffn_router_w": "router_w", "L0_ffn_router_b": "router_b", "L0_ffn_sw1": "sw1", "L0_ffn_sb1": "sb1",
        "L0_ffn_sw2": "sw2", "L0_ffn_sb2": "sb2", "L0_ffn_rw1": "rw1", "L0_ffn_rb1": "rb1", "L0_ffn_rw2": "rw2",
        "L0_ffn_rb2": "rb2"}


def kernel(**inputs):
    import numpy as _np
    import concourse.bacc as _bacc
    from concourse import mybir as _mybir
    from concourse.bass_utils import run_bass_kernel_spmd as _run

    nc = _bacc.Bacc("TRN2", target_bir_lowering=False, num_devices=1)
    arrays, dram = {}, {}
    for name, short in _INS.items():
        a = _np.ascontiguousarray(inputs[name])
        arrays[f"in_{short}"] = a
        dram[short] = nc.dram_tensor(f"in_{short}", a.shape, _mybir.dt.from_np(a.dtype), kind="ExternalInput").ap()
    shape = inputs["L0_attn_x"].shape
    dram["out"] = nc.dram_tensor("out_x", shape, _mybir.dt.float32, kind="ExternalOutput").ap()
    macaron(nc, dram)
    r = _run(nc, [arrays], core_ids=[0])
    return r.results[0]["out_x"]
```

```python
from contextlib import ExitStack

import concourse.bass as bass
from concourse import mybir

P = 128
F32 = mybir.dt.float32
F32R = mybir.dt.float32r
ALU = mybir.AluOpType
ACT = mybir.ActivationFunctionType
AX_X = mybir.AxisListType.X

T = 4096
D = 256
TILES = T // P
GT = 4
G = TILES // GT
GN = GT * P
KD = D // P
H = 512
KH = H // P
E = 8
NX = E + 1
TOP = 2
SLOTS = GN
ROW = D + 1
JOBS = TOP * T // SLOTS + E - 1
EPS = 1e-5
B = 8
NH, DK, DV = 4, 64, 128
WALL = 2 * NH * DK + 2 * NH * DV
GLN = 16.0
NEVER = -1e4


def wait_apart(eng, k, sem, value):
    eng.wait_ge(sem, value)
    eng.sem_inc(k.passed, 1)


class Core:
    pass


def zero_slots(eng, k, dram):
    with eng.Fori(0, JOBS) as j:
        eng.dma_start(dram["slot_x"].rearrange("(j p r) d -> j p r d", p=P, r=SLOTS // P)[bass.ds(j, 1)]
                      .rearrange("o p r d -> p (o r) d"), k.zero_rows[:, :, :]).then_inc(k.slots_zeroed, 16)


def constants(nc, k, dram):
    with ExitStack() as ctx:
        x_in = ctx.enter_context(nc.semaphore("x_in"))
        small_in = ctx.enter_context(nc.semaphore("small_in"))
        zeroed = ctx.enter_context(nc.semaphore("zeroed"))
        slots_named = ctx.enter_context(nc.semaphore("slots_named"))
        built = ctx.enter_context(nc.semaphore("built"))
        turned = ctx.enter_context(nc.semaphore("turned"))
        b1_rows = ctx.enter_context(nc.sbuf_tensor("b1_rows", [NX * KH, P], F32))
        ps = ctx.enter_context(nc.psum_tensor("const_ps", [P, 512], F32))
        sb2 = ctx.enter_context(nc.sbuf_tensor("sb2_rows", [P, D], F32))
        all_ones = ctx.enter_context(nc.sbuf_tensor("all_ones", [P, E, E], F32))
        block = ctx.enter_context(nc.Block())
        x_rows = dram["x"].rearrange("b n d -> (b n) d").rearrange("(t p) d -> p t d", p=P)

        @block.sync
        def _(sp):
            for g in range(4):
                sp.dma_start(k.x[:, 8 * g:8 * g + 8, :], x_rows[:, 8 * g:8 * g + 8, :]).then_inc(x_in, 16)
            sp.wait_ge(slots_named, 1)
            zero_slots(sp, k, dram)
            sp.wait_ge(x_in, 64)

        @block.scalar
        def _(act):
            act.dma_start(b1_rows[0:KH, :], dram["sb1"].rearrange("(c p) -> c p", p=P)).then_inc(small_in, 16)
            act.dma_start(b1_rows[KH:NX * KH, :],
                          dram["rb1"].rearrange("e (c p) -> (e c) p", p=P)).then_inc(small_in, 16)
            act.dma_start(k.router_w[:, :, :], dram["router_w"].rearrange("(k p) e -> p k e", p=P)).then_inc(small_in, 16)
            act.dma_start(k.router_b[:, :], dram["router_b"].rearrange("(o e) -> o e", o=1).to_broadcast([P, E])
                          ).then_inc(small_in, 16)
            act.dma_start(sb2[:, :], dram["sb2"].rearrange("(o d) -> o d", o=1).to_broadcast([P, D])).then_inc(small_in, 16)
            act.wait_ge(small_in, 80)

        @block.gpsimd
        def _(pool):
            pool.memset(k.ident[:, :], 0.0).then_inc(zeroed, 1)
            pool.memset(k.neg_half[:, :], -0.5).then_inc(zeroed, 1)
            pool.memset(k.zero_rows[:, :, :], 0.0).then_inc(zeroed, 1)
            pool.wait_ge(zeroed, 3)
            pool.iota(k.zero_rows[:, :, D], pattern=[[1, SLOTS // P]], base=TOP * T, channel_multiplier=SLOTS // P,
                      allow_small_or_imprecise_dtypes=True).then_inc(slots_named, 1)
            pool.memset(all_ones[:, :, :], 1.0).then_inc(zeroed, 1)
            pool.memset(k.ones[:, :], 1.0).then_inc(zeroed, 1)
            pool.iota(k.job_starts[:, :], pattern=[[SLOTS, T // SLOTS]], base=0, channel_multiplier=0,
                      allow_small_or_imprecise_dtypes=True).then_inc(zeroed, 1)
            pool.iota(k.expert_numbers[:, :], pattern=[[1, E]], base=0, channel_multiplier=0,
                      allow_small_or_imprecise_dtypes=True).then_inc(zeroed, 1)
            pool.iota(k.job_numbers[:, :], pattern=[[1, JOBS]], base=0, channel_multiplier=0,
                      allow_small_or_imprecise_dtypes=True).then_inc(zeroed, 1)
            pool.iota(k.pair_rows[:, :, :], pattern=[[1, TOP], [TOP * P, TILES]], base=0, channel_multiplier=TOP,
                      allow_small_or_imprecise_dtypes=True).then_inc(zeroed, 1)
            pool.wait_ge(zeroed, 9)
            pool.affine_select(out=k.earlier[:, :], in_=k.ones[:, :], compare_op=ALU.is_ge, fill=0.0, base=-1,
                               pattern=[[1, P]], channel_multiplier=-1).then_inc(built, 1)
            pool.affine_select(out=k.lower[:, :, :], in_=all_ones[:, :, :], compare_op=ALU.is_ge, fill=0.0, base=-1,
                               pattern=[[1, E], [-1, E]], channel_multiplier=0).then_inc(built, 1)
            pool.affine_select(out=k.ident[:, :], in_=k.ident[:, :], compare_op=ALU.not_equal, fill=1.0,
                               base=0, pattern=[[-1, P]], channel_multiplier=1).then_inc(built, 1)

        @block.tensor
        def _(pe):
            pe.wait_ge(built, 3)
            pe.wait_ge(small_in, 80)
            pe.transpose(ps[:, 0:NX * KH], b1_rows[:, :], k.ident[0:NX * KH, 0:NX * KH]).then_inc(turned, 1)

        @block.vector
        def _(dve):
            dve.wait_ge(turned, 1)
            dve.tensor_copy(k.b1[:, :, :], ps[:, 0:NX * KH].rearrange("p (x c) -> p x c", x=NX)).then_inc(built, 1)
            dve.tensor_scalar(k.half_sb2[:, :], sb2[:, :], 0.5, None, ALU.mult).then_inc(built, 1)


class Weights:

    def __init__(self, nc, ctx, name):
        def sb(n, shape, dt=F32):
            return ctx.enter_context(nc.sbuf_tensor(f"{name}_{n}", shape, dt))

        def sem(n):
            return nc.alloc_semaphore(f"{name}_{n}")

        self.w1_in, self.w2_in = sb("w1_in", [P, KD, H]), sb("w2_in", [P, KH, D])
        self.w1_hi, self.w1_lo = sb("w1_hi", [P, KD, H], F32R), sb("w1_lo", [P, KD, H], F32R)
        self.w2_hi, self.w2_lo = sb("w2_hi", [P, KH, D], F32R), sb("w2_lo", [P, KH, D], F32R)
        self.w1_loaded, self.w2_loaded = sem("w1_loaded"), sem("w2_loaded")
        self.w1_hi_done, self.w1_split = sem("w1_hi_done"), sem("w1_split")
        self.w2_hi_done, self.w2_split = sem("w2_hi_done"), sem("w2_split")

    def w1_high(self, act, n):
        act.wait_ge(self.w1_loaded, 16 * n + 16)
        act.activation(self.w1_hi[:, :, :], self.w1_in[:, :, :], ACT.Copy).then_inc(self.w1_hi_done, 1)

    def w2_high(self, act, n):
        act.wait_ge(self.w2_loaded, 16 * n + 16)
        act.activation(self.w2_hi[:, :, :], self.w2_in[:, :, :], ACT.Copy).then_inc(self.w2_hi_done, 1)

    def w1_low(self, dve, n):
        dve.wait_ge(self.w1_hi_done, n + 1)
        dve.tensor_tensor(self.w1_lo[:, :, :], self.w1_in[:, :, :], self.w1_hi[:, :, :].bitcast(F32),
                          ALU.subtract).then_inc(self.w1_split, 1)

    def w2_low(self, dve, n):
        dve.wait_ge(self.w2_hi_done, n + 1)
        dve.tensor_tensor(self.w2_lo[:, :, :], self.w2_in[:, :, :], self.w2_hi[:, :, :].bitcast(F32),
                          ALU.subtract).then_inc(self.w2_split, 1)


def normalise(nc, k, dram, w, name):
    with ExitStack() as ctx:
        def sem(n):
            return nc.alloc_semaphore(f"{name}_{n}")

        def sb(n, shape, dt=F32):
            return ctx.enter_context(nc.sbuf_tensor(f"{name}_{n}", shape, dt))

        stats = sb("stats", [P, 2, GT, 6])
        mean_var = sb("mean_var", [P, 2, GT, 2])
        var_eps = sb("var_eps", [P, 2, GT])
        rstd = sb("rstd", [P, 2, GT])
        xn = sb("xn", [P, 2, GT, D])
        kept = sem("kept")
        xT32 = sb("xT32", [P, 2, KD, GN])
        first = sb("first", [P, TILES, E])
        second = sb("second", [P, TILES, E])
        chosen = sb("chosen", [P, TILES, E])
        tiles_sum = sb("tiles_sum", [P, 2, TILES, E])
        slot = sb("slot", [P, TILES, E])
        picked = sb("picked", [P, 2, TILES, E])
        fills = sb("fills", [P, E, T // SLOTS])
        jobs = sb("jobs", [P, E])
        behind = sb("behind", [P, E, E])
        start = sb("start", [P, E])
        end = sb("end", [P, E])
        passed_by = sb("passed_by", [P, JOBS, E])
        owner = sb("owner", [P, JOBS])
        slot_f = sb("slot_f", [P, TOP, TILES])
        logits = sb("logits", [P, TILES, E])
        top = sb("top", [P, TILES])
        probs = sb("probs", [P, TILES, E])
        total = sb("total", [P, TILES])
        beats = sb("beats", [P, E, TILES, E])
        rank = sb("rank", [P, TILES, E])
        owned = sb("owned", [P, JOBS, E])
        owned_b1 = sb("owned_b1", [P, JOBS, KH, E])
        turn_ps = ctx.enter_context(nc.psum_tensor(f"{name}_turn_ps", [P, 2, KD, 512], F32))
        logit_ps = ctx.enter_context(nc.psum_tensor(f"{name}_logit_ps", [P, 512], F32))
        count_ps = ctx.enter_context(nc.psum_tensor(f"{name}_count_ps", [P, 2, TILES, E], F32))

        stats_done, agg_done, rstd_done, eps_done = sem("stats_done"), sem("agg_done"), sem("rstd_done"), sem("eps_done")
        xn_done, turned, copied = sem("xn_done"), sem("turned"), sem("copied")
        hi_done, lo_done, logits_done = sem("hi_done"), sem("lo_done"), sem("logits_done")
        chain, exp_in, exp_out, diag_zero = sem("chain"), sem("exp_in"), sem("exp_out"), sem("diag_zero")
        chosen_done, counted = sem("chosen_done"), sem("counted")
        block = ctx.enter_context(nc.Block())

        @block.sync
        def _(sp):
            sp.dma_start(w.w1_in[:, :, :], dram["sw1"].rearrange("(k p) h -> p k h", p=P)).then_inc(w.w1_loaded, 16)
            sp.dma_start(w.w2_in[:, :, :], dram["sw2"].rearrange("(k p) d -> p k d", p=P)).then_inc(w.w2_loaded, 16)

        @block.gpsimd
        def _(pool):
            pool.memset(beats[:, :, :, :], 0.0).then_inc(diag_zero, 1)

            def rsqrt(g, p):
                wait_apart(pool, k, agg_done, g + 1)
                pool.tensor_scalar(var_eps[:, p, :], mean_var[:, p, :, 1], EPS, None, ALU.add).then_inc(eps_done, 1)
                pool.wait_ge(eps_done, g + 1)
                pool.tensor_tensor(rstd[:, p, :], var_eps[:, p, :], k.neg_half[:, 0:GT], ALU.pow).then_inc(rstd_done, 1)

            with pool.Fori(0, G // 2) as j:
                rsqrt(2 * j, 0)
                rsqrt(2 * j + 1, 1)

        @block.vector
        def _(dve):
            def statistics(g, p):
                for t in range(GT):
                    last = dve.bn_stats(stats[:, p, t, :], k.x[:, GT * g + t, :])
                last.then_inc(stats_done, 1)

            def aggregate(g, p):
                wait_apart(dve, k, stats_done, g + 1)
                for t in range(GT):
                    last = dve.bn_aggr(mean_var[:, p, t, :], stats[:, p, t, :])
                last.then_inc(agg_done, 1)

            def scale(g, p, reuse):
                if reuse:
                    dve.wait_ge(turned, g - 1)
                    dve.wait_ge(kept, g - 1)
                dve.wait_ge(rstd_done, g + 1)
                for t in range(GT):
                    last = dve.tensor_scalar(xn[:, p, t, :], k.x[:, GT * g + t, :], mean_var[:, p, t, 0:1],
                                             rstd[:, p, t:t + 1], ALU.subtract, ALU.mult)
                last.then_inc(xn_done, 1)

            def low(g, p):
                dve.wait_ge(hi_done, g + 1)
                at = bass.ds(g * GN, GN)
                dve.tensor_tensor(k.xT_lo[:, :, at], xT32[:, p, :, :], k.xT_hi[:, :, at].bitcast(F32),
                                  ALU.subtract).then_inc(lo_done, 1)

            def step(g, p, reuse):
                scale(g, p, reuse)
                aggregate(g + 1, 1 - p)
                statistics(g + 2, p)

            statistics(0, 0)
            statistics(1, 1)
            aggregate(0, 0)
            step(0, 0, False)
            step(1, 1, False)
            low(0, 0)
            with dve.Fori(1, G // 2 - 1) as j:
                step(2 * j, 0, True)
                low(2 * j - 1, 1)
                step(2 * j + 1, 1, True)
                low(2 * j, 0)
            scale(G - 2, 0, True)
            low(G - 3, 1)
            aggregate(G - 1, 1)
            scale(G - 1, 1, True)
            low(G - 2, 0)
            low(G - 1, 1)

            links = [0]

            def link(ins):
                links[0] += 1
                ins.then_inc(chain, 1)
                dve.wait_ge(chain, links[0])

            dve.wait_ge(logits_done, G)
            link(dve.tensor_tensor(logits[:, :, :], logit_ps[:, 0:TILES * E].rearrange("p (t e) -> p t e", e=E),
                                   k.router_b[:, :].unsqueeze(1).to_broadcast([P, TILES, E]), ALU.add))
            link(dve.tensor_reduce(top[:, :], logits[:, :, :], AX_X, ALU.max))
            dve.tensor_tensor(probs[:, :, :], logits[:, :, :], top[:, :].unsqueeze(2).to_broadcast([P, TILES, E]),
                              ALU.subtract).then_inc(exp_in, 1)
            dve.wait_ge(diag_zero, 1)
            for j in range(E):
                rival = logits[:, :, j:j + 1]
                if j:
                    last = dve.tensor_tensor(beats[:, j, :, 0:j], rival.to_broadcast([P, TILES, j]),
                                             logits[:, :, 0:j], ALU.is_gt)
                if j < E - 1:
                    last = dve.tensor_tensor(beats[:, j, :, j + 1:E], rival.to_broadcast([P, TILES, E - 1 - j]),
                                             logits[:, :, j + 1:E], ALU.is_ge)
            link(last)
            link(dve.tensor_reduce(rank[:, :, :], beats[:, :, :, :].rearrange("p j t e -> p t e j"), AX_X, ALU.add))
            dve.tensor_scalar(chosen[:, :, :], rank[:, :, :], float(TOP), None, ALU.is_lt).then_inc(chosen_done, 1)
            dve.tensor_scalar(first[:, :, :], rank[:, :, :], 0.0, None, ALU.is_equal)
            link(dve.tensor_scalar(second[:, :, :], rank[:, :, :], 1.0, None, ALU.is_equal))
            dve.wait_ge(exp_out, 1)
            link(dve.tensor_reduce(total[:, :], probs[:, :, :], AX_X, ALU.add))
            link(dve.reciprocal(total[:, :], total[:, :]))
            link(dve.tensor_tensor(probs[:, :, :], probs[:, :, :], total[:, :].unsqueeze(2).to_broadcast([P, TILES, E]),
                                   ALU.mult))
            dve.wait_ge(chosen_done, 1)
            link(dve.scalar_tensor_tensor(out=k.gate[:, :, 1:NX], in0=probs[:, :, :], scalar=0.5, in1=chosen[:, :, :],
                                          op0=ALU.mult, op1=ALU.mult))
            link(dve.memset(k.gate[:, :, 0:1], 0.5))

            dve.wait_ge(counted, 1)
            per_tile = count_ps[:, 1, :, :]
            link(dve.tensor_copy(tiles_sum[:, 0, :, :], per_tile))
            a, step = 0, 1
            while step < TILES:
                dve.tensor_copy(tiles_sum[:, 1 - a, 0:step, :], tiles_sum[:, a, 0:step, :])
                link(dve.tensor_tensor(tiles_sum[:, 1 - a, step:, :], tiles_sum[:, a, step:, :],
                                       tiles_sum[:, a, 0:TILES - step, :], ALU.add))
                a, step = 1 - a, 2 * step
            link(dve.tensor_tensor(fills[:, :, :], tiles_sum[:, a, TILES - 1, :].unsqueeze(2).to_broadcast([P, E, T // SLOTS]),
                                   k.job_starts[:, :].unsqueeze(1).to_broadcast([P, E, T // SLOTS]), ALU.is_gt))
            link(dve.tensor_reduce(jobs[:, :], fills[:, :, :], AX_X, ALU.add))
            link(dve.tensor_tensor(behind[:, :, :], jobs[:, :].unsqueeze(1).to_broadcast([P, E, E]), k.lower[:, :, :], ALU.mult))
            link(dve.tensor_reduce(start[:, :], behind[:, :, :], AX_X, ALU.add))
            dve.tensor_tensor(end[:, :], start[:, :], jobs[:, :], ALU.add)
            dve.tensor_tensor(slot[:, :, :], tiles_sum[:, a, :, :], per_tile, ALU.subtract)
            link(dve.tensor_scalar(start[:, :], start[:, :], float(SLOTS), None, ALU.mult))
            link(dve.tensor_tensor(slot[:, :, :], slot[:, :, :], count_ps[:, 0, :, :], ALU.add))
            link(dve.tensor_tensor(slot[:, :, :], slot[:, :, :], start[:, :].unsqueeze(1).to_broadcast([P, TILES, E]), ALU.add))
            dve.tensor_tensor(picked[:, 0, :, :], slot[:, :, :], first[:, :, :], ALU.mult)
            link(dve.tensor_tensor(picked[:, 1, :, :], slot[:, :, :], second[:, :, :], ALU.mult))
            link(dve.tensor_reduce(slot_f[:, :, :], picked[:, :, :, :], AX_X, ALU.add))
            link(dve.tensor_copy(k.slot_ids[:, :, :], slot_f[:, :, :]))
            dve.tensor_tensor(picked[:, 0, :, :], k.gate[:, :, 1:NX], first[:, :, :], ALU.mult)
            link(dve.tensor_tensor(picked[:, 1, :, :], k.gate[:, :, 1:NX], second[:, :, :], ALU.mult))
            link(dve.tensor_reduce(k.pair_gate[:, :, :], picked[:, :, :, :], AX_X, ALU.add))
            link(dve.tensor_tensor(passed_by[:, :, :], k.job_numbers[:, :].unsqueeze(2).to_broadcast([P, JOBS, E]),
                                   end[:, :].unsqueeze(1).to_broadcast([P, JOBS, E]), ALU.is_ge))
            link(dve.tensor_reduce(owner[:, :], passed_by[:, :, :], AX_X, ALU.add))
            link(dve.tensor_scalar(owner[:, :], owner[:, :], float(E - 1), None, ALU.min))
            link(dve.tensor_copy(k.job_expert[:, :], owner[:, :]))

            dve.tensor_copy(k.xn[:, :, D], k.pair_rows[:, 0, :])
            link(dve.tensor_tensor(owned[:, :, :], owner[:, :].unsqueeze(2).to_broadcast([P, JOBS, E]),
                                   k.expert_numbers[:, :].unsqueeze(1).to_broadcast([P, JOBS, E]), ALU.is_equal))
            link(dve.tensor_tensor(owned_b1[:, :, :, :], owned[:, :, :].unsqueeze(2).to_broadcast([P, JOBS, KH, E]),
                                   k.b1[:, 1:NX, :].rearrange("p e c -> p c e").unsqueeze(1).to_broadcast([P, JOBS, KH, E]),
                                   ALU.mult))
            link(dve.tensor_reduce(k.job_b1[:, :, :], owned_b1[:, :, :, :], AX_X, ALU.add))
            w.w1_low(dve, 0)
            w.w2_low(dve, 0)

        @block.tensor
        def _(pe):
            def turn(g, p, reuse):
                pe.wait_ge(xn_done, g + 1)
                if reuse:
                    pe.wait_ge(copied, g - 1)
                for kd in range(KD):
                    for t in range(GT):
                        last = pe.transpose(turn_ps[:, p, kd, t * P:(t + 1) * P], xn[:, p, t, kd * P:(kd + 1) * P],
                                            k.ident[:, :])
                last.then_inc(turned, 1)

            def route(g, p):
                pe.wait_ge(copied, g + 1)
                for t in range(GT):
                    for kd in range(KD):
                        last = pe.matmul(logit_ps[:, bass.ds((GT * g + t) * E, E)], xT32[:, p, kd, t * P:(t + 1) * P],
                                         k.router_w[:, kd, :], start=(kd == 0), stop=(kd == KD - 1))
                last.then_inc(logits_done, 1)

            turn(0, 0, False)
            turn(1, 1, False)
            route(0, 0)
            route(1, 1)
            with pe.Fori(1, G // 2) as j:
                turn(2 * j, 0, True)
                turn(2 * j + 1, 1, True)
                route(2 * j, 0)
                route(2 * j + 1, 1)

            pe.wait_ge(chosen_done, 1)
            for n, tri in enumerate((k.earlier, k.ones)):
                last = pe.matmul(count_ps[:, n, :, :].rearrange("p t e -> p (t e)"), tri[:, :],
                                 chosen[:, :, :].rearrange("p t e -> p (t e)"), start=True, stop=True)
            last.then_inc(counted, 1)

        @block.scalar
        def _(act):
            def copy(g, p, reuse):
                act.wait_ge(turned, g + 1)
                if reuse:
                    act.wait_ge(logits_done, g - 1)
                    act.wait_ge(lo_done, g - 1)
                for kd in range(KD):
                    last = act.activation(xT32[:, p, kd, :], turn_ps[:, p, kd, :], ACT.Copy)
                last.then_inc(copied, 1)
                act.wait_ge(copied, g + 1)
                act.activation(k.xT_hi[:, :, bass.ds(g * GN, GN)], xT32[:, p, :, :], ACT.Copy).then_inc(hi_done, 1)
                act.activation(k.xn[:, bass.ds(GT * g, GT), 0:D], xn[:, p, :, :], ACT.Copy).then_inc(kept, 1)

            copy(0, 0, False)
            copy(1, 1, False)
            with act.Fori(1, G // 2) as j:
                copy(2 * j, 0, True)
                copy(2 * j + 1, 1, True)
            act.wait_ge(exp_in, 1)
            act.activation(probs[:, :, :], probs[:, :, :], ACT.Exp).then_inc(exp_out, 1)
            w.w1_high(act, 0)
            w.w2_high(act, 0)


def experts(nc, k, dram, w, name):
    with ExitStack() as ctx:
        def sem(n):
            return nc.alloc_semaphore(f"{name}_{n}")

        def sb(n, shape, dt=F32):
            return ctx.enter_context(nc.sbuf_tensor(f"{name}_{n}", shape, dt))

        h32 = sb("h32", [P, KH, GN])
        h_hi, h_lo = sb("h_hi", [P, KH, GN], F32R), sb("h_lo", [P, KH, GN], F32R)
        rows_in = sb("rows_in", [P, GT, ROW])
        b2_in = sb("b2_in", [P, D])
        out_rows = sb("out_rows", [P, JOBS, GT])
        out_ids = sb("out_ids", [P, GT], mybir.dt.uint32)
        jobT_hi, jobT_lo = sb("jobT_hi", [P, KD, SLOTS], F32R), sb("jobT_lo", [P, KD, SLOTS], F32R)
        rows_out = sb("rows_out", [P, GT, D])
        HB = 4
        hid_ps = ctx.enter_context(nc.psum_tensor(f"{name}_hid_ps", [P, HB, GN], F32))
        turn_ps = ctx.enter_context(nc.psum_tensor(f"{name}_turn_ps", [P, KD, SLOTS], F32))
        out_ps = ctx.enter_context(nc.psum_tensor(f"{name}_out_ps", [P, GT // 2, 512], F32))

        scattered, rows_loaded, turned = sem("scattered"), sem("rows_loaded"), sem("turned")
        jobT_hi_done, job_split = sem("jobT_hi_done"), sem("job_split")
        hid_done, gelu_done, h_hi_done, h_split = sem("hid_done"), sem("gelu_done"), sem("h_hi_done"), sem("h_split")
        chunk_used, out_done, out_taken = sem("chunk_used"), sem("out_done"), sem("out_taken")
        rows_stored, b2_loaded, ids_done, rows_noted, based = (sem("rows_stored"), sem("b2_loaded"), sem("ids_done"),
                                                               sem("rows_noted"), sem("based"))
        first_half_in, first_rest_in, renamed = sem("first_half_in"), sem("first_rest_in"), sem("renamed")
        block = ctx.enter_context(nc.Block())
        w1_dram = dram["rw1"].rearrange("e (k p) h -> e p k h", p=P)
        w2_dram = dram["rw2"].rearrange("e (k p) d -> e p k d", p=P)
        x_dram = dram["slot_x"].rearrange("(j p t) d -> j p t d", t=GT, p=P)
        @block.gpsimd
        def _(pool):
            pool.wait_ge(k.slots_zeroed, 16 * JOBS * k.ffns)

            def scatter(a, tiles, sem):
                for t in tiles:
                    pool.indirect_dma_start(dram["slot_x"], bass.IndirectOffsetOnAxis(ap=k.slot_ids[:, a, t:t + 1], axis=0),
                                            k.xn[:, t, :], None).then_inc(sem, 16)

            halves = (range(TILES // 2), range(TILES // 2, TILES))
            sems = (first_half_in, first_rest_in)
            for tiles, sem in zip(halves, sems):
                scatter(0, tiles, sem)
            for n, (tiles, sem) in enumerate(zip(halves, sems)):
                pool.wait_ge(sem, 16 * len(tiles))
                pool.tensor_copy(k.xn[:, tiles[0]:tiles[-1] + 1, D], k.pair_rows[:, 1, tiles[0]:tiles[-1] + 1]).then_inc(renamed, 1)
                pool.wait_ge(renamed, n + 1)
                scatter(1, tiles, scattered)

            def store(j):
                pool.wait_ge(ids_done, j + 1)
                for t in range(GT):
                    wait_apart(pool, k, out_taken, GT * (G + j) + 2 * (t // 2) + 2)
                    pool.indirect_dma_start(dram["slot_y"], bass.IndirectOffsetOnAxis(ap=out_ids[:, t:t + 1], axis=0),
                                            rows_out[:, t, :], None).then_inc(rows_stored, 16)

            with pool.Fori(0, JOBS) as j:
                store(j)
            pool.wait_ge(rows_stored, 16 * GT * JOBS)

        @block.sync
        def _(sp):
            def one(ap, i):
                return ap[bass.ds(i, 1)].rearrange("o p a b -> p (o a) b")

            def load_w1(j, e):
                sp.wait_ge(w.w1_split, j + 1)
                sp.dma_start(w.w1_in[:, :, :], one(w1_dram, e)).then_inc(w.w1_loaded, 16)

            def load_w2(j, e):
                sp.wait_ge(w.w2_split, j + 1)
                sp.dma_start(w.w2_in[:, :, :], one(w2_dram, e)).then_inc(w.w2_loaded, 16)

            def load_b2(j, e, reuse):
                if reuse:
                    sp.wait_ge(out_taken, GT * (G + j))
                sp.dma_start(b2_in[:, :], dram["rb2"][bass.ds(e, 1)].to_broadcast([P, D])).then_inc(b2_loaded, 16)

            def expert_of(j):
                return sp.value_load(k.job_expert[0:1, bass.ds(j, 1)], min_val=0, max_val=E - 1)

            load_w1(0, expert_of(0))
            load_w1(1, expert_of(1))
            e = expert_of(0)
            load_w2(0, e)
            load_b2(0, e, False)
            with sp.Fori(1, JOBS - 1) as j:
                load_w1(j + 1, expert_of(j + 1))
                e = expert_of(j)
                load_w2(j, e)
                load_b2(j, e, True)
            e = expert_of(JOBS - 1)
            load_w2(JOBS - 1, e)
            load_b2(JOBS - 1, e, True)

        @block.scalar
        def _(act):
            def w1_high(n, i):
                act.wait_ge(hid_done, KH * i)
                w.w1_high(act, n)

            def w2_high(n, i):
                act.wait_ge(out_done, GT * i)
                w.w2_high(act, n)

            def hidden(bias, i, reuse):
                for c in range(KH):
                    if reuse:
                        act.wait_ge(h_split, KH * (i - 1) + c + 1)
                    wait_apart(act, k, hid_done, KH * i + c + 1)
                    act.activation(h32[:, c, :], hid_ps[:, c % HB, :], ACT.Gelu, bias=bias(c)).then_inc(gelu_done, 1)

            def high(i, reuse):
                for c in range(KH):
                    act.wait_ge(gelu_done, KH * i + c + 1)
                    if reuse and c < KH - 1:
                        act.wait_ge(chunk_used, (KH - 1) * (i - 1) + c + 1)
                    elif reuse:
                        act.wait_ge(out_done, GT * i)
                    act.activation(h_hi[:, c, :], h32[:, c, :], ACT.Copy).then_inc(h_hi_done, 1)

            def job_high(j, i):
                act.wait_ge(turned, j + 1)
                act.wait_ge(hid_done, KH * i)
                for kd in range(KD):
                    last = act.activation(jobT_hi[:, kd, :], turn_ps[:, kd, :], ACT.Copy)
                last.then_inc(jobT_hi_done, 1)

            def bias_of(j):
                return lambda c: k.job_b1[:, bass.ds(j, 1), c]

            def load_rows(j, reuse):
                if reuse:
                    act.wait_ge(turned, j)
                    act.wait_ge(rows_noted, j)
                act.dma_start(rows_in[:, :, :], x_dram[bass.ds(j, 1)].rearrange("o p t d -> p (o t) d")
                              ).then_inc(rows_loaded, 16)

            def shared_bias(c):
                return k.b1[:, 0, c:c + 1]

            def job(j, prefetch):
                hidden(bias_of(j), G + j, True)
                if prefetch:
                    job_high(j + 1, G + j + 1)
                    if prefetch > 1:
                        load_rows(j + 2, True)
                    w1_high(j + 2, G + j + 1)
                high(G + j, True)
                w2_high(j + 1, G + j)

            hidden(shared_bias, 0, False)
            high(0, False)
            with act.Fori(1, G) as g:
                hidden(shared_bias, g, True)
                high(g, True)
            w1_high(1, G)
            act.wait_ge(scattered, 16 * TILES)
            load_rows(0, False)
            job_high(0, G)
            load_rows(1, True)
            with act.Fori(0, JOBS - 2) as j:
                job(j, 2)
            job(JOBS - 2, 1)
            job(JOBS - 1, 0)

        @block.vector
        def _(dve):
            def low(i):
                for c in range(KH):
                    dve.wait_ge(h_hi_done, KH * i + c + 1)
                    dve.tensor_tensor(h_lo[:, c, :], h32[:, c, :], h_hi[:, c, :].bitcast(F32),
                                      ALU.subtract).then_inc(h_split, 1)

            def job_low(j):
                dve.wait_ge(jobT_hi_done, j + 1)
                dve.tensor_tensor(jobT_lo[:, :, :], turn_ps[:, :, :], jobT_hi[:, :, :].bitcast(F32),
                                  ALU.subtract).then_inc(job_split, 1)

            def base(g):
                xg = k.x[:, bass.ds(GT * g, GT), :]
                dve.tensor_tensor(xg, xg, k.half_sb2[:, :].unsqueeze(1).to_broadcast([P, GT, D]), ALU.add).then_inc(based, 1)

            def add(g):
                dve.wait_ge(based, g + 1)
                for a in range(GT // 2):
                    dve.wait_ge(out_done, GT * g + 2 * a + 2)
                    xt = k.x[:, bass.ds(GT * g + 2 * a, 2), :]
                    dve.scalar_tensor_tensor(out=xt, in0=out_ps[:, a, :].rearrange("p (t d) -> p t d", t=2), scalar=0.5,
                                             in1=xt, op0=ALU.mult, op1=ALU.add).then_inc(out_taken, 2)

            def take(j, reuse):
                dve.wait_ge(b2_loaded, 16 * j + 16)
                if reuse:
                    dve.wait_ge(rows_stored, 16 * GT * j)
                dve.tensor_copy(out_ids[:, :], out_rows[:, bass.ds(j, 1), :].rearrange("p o t -> p (o t)")).then_inc(ids_done, 1)
                for a in range(GT // 2):
                    dve.wait_ge(out_done, GT * (G + j) + 2 * a + 2)
                    dve.tensor_tensor(rows_out[:, 2 * a:2 * a + 2, :], out_ps[:, a, :].rearrange("p (t d) -> p t d", t=2),
                                      b2_in[:, :].unsqueeze(1).to_broadcast([P, 2, D]), ALU.add).then_inc(out_taken, 2)

            def note(j):
                dve.wait_ge(rows_loaded, 16 * j + 16)
                dve.tensor_copy(out_rows[:, bass.ds(j, 1), :].rearrange("p o t -> p (o t)"), rows_in[:, :, D]).then_inc(rows_noted, 1)

            base(0)
            low(0)
            with dve.Fori(1, G) as g:
                base(g)
                low(g)
                add(g - 1)
            w.w1_low(dve, 1)
            add(G - 1)
            note(0)
            job_low(0)

            def job(j):
                note(j + 1)
                job_low(j + 1)
                w.w1_low(dve, j + 2)
                low(G + j)

            job(0)
            w.w2_low(dve, 1)
            job(1)
            take(0, False)
            w.w2_low(dve, 2)
            with dve.Fori(2, JOBS - 1) as j:
                job(j)
                take(j - 1, True)
                w.w2_low(dve, j + 1)
            low(G + JOBS - 1)
            take(JOBS - 2, True)
            w.w2_low(dve, JOBS)
            take(JOBS - 1, True)

        @block.tensor
        def _(pe):
            def first(xs, i, start):
                for c in range(KH):
                    if not (start and c < HB):
                        pe.wait_ge(gelu_done, KH * i + c + 1 - HB)
                    passes = [(w1, xs(n, kd), kd) for kd in range(KD) for w1, n in ((w.w1_hi, 0), (w.w1_hi, 1), (w.w1_lo, 0))]
                    for n, (w1, x, kd) in enumerate(passes):
                        last = pe.matmul(hid_ps[:, c % HB, :], w1[:, kd, c * P:(c + 1) * P], x,
                                         start=(n == 0), stop=(n == len(passes) - 1))
                    last.then_inc(hid_done, 1)

            def second(i, reuse):
                for c in range(KH):
                    pe.wait_ge(h_split, KH * i + c + 1)
                    for t in range(GT):
                        if reuse and c == 0:
                            pe.wait_ge(out_taken, GT * (i - 1) + t + 1)
                        for n, (h, w2) in enumerate(((h_hi, w.w2_hi), (h_hi, w.w2_lo), (h_lo, w.w2_hi))):
                            last = pe.matmul(out_ps[:, t // 2, (t % 2) * D:(t % 2 + 1) * D], h[:, c, t * P:(t + 1) * P], w2[:, c, :],
                                             start=(c == 0 and n == 0 and t % 2 == 0), stop=(c == KH - 1 and n == 2), skip_group_check=True)
                        if c == KH - 1:
                            last.then_inc(out_done, 1)
                    if c < KH - 1:
                        last.then_inc(chunk_used, 1)

            def group(g):
                return lambda n, kd: (k.xT_hi, k.xT_lo)[n][:, kd, bass.ds(g * GN, GN)]

            def job_rows(n, kd):
                return (jobT_hi, jobT_lo)[n][:, kd, :]

            def turn(j, reuse):
                pe.wait_ge(rows_loaded, 16 * j + 16)
                if reuse:
                    pe.wait_ge(job_split, j)
                for kd in range(KD):
                    for t in range(GT):
                        last = pe.transpose(turn_ps[:, kd, t * P:(t + 1) * P], rows_in[:, t, kd * P:(kd + 1) * P], k.ident[:, :])
                last.then_inc(turned, 1)

            def job_first(j):
                pe.wait_ge(w.w1_split, j + 2)
                pe.wait_ge(job_split, j + 1)
                first(job_rows, G + j, False)

            pe.wait_ge(w.w1_split, 1)
            first(group(0), 0, True)
            pe.wait_ge(w.w2_split, 1)
            first(group(1), 1, False)
            second(0, False)
            with pe.Fori(2, G) as g:
                first(group(g), g, False)
                second(g - 1, True)
            second(G - 1, True)
            turn(0, False)
            job_first(0)
            turn(1, True)
            with pe.Fori(1, JOBS - 1) as j:
                job_first(j)
                turn(j + 1, True)
                pe.wait_ge(w.w2_split, j + 1)
                second(G + j - 1, True)
            job_first(JOBS - 1)
            pe.wait_ge(w.w2_split, JOBS)
            second(G + JOBS - 2, True)
            pe.wait_ge(w.w2_split, JOBS + 1)
            second(G + JOBS - 1, True)


def combine(nc, k, dram, name, stores):
    R = 2
    with ExitStack() as ctx:
        got = ctx.enter_context(nc.sbuf_tensor(f"{name}_got", [P, R, GT, TOP, D], F32))
        got_in = [nc.alloc_semaphore(f"{name}_got_in{r}") for r in range(R)]
        added = nc.alloc_semaphore(f"{name}_added")
        half_added = nc.alloc_semaphore(f"{name}_half_added")
        stored = nc.alloc_semaphore(f"{name}_stored")
        block = ctx.enter_context(nc.Block())
        y_rows = dram["slot_y"][0:TOP * T].rearrange("(g t p a) d -> g p t a d", t=GT, p=P, a=TOP)
        out_rows = dram["out"].rearrange("b n d -> (b n) d").rearrange("(g t p) d -> g p t d", t=GT, p=P)

        @block.sync
        def _(sp):
            def load(g, r, reuse):
                if reuse:
                    sp.wait_ge(added, GT * (g - R + 1))
                sp.dma_start(got[:, r, :, :, :], y_rows[bass.ds(g, 1)].rearrange("o p t a d -> p (o t) a d")
                             ).then_inc(got_in[r], 16)

            for r in range(R):
                load(r, r, False)
            with sp.Fori(1, G // R) as q:
                for r in range(R):
                    load(R * q + r, r, True)

        @block.scalar
        def _(act):
            if not stores:
                return
            with act.Fori(0, G) as g:
                act.wait_ge(added, GT * (g + 1))
                act.dma_start(out_rows[bass.ds(g, 1)].rearrange("o p t d -> p (o t) d"), k.x[:, bass.ds(GT * g, GT), :]
                              ).then_inc(stored, 16)
            act.wait_ge(stored, 16 * G)

        @block.vector
        def _(dve):
            with dve.Fori(0, G // R) as q:
                for r in range(R):
                    g = R * q + r
                    dve.wait_ge(got_in[r], 16 * (q + 1))
                    for a, done in ((0, half_added), (1, added)):
                        for t in range(GT):
                            if a:
                                dve.wait_ge(half_added, GT * g + t + 1)
                            xt = k.x[:, GT * g + t, :]
                            dve.scalar_tensor_tensor(out=xt, in0=got[:, r, t, a, :],
                                                     scalar=k.pair_gate[:, a, bass.ds(GT * g + t, 1)],
                                                     in1=xt, op0=ALU.mult, op1=ALU.add).then_inc(done, 1)


def attention(nc, k, dram):
    with ExitStack() as ctx:
        def sem(n):
            return ctx.enter_context(nc.semaphore(f"attn_{n}"))

        def sb(n, shape, dt=F32):
            return ctx.enter_context(nc.sbuf_tensor(f"attn_{n}", shape, dt))

        def bank(n):
            return ctx.enter_context(nc.psum_tensor(f"attn_{n}_ps", [P, 512], F32))

        w_in = sb("w_in", [P, KD, WALL])
        w_hi, w_lo = sb("w_hi", [P, KD, WALL], F32R), sb("w_lo", [P, KD, WALL], F32R)
        wo_in, wo_scaled = sb("wo_in", [P, NH, D]), sb("wo_scaled", [P, NH, D])
        wo_hi, wo_lo = sb("wo_hi", [P, NH, D], F32R), sb("wo_lo", [P, NH, D], F32R)
        gnorm = sb("gnorm", [P, 1])
        wgk = sb("wgk", [P, KD, NH])
        bgk = sb("bgk", [P, NH])
        upto = sb("upto", [P, P])
        causal = sb("causal", [P, P])
        stats = sb("stats", [P, GT, 6])
        mean_var = sb("mean_var", [P, GT, 2])
        var_eps = sb("var_eps", [P, GT])
        rstd = sb("rstd", [P, GT])
        xn = sb("xn", [P, GT, D])
        xT32 = sb("xT32", [P, KD, GN])
        xT_hi, xT_lo = sb("xT_hi", [P, KD, GN], F32R), sb("xT_lo", [P, KD, GN], F32R)
        z = sb("z", [P, GT, NH])
        z_min = sb("z_min", [P, GT, NH])
        z_abs = sb("z_abs", [P, GT, NH])
        z_exp = sb("z_exp", [P, GT, NH])
        z_log = sb("z_log", [P, GT, NH])
        decay = sb("decay", [P, GT, NH])
        kT = sb("kT", [P, 2, GN])
        q_pad = sb("q_pad", [P, 2, 2, GN])
        steps = sb("steps", [P, 2, NH, P])
        cum = sb("cum", [P, NH, P])
        cum_exp = sb("cum_exp", [P, 2, NH, P])
        cum_col = sb("cum_col", [P, NH])
        gap = sb("gap", [P, NH, P])
        gap_exp = sb("gap_exp", [P, NH, P])
        k_gap = sb("k_gap", [P, NH])
        k_fac = sb("k_fac", [P, NH])
        q_dec = sb("q_dec", [P, 2, 2, P])
        k_dec = sb("k_dec", [P, 2, NH, DK])
        v32 = sb("v32", [P, 2, NH * DV])
        score = sb("score", [P, 2, NH, P])
        tanh_g = sb("tanh_g", [P, NH * DV])
        gate = sb("gate", [P, 2, NH * DV])
        state = sb("state", [P, 2, 2, DV])
        o32 = sb("o32", [P, NH * DV])
        o_sq = sb("o_sq", [P, NH, DV])
        o_sum = sb("o_sum", [P, NH])
        o_mean = sb("o_mean", [P, NH])
        o_rstd = sb("o_rstd", [P, NH])
        o_gated = sb("o_gated", [P, NH * DV])
        oT_hi, oT_lo = sb("oT_hi", [P, NH * P], F32R), sb("oT_lo", [P, NH * P], F32R)
        cum_ps, score_ps, v_ps, g_ps = bank("cum"), bank("score"), bank("v"), bank("g")
        o_ps, s_ps, y_ps, k_ps = bank("o"), bank("s"), bank("y"), bank("k")
        COL, GK = NH * DK, NH * DK + 16

        loaded, w_hi_done, w_ready = sem("loaded"), sem("w_hi_done"), sem("w_ready")
        const_made, const_ready, wo_scaled_done = sem("const_made"), sem("const_ready"), sem("wo_scaled_done")
        stats_done, agg_done, eps_done, rstd_done = sem("stats_done"), sem("agg_done"), sem("eps_done"), sem("rstd_done")
        xn_done, turned, copied, hi_done, split_done = (sem("xn_done"), sem("turned"), sem("copied"), sem("hi_done"),
                                                        sem("split_done"))
        gk_done, z_done, z_abs_done, z_exp_done, z_log_done, z_min_done, log_sig_done, decay_done = (
            sem("gk_done"), sem("z_done"), sem("z_abs_done"), sem("z_exp_done"), sem("z_log_done"), sem("z_min_done"),
            sem("log_sig_done"), sem("decay_done"))
        qk_done, qk_copied = sem("qk_done"), sem("qk_copied")
        steps_done, k_done, score_done, cum_done, v_done, g_done = (
            sem("steps_done"), sem("k_done"), sem("score_done"), sem("cum_done"), sem("v_done"), sem("g_done"))
        cum_copied, cum_exp_done, col_copied, gap_done, gap_exp_done = (
            sem("cum_copied"), sem("cum_exp_done"), sem("col_copied"), sem("gap_done"), sem("gap_exp_done"))
        k_gap_done, k_fac_done, v_copied, tanh_done = sem("k_gap_done"), sem("k_fac_done"), sem("v_copied"), sem("tanh_done")
        q_dec_done, k_dec_done, masked, gated = sem("q_dec_done"), sem("k_dec_done"), sem("masked"), sem("gated")
        s_done, o_done, state_done = sem("s_done"), sem("o_done"), sem("state_done")
        o_copied, sq_done, sum_done, mean_done, o_rstd_done, o_gated_done = (
            sem("o_copied"), sem("sq_done"), sem("sum_done"), sem("mean_done"), sem("o_rstd_done"), sem("o_gated_done"))
        oT_done, oT_hi_done, oT_split, y_done, y_added = (
            sem("oT_done"), sem("oT_hi_done"), sem("oT_split"), sem("y_done"), sem("y_added"))
        block = ctx.enter_context(nc.Block())

        def states(b, c):
            return (GT - 1) * b + min(c + 1, GT - 1)

        def schedule(eng, slot, drain):
            for c in range(GT):
                slot(0, c, True)
            with eng.Fori(1, B - 1) as b:
                for c in range(GT):
                    slot(b, c, True)
            for c in range(GT):
                slot(B - 1, c, False)
            drain()

        def before(b, c, back):
            if c >= back:
                return b, c - back
            if isinstance(b, int) and b == 0:
                return None
            return b - 1, c - back + GT

        @block.sync
        def _(sp):
            for n, (name, width) in enumerate((("Wq", 256), ("Wk", 256), ("Wv", 512), ("Wg", 512))):
                at = (0, 256, 512, 1024)[n]
                sp.dma_start(w_in[:, :, at:at + width], dram[name].rearrange("(k p) n -> p k n", p=P)).then_inc(loaded, 16)
            sp.dma_start(wo_in[:, :, :], dram["Wo"].rearrange("(h p) d -> p h d", p=P)).then_inc(loaded, 16)
            sp.dma_start(gnorm[:, :], dram["gnorm_w"].rearrange("(p o) -> p o", o=1)).then_inc(loaded, 16)
            sp.dma_start(wgk[:, :, :], dram["Wgk"].rearrange("(k p) h -> p k h", p=P)).then_inc(loaded, 16)
            sp.dma_start(bgk[:, :], dram["bgk"].rearrange("(o h) -> o h", o=1).to_broadcast([P, NH])).then_inc(loaded, 16)
            zero_slots(sp, k, dram)
            sp.wait_ge(loaded, 128)

        @block.gpsimd
        def _(pool):
            pool.memset(causal[:, :], 0.0).then_inc(const_made, 1)
            pool.memset(q_pad[:, :, :, :], 0.0).then_inc(const_made, 1)
            pool.memset(state[:, :, :, :], 0.0).then_inc(const_made, 1)
            pool.wait_ge(const_made, 3)
            pool.affine_select(out=upto[:, :], in_=k.ones[:, :], compare_op=ALU.is_ge, fill=0.0, base=0,
                               pattern=[[1, P]], channel_multiplier=-1).then_inc(const_ready, 1)
            pool.affine_select(out=causal[:, :], in_=causal[:, :], compare_op=ALU.is_ge, fill=NEVER, base=0,
                               pattern=[[1, P]], channel_multiplier=-1).then_inc(const_ready, 1)
            pool.wait_ge(const_ready, 2)

            def norm_rsqrt(b):
                wait_apart(pool, k, agg_done, b + 1)
                pool.tensor_scalar(var_eps[:, :], mean_var[:, :, 1], EPS, None, ALU.add).then_inc(eps_done, 1)
                pool.wait_ge(eps_done, b + 1)
                pool.tensor_tensor(rstd[:, :], var_eps[:, :], k.neg_half[:, 0:GT], ALU.pow).then_inc(rstd_done, 1)

            def spread(b, c):
                n = GT * b + c
                if c == 0:
                    pool.wait_ge(decay_done, b + 1)
                if before(b, c, 2):
                    pool.wait_ge(cum_done, n - 1)
                pool.tensor_tensor(steps[:, c % 2, :, :], upto[:, :].unsqueeze(1).to_broadcast([P, NH, P]),
                                   decay[:, c, :].unsqueeze(2).to_broadcast([P, NH, P]), ALU.mult).then_inc(steps_done, 1)

            def out_rsqrt(b, c):
                n = GT * b + c
                wait_apart(pool, k, sum_done, n + 1)
                pool.tensor_scalar(o_mean[:, :], o_sum[:, :], 1.0 / DV, EPS, ALU.mult, ALU.add).then_inc(mean_done, 1)
                pool.wait_ge(mean_done, n + 1)
                pool.tensor_tensor(o_rstd[:, :], o_mean[:, :], k.neg_half[:, 0:NH], ALU.pow).then_inc(o_rstd_done, 1)

            def slot(b, c, more):
                if before(b, c, 2):
                    out_rsqrt(*before(b, c, 2))
                if c == 0:
                    spread(b, 0)
                if c < GT - 1:
                    spread(b, c + 1)
                if c == 1 and more:
                    norm_rsqrt(b + 1)

            def drain():
                out_rsqrt(B - 1, GT - 2)
                out_rsqrt(B - 1, GT - 1)

            norm_rsqrt(0)
            schedule(pool, slot, drain)

        @block.vector
        def _(dve):
            def statistics(b):
                for t in range(GT):
                    last = dve.bn_stats(stats[:, t, :], k.x[:, GT * b + t, :])
                last.then_inc(stats_done, 1)
                wait_apart(dve, k, stats_done, b + 1)
                for t in range(GT):
                    last = dve.bn_aggr(mean_var[:, t, :], stats[:, t, :])
                last.then_inc(agg_done, 1)

            def scale(b, reuse):
                if reuse:
                    dve.wait_ge(turned, b)
                dve.wait_ge(rstd_done, b + 1)
                for t in range(GT):
                    last = dve.tensor_scalar(xn[:, t, :], k.x[:, GT * b + t, :], mean_var[:, t, 0:1], rstd[:, t:t + 1],
                                             ALU.subtract, ALU.mult)
                last.then_inc(xn_done, 1)

            def split(b):
                dve.wait_ge(copied, b + 1)
                if before(b, 0, 1):
                    dve.wait_ge(g_done, GT * b)
                dve.tensor_copy(xT_hi[:, :, :], xT32[:, :, :]).then_inc(hi_done, 1)
                dve.wait_ge(hi_done, b + 1)
                dve.tensor_tensor(xT_lo[:, :, :], xT32[:, :, :], xT_hi[:, :, :].bitcast(F32), ALU.subtract).then_inc(split_done, 1)

            def logit(b):
                dve.wait_ge(gk_done, b + 1)
                dve.tensor_tensor(z[:, :, :], k_ps[:, GK:GK + GT * NH].rearrange("p (t h) -> p t h", h=NH),
                                  bgk[:, :].unsqueeze(1).to_broadcast([P, GT, NH]), ALU.add).then_inc(z_done, 1)
                dve.wait_ge(z_done, b + 1)
                dve.scalar_tensor_tensor(out=z_abs[:, :, :], in0=z[:, :, :], scalar=-1.0, in1=z[:, :, :],
                                         op0=ALU.mult, op1=ALU.min).then_inc(z_abs_done, 1)
                dve.tensor_scalar(z_min[:, :, :], z[:, :, :], 0.0, None, ALU.min).then_inc(z_min_done, 1)

            def log_sigmoid(b):
                dve.wait_ge(z_log_done, b + 1)
                dve.wait_ge(z_min_done, b + 1)
                if before(b, 0, 1):
                    dve.wait_ge(steps_done, GT * b)
                dve.tensor_tensor(z_min[:, :, :], z_min[:, :, :], z_log[:, :, :], ALU.subtract).then_inc(log_sig_done, 1)
                dve.wait_ge(log_sig_done, b + 1)
                dve.tensor_scalar(decay[:, :, :], z_min[:, :, :], 1.0 / GLN, None, ALU.mult).then_inc(decay_done, 1)

            def gaps(b, c):
                n = GT * b + c
                dve.wait_ge(cum_done, n + 1)
                dve.tensor_copy(cum_col[:, :], k_ps[:, COL:COL + NH]).then_inc(col_copied, 1)
                dve.wait_ge(col_copied, n + 1)
                dve.wait_ge(cum_copied, n + 1)
                if before(b, c, 1):
                    dve.wait_ge(k_fac_done, n)
                    dve.wait_ge(gap_exp_done, n)
                dve.tensor_tensor(k_gap[:, :], cum[:, :, P - 1], cum_col[:, :], ALU.subtract).then_inc(k_gap_done, 1)
                for h in range(NH):
                    last = dve.scalar_tensor_tensor(out=gap[:, h, :], in0=cum[:, h, :], scalar=cum_col[:, h:h + 1],
                                                    in1=causal[:, :], op0=ALU.subtract, op1=ALU.min)
                last.then_inc(gap_done, 1)

            def decayed(b, c):
                n = GT * b + c
                dve.wait_ge(cum_exp_done, n + 1)
                if c == 0:
                    dve.wait_ge(qk_copied, 4 * (b + 1))
                if before(b, c, 2):
                    dve.wait_ge(o_done, n - 1)
                for i in range(2):
                    rows = slice(DK * i, DK * i + DK)
                    last = dve.tensor_tensor(q_dec[rows, c % 2, :, :], q_pad[rows, :, i, c * P:(c + 1) * P],
                                             cum_exp[rows, c % 2, i:NH:2, :], ALU.mult)
                last.then_inc(q_dec_done, 1)
                dve.wait_ge(k_done, n + 1)
                dve.wait_ge(k_fac_done, n + 1)
                dve.tensor_tensor(k_dec[:, c % 2, :, :], k_ps[:, 0:NH * DK].rearrange("p (h d) -> p h d", h=NH),
                                  k_fac[:, :].unsqueeze(2).to_broadcast([P, NH, DK]), ALU.mult).then_inc(k_dec_done, 1)

            def mask(b, c):
                n = GT * b + c
                dve.wait_ge(score_done, n + 1)
                dve.wait_ge(gap_exp_done, n + 1)
                dve.tensor_tensor(score[:, c % 2, :, :], score_ps[:, :].rearrange("p (h t) -> p h t", h=NH),
                                  gap_exp[:, :, :], ALU.mult).then_inc(masked, 1)

            def swish(b, c):
                n = GT * b + c
                dve.wait_ge(tanh_done, n + 1)
                if before(b, c, 2):
                    dve.wait_ge(o_gated_done, n - 1)
                dve.scalar_tensor_tensor(out=gate[:, c % 2, :], in0=tanh_g[:, :], scalar=1.0, in1=g_ps[:, :],
                                         op0=ALU.add, op1=ALU.mult).then_inc(gated, 1)

            def update(b, c):
                n = GT * b + c
                dve.wait_ge(o_done, n + 1)
                if before(b, c, 1):
                    dve.wait_ge(state_done, states(*before(b, c, 1)))
                new = s_ps[:, :].rearrange("p (a i d) -> p a i d", a=2, i=2)
                for i in range(2):
                    rows = slice(DK * i, DK * i + DK)
                    if c == 0:
                        last = dve.tensor_copy(state[rows, :, i, :], new[rows, :, i, :])
                        continue
                    for a in range(2):
                        last = dve.scalar_tensor_tensor(out=state[rows, a, i, :], in0=state[rows, a, i, :],
                                                        scalar=cum_exp[rows, c % 2, 2 * a + i, P - 1:P],
                                                        in1=new[rows, a, i, :], op0=ALU.mult, op1=ALU.add)
                last.then_inc(state_done, 1)

            def square_sum(b, c):
                n = GT * b + c
                dve.wait_ge(sq_done, n + 1)
                if before(b, c, 1):
                    dve.wait_ge(mean_done, n)
                dve.tensor_reduce(o_sum[:, :], o_sq[:, :, :], AX_X, ALU.add).then_inc(sum_done, 1)

            def gate_out(b, c):
                n = GT * b + c
                dve.wait_ge(o_rstd_done, n + 1)
                if before(b, c, 1):
                    dve.wait_ge(oT_done, n)
                for h in range(NH):
                    cols = slice(h * DV, (h + 1) * DV)
                    last = dve.scalar_tensor_tensor(out=o_gated[:, cols], in0=o32[:, cols], scalar=o_rstd[:, h:h + 1],
                                                    in1=gate[:, c % 2, cols], op0=ALU.mult, op1=ALU.mult)
                last.then_inc(o_gated_done, 1)

            def out_low(b, c):
                n = GT * b + c
                dve.wait_ge(oT_hi_done, n + 1)
                dve.tensor_tensor(oT_lo[:, :], y_ps[:, :], oT_hi[:, :].bitcast(F32), ALU.subtract).then_inc(oT_split, 1)

            def add_out(b, c):
                n = GT * b + c
                dve.wait_ge(y_done, n + 1)
                xt = k.x[:, n, :]
                dve.tensor_tensor(xt, y_ps[:, 0:D], xt, ALU.add).then_inc(y_added, 1)

            def slot(b, c, more):
                mid, tail = before(b, c, 1), before(b, c, 2)
                if tail:
                    square_sum(*tail)
                if c == 0:
                    logit(b)
                if c == 3 and more:
                    scale(b + 1, True)
                if tail:
                    gate_out(*tail)
                if c == 0:
                    log_sigmoid(b)
                    if tail:
                        out_low(*tail)
                gaps(b, c)
                decayed(b, c)
                if tail and c:
                    out_low(*tail)
                mask(b, c)
                swish(b, c)
                if mid and c:
                    update(*mid)
                if tail:
                    add_out(*tail)
                if c == 1 and more:
                    statistics(b + 1)
                if c == 3 and more:
                    split(b + 1)

            def drain():
                for c in (GT - 2, GT - 1):
                    square_sum(B - 1, c)
                    gate_out(B - 1, c)
                    out_low(B - 1, c)
                    add_out(B - 1, c)

            dve.wait_ge(loaded, 128)
            for h in range(NH):
                last = dve.tensor_scalar(wo_scaled[:, h, :], wo_in[:, h, :], gnorm[:, 0:1], 0.5, ALU.mult, ALU.mult)
            last.then_inc(wo_scaled_done, 1)
            dve.wait_ge(w_hi_done, 1)
            dve.tensor_tensor(w_lo[:, :, :], w_in[:, :, :], w_hi[:, :, :].bitcast(F32), ALU.subtract).then_inc(w_ready, 1)
            dve.wait_ge(w_hi_done, 2)
            dve.tensor_tensor(wo_lo[:, :, :], wo_scaled[:, :, :], wo_hi[:, :, :].bitcast(F32), ALU.subtract).then_inc(w_ready, 1)
            dve.wait_ge(const_ready, 2)
            statistics(0)
            scale(0, False)
            split(0)
            schedule(dve, slot, drain)

        @block.scalar
        def _(act):
            def copy(b):
                act.wait_ge(turned, b + 1)
                if before(b, 0, 1):
                    act.wait_ge(gk_done, b)
                    act.wait_ge(split_done, b)
                act.activation(xT32[:, 0, :], v_ps[:, :], ACT.Copy)
                act.activation(xT32[:, 1, :], g_ps[:, :], ACT.Copy).then_inc(copied, 1)

            def log1p_exp(b):
                act.wait_ge(z_abs_done, b + 1)
                act.activation(z_exp[:, :, :], z_abs[:, :, :], ACT.Exp).then_inc(z_exp_done, 1)
                act.wait_ge(z_exp_done, b + 1)
                act.activation(z_log[:, :, :], z_exp[:, :, :], ACT.Ln, bias=1.0).then_inc(z_log_done, 1)

            def qk_copy(b):
                if before(b, 0, 1):
                    act.wait_ge(score_done, GT * b)
                    act.wait_ge(q_dec_done, GT * b)
                else:
                    act.wait_ge(const_ready, 2)
                for a, ps in enumerate((cum_ps, score_ps)):
                    act.wait_ge(qk_done, 4 * b + a + 1)
                    act.activation(kT[:, a, :], ps[:, :], ACT.Copy).then_inc(qk_copied, 1)
                for a, ps in enumerate((v_ps, g_ps)):
                    act.wait_ge(qk_done, 4 * b + a + 3)
                    act.activation(q_pad[0:DK, a, 0, :], ps[0:DK, :], ACT.Copy, scale=DK ** -0.5)
                    act.activation(q_pad[DK:P, a, 1, :], ps[DK:P, :], ACT.Copy, scale=DK ** -0.5).then_inc(qk_copied, 1)

            def front(b, c, tail):
                n = GT * b + c
                act.wait_ge(v_done, n + 1)
                if before(b, c, 2):
                    act.wait_ge(o_done, n - 1)
                act.activation(v32[:, c % 2, :], v_ps[:, :], ACT.Copy).then_inc(v_copied, 1)
                act.wait_ge(cum_done, n + 1)
                if before(b, c, 1):
                    act.wait_ge(gap_done, n)
                act.activation(cum[:, :, :], cum_ps[:, :].rearrange("p (h t) -> p h t", h=NH), ACT.Copy).then_inc(cum_copied, 1)
                act.wait_ge(cum_copied, n + 1)
                if before(b, c, 2):
                    act.wait_ge(state_done, states(*before(b, c, 2)))
                    act.wait_ge(q_dec_done, n - 1)
                act.activation(cum_exp[:, c % 2, :, :], cum[:, :, :], ACT.Exp).then_inc(cum_exp_done, 1)
                act.wait_ge(k_gap_done, n + 1)
                if before(b, c, 1):
                    act.wait_ge(k_dec_done, n)
                act.activation(k_fac[:, :], k_gap[:, :], ACT.Exp).then_inc(k_fac_done, 1)
                if tail:
                    out_high(*tail)
                act.wait_ge(gap_done, n + 1)
                if before(b, c, 1):
                    act.wait_ge(masked, n)
                act.activation(gap_exp[:, :, :], gap[:, :, :], ACT.Exp).then_inc(gap_exp_done, 1)
                act.wait_ge(g_done, n + 1)
                if before(b, c, 1):
                    act.wait_ge(gated, n)
                act.activation(tanh_g[:, :], g_ps[:, :], ACT.Tanh, scale=0.5).then_inc(tanh_done, 1)

            def out_copy(b, c):
                n = GT * b + c
                act.wait_ge(o_done, n + 1)
                if before(b, c, 1):
                    act.wait_ge(o_gated_done, n)
                    act.wait_ge(sum_done, n)
                act.activation(o32[:, :], o_ps[:, :], ACT.Copy).then_inc(o_copied, 1)
                act.wait_ge(o_copied, n + 1)
                act.activation(o_sq[:, :, :].rearrange("p h d -> p (h d)"), o32[:, :], ACT.Square).then_inc(sq_done, 1)

            def out_high(b, c):
                n = GT * b + c
                act.wait_ge(oT_done, n + 1)
                if before(b, c, 1):
                    act.wait_ge(y_done, n)
                act.activation(oT_hi[:, :], y_ps[:, :], ACT.Copy).then_inc(oT_hi_done, 1)

            def slot(b, c, more):
                tail = before(b, c, 2)
                if tail:
                    out_copy(*tail)
                if c == 0:
                    copy(b)
                    log1p_exp(b)
                    qk_copy(b)
                    if tail:
                        out_high(*tail)
                front(b, c, tail if c else None)

            def drain():
                for c in (GT - 2, GT - 1):
                    out_copy(B - 1, c)
                    out_high(B - 1, c)

            act.wait_ge(loaded, 128)
            act.activation(w_hi[:, :, :], w_in[:, :, :], ACT.Copy).then_inc(w_hi_done, 1)
            act.wait_ge(wo_scaled_done, 1)
            act.activation(wo_hi[:, :, :], wo_scaled[:, :, :], ACT.Copy).then_inc(w_hi_done, 1)
            schedule(act, slot, drain)

        @block.tensor
        def _(pe):
            def product(out, pairs):
                for i, (w, x) in enumerate(pairs):
                    last = pe.matmul(out, w, x, start=(i == 0), stop=(i == len(pairs) - 1))
                return last

            def turn(b):
                pe.wait_ge(xn_done, b + 1)
                if before(b, 0, 1):
                    pe.wait_ge(v_copied, GT * b)
                    pe.wait_ge(gated, GT * b)
                for kd, ps in enumerate((v_ps, g_ps)):
                    for t in range(GT):
                        last = pe.transpose(ps[:, t * P:(t + 1) * P], xn[:, t, kd * P:(kd + 1) * P], k.ident[:, :])
                last.then_inc(turned, 1)

            def decay_logits(b):
                pe.wait_ge(copied, b + 1)
                if before(b, 0, 1):
                    pe.wait_ge(k_dec_done, GT * b)
                for t in range(GT):
                    last = product(k_ps[:, GK + NH * t:GK + NH * (t + 1)],
                                   [(xT32[:, kd, t * P:(t + 1) * P], wgk[:, kd, :]) for kd in range(KD)])
                last.then_inc(gk_done, 1)

            def qk(b):
                pe.wait_ge(split_done, b + 1)
                if before(b, 0, 1):
                    pe.wait_ge(cum_copied, GT * b)
                    pe.wait_ge(masked, GT * b)
                for ps, at in ((cum_ps, 256), (score_ps, 384), (v_ps, 0), (g_ps, 128)):
                    product(ps[:, :], [(w[:, kd, at:at + P], x[:, kd, :]) for kd in range(KD)
                                       for w, x in ((w_hi, xT_hi), (w_hi, xT_lo), (w_lo, xT_hi))]).then_inc(qk_done, 1)

            def rows(out, b, c, at, width):
                toks = slice(c * P, (c + 1) * P)
                return product(out, [(x[:, kd, toks], w[:, kd, at:at + width]) for kd in range(KD)
                                     for x, w in ((xT_hi, w_hi), (xT_hi, w_lo), (xT_lo, w_hi))])

            def front(b, c):
                n = GT * b + c
                if c:
                    pe.wait_ge(v_copied, n)
                else:
                    pe.wait_ge(qk_copied, 4 * (b + 1))
                rows(v_ps[:, :], b, c, 512, 512).then_inc(v_done, 1)
                if before(b, c, 1):
                    pe.wait_ge(k_dec_done, n)
                if c == 0:
                    pe.wait_ge(z_done, b + 1)
                rows(k_ps[:, 0:NH * DK], b, c, 256, 256).then_inc(k_done, 1)
                pe.wait_ge(steps_done, n + 1)
                product(k_ps[:, COL:COL + NH], [(upto[:, :], decay[:, c, :])])
                if c:
                    pe.wait_ge(cum_copied, n)
                product(cum_ps[:, :], [(k.ones[:, :], steps[:, c % 2, :, :].rearrange("p h t -> p (h t)"))]).then_inc(cum_done, 1)
                if c:
                    pe.wait_ge(masked, n)
                for a in range(2):
                    last = product(score_ps[:, 256 * a:256 * a + 256],
                                   [(kT[:, a, c * P:(c + 1) * P], q_pad[:, a, :, c * P:(c + 1) * P])])
                last.then_inc(score_done, 1)
                if c:
                    pe.wait_ge(gated, n)
                rows(g_ps[:, :], b, c, 1024, 512).then_inc(g_done, 1)

            def mid(b, c):
                n = GT * b + c
                pe.wait_ge(v_copied, n + 1)
                pe.wait_ge(k_dec_done, n + 1)
                pe.wait_ge(masked, n + 1)
                if before(b, c, 1):
                    pe.wait_ge(state_done, states(*before(b, c, 1)))
                    pe.wait_ge(o_copied, n)
                if c < GT - 1:
                    for a in range(2):
                        last = product(s_ps[:, 256 * a:256 * a + 256],
                                       [(k_dec[:, c % 2, 2 * a:2 * a + 2, :].rearrange("p h d -> p (h d)"),
                                         v32[:, c % 2, 256 * a:256 * a + 256])])
                    last.then_inc(s_done, 1)
                for a in range(2):
                    if c:
                        pe.matmul(o_ps[:, 256 * a:256 * a + 256], q_dec[:, c % 2, a, :],
                                  state[:, a, :, :].rearrange("p i d -> p (i d)"), start=True, stop=True,
                                  skip_group_check=True)
                    for h in (2 * a, 2 * a + 1):
                        cols = slice(h * DV, (h + 1) * DV)
                        last = pe.matmul(o_ps[:, cols], score[:, c % 2, h, :], v32[:, c % 2, cols],
                                         start=(c == 0), stop=True, skip_group_check=True)
                last.then_inc(o_done, 1)

            def turn_out(b, c):
                n = GT * b + c
                pe.wait_ge(o_gated_done, n + 1)
                if before(b, c, 1):
                    pe.wait_ge(y_added, n)
                for h in range(NH):
                    last = pe.transpose(y_ps[:, h * P:(h + 1) * P], o_gated[:, h * DV:(h + 1) * DV], k.ident[:, :])
                last.then_inc(oT_done, 1)

            def project(b, c):
                pe.wait_ge(oT_split, GT * b + c + 1)
                product(y_ps[:, 0:D], [(o[:, h * P:(h + 1) * P], w[:, h, :]) for h in range(NH)
                                       for o, w in ((oT_hi, wo_hi), (oT_hi, wo_lo), (oT_lo, wo_hi))]).then_inc(y_done, 1)

            def slot(b, c, more):
                m, tail = before(b, c, 1), before(b, c, 2)
                if c == 0:
                    if m:
                        mid(*m)
                    decay_logits(b)
                    qk(b)
                    if m:
                        turn_out(*tail)
                    front(b, 0)
                    if m:
                        project(*tail)
                    return
                front(b, c)
                if tail:
                    turn_out(*tail)
                mid(*m)
                if tail:
                    project(*tail)
                if c == 3 and more:
                    turn(b + 1)

            def drain():
                mid(B - 1, GT - 1)
                for c in (GT - 2, GT - 1):
                    turn_out(B - 1, c)
                    project(B - 1, c)

            pe.wait_ge(w_ready, 2)
            pe.wait_ge(const_ready, 2)
            turn(0)
            schedule(pe, slot, drain)


def store(nc, k, dram):
    with ExitStack() as ctx:
        stored = ctx.enter_context(nc.semaphore("stored"))
        block = ctx.enter_context(nc.Block())
        rows = dram["out"].rearrange("b n d -> (b n) d").rearrange("(t p) d -> p t d", p=P)

        @block.sync
        def _(sp):
            for g in range(4):
                sp.dma_start(rows[:, 8 * g:8 * g + 8, :], k.x[:, 8 * g:8 * g + 8, :]).then_inc(stored, 16)
            sp.wait_ge(stored, 64)


def macaron(nc, dram, parts=("ffn1", "attn", "ffn2")):
    k = Core()
    with ExitStack() as ctx:
        def sb(n, shape, dt=F32):
            return ctx.enter_context(nc.sbuf_tensor(n, shape, dt))

        k.x = sb("x", [P, TILES, D])
        k.ident = sb("ident", [P, P])
        k.neg_half = sb("neg_half", [P, GT])
        k.router_w = sb("router_w", [P, KD, E])
        k.router_b = sb("router_b", [P, E])
        k.b1 = sb("b1", [P, NX, KH])
        k.half_sb2 = sb("half_sb2", [P, D])
        k.job_b1 = sb("job_b1", [P, JOBS, KH])
        k.pair_rows = sb("pair_rows", [P, TOP, TILES])
        k.gate = sb("gate", [P, TILES, NX])
        k.ones = sb("ones", [P, P])
        k.zero_rows = sb("zero_rows", [P, SLOTS // P, ROW])
        k.earlier = sb("earlier", [P, P])
        k.lower = sb("lower", [P, E, E])
        k.job_starts = sb("job_starts", [P, T // SLOTS])
        k.expert_numbers = sb("expert_numbers", [P, E])
        k.job_numbers = sb("job_numbers", [P, JOBS])
        k.slot_ids = sb("slot_ids", [P, TOP, TILES], mybir.dt.uint32)
        k.pair_gate = sb("pair_gate", [P, TOP, TILES])
        k.job_expert = sb("job_expert", [P, JOBS], mybir.dt.int32)
        k.slots_zeroed = ctx.enter_context(nc.semaphore("slots_zeroed"))
        dram["slot_x"] = nc.dram_tensor("slot_x", (JOBS * SLOTS, ROW), F32, kind="Internal").ap()
        dram["slot_y"] = nc.dram_tensor("slot_y", (TOP * T + SLOTS, D), F32, kind="Internal").ap()
        k.passed = ctx.enter_context(nc.semaphore("passed"))
        k.ffns = 0
        constants(nc, k, dram)
        for part in parts:
            if part == "attn":
                attention(nc, k, dram)
                continue
            with nc.cleanup_on_exit():
                with ExitStack() as phase:
                    k.xn = phase.enter_context(nc.sbuf_tensor(f"{part}_xn", [P, TILES, ROW], F32))
                    k.xT_hi = phase.enter_context(nc.sbuf_tensor(f"{part}_xT_hi", [P, KD, T], F32R))
                    k.xT_lo = phase.enter_context(nc.sbuf_tensor(f"{part}_xT_lo", [P, KD, T], F32R))
                    w = Weights(nc, phase, part)
                    k.ffns += 1
                    normalise(nc, k, dram, w, f"{part}_norm")
                    experts(nc, k, dram, w, f"{part}_experts")
                combine(nc, k, dram, f"{part}_combine", part == parts[-1])
        if parts[-1] == "attn":
            store(nc, k, dram)


_INS = {"L0_attn_x": "x", "L0_attn_Wq": "Wq", "L0_attn_Wk": "Wk", "L0_attn_Wv": "Wv", "L0_attn_Wg": "Wg",
        "L0_attn_Wgk": "Wgk", "L0_attn_bgk": "bgk", "L0_attn_Wo": "Wo", "L0_attn_gnorm_w": "gnorm_w",
        "L0_ffn_router_w": "router_w", "L0_ffn_router_b": "router_b", "L0_ffn_sw1": "sw1", "L0_ffn_sb1": "sb1",
        "L0_ffn_sw2": "sw2", "L0_ffn_sb2": "sb2", "L0_ffn_rw1": "rw1", "L0_ffn_rb1": "rb1", "L0_ffn_rw2": "rw2",
        "L0_ffn_rb2": "rb2"}


def kernel(**inputs):
    import numpy as _np
    import concourse.bacc as _bacc
    from concourse import mybir as _mybir
    from concourse.bass_utils import run_bass_kernel_spmd as _run

    nc = _bacc.Bacc("TRN2", target_bir_lowering=False, num_devices=1)
    arrays, dram = {}, {}
    for name, short in _INS.items():
        a = _np.ascontiguousarray(inputs[name])
        arrays[f"in_{short}"] = a
        dram[short] = nc.dram_tensor(f"in_{short}", a.shape, _mybir.dt.from_np(a.dtype), kind="ExternalInput").ap()
    shape = inputs["L0_attn_x"].shape
    dram["out"] = nc.dram_tensor("out_x", shape, _mybir.dt.float32, kind="ExternalOutput").ap()
    macaron(nc, dram)
    r = _run(nc, [arrays], core_ids=[0])
    return r.results[0]["out_x"]
```

```python
from contextlib import ExitStack

import numpy as np

import concourse.bass as bass
from concourse import mybir

P = 128
F32 = mybir.dt.float32
F32R = mybir.dt.float32r
ALU = mybir.AluOpType
ACT = mybir.ActivationFunctionType
AX_X = mybir.AxisListType.X

T = 4096
D = 256
TILES = T // P
GT = 4
G = TILES // GT
GN = GT * P
KD = D // P
H = 512
KH = H // P
E = 8
NX = E + 1
TOP = 2
SLOTS = GN
ROW = D + 1
JOBS = TOP * T // SLOTS + E - 1
EPS = 1e-5
B = 8
NH, DK, DV = 4, 64, 128
WALL = 2 * NH * DK + 2 * NH * DV
GLN = 16.0
NEVER = -1e4


def wait_apart(eng, k, sem, value):
    eng.wait_ge(sem, value)
    eng.sem_inc(k.passed, 1)


class Core:
    pass


def zero_slots(eng, k, dram):
    with eng.Fori(0, JOBS) as j:
        eng.dma_start(dram["slot_x"].rearrange("(j p r) d -> j p r d", p=P, r=SLOTS // P)[bass.ds(j, 1)]
                      .rearrange("o p r d -> p (o r) d"), k.zero_rows[:, :, :]).then_inc(k.slots_zeroed, 16)


def constants(nc, k, dram):
    with ExitStack() as ctx:
        small_in = ctx.enter_context(nc.semaphore("small_in"))
        zeroed = ctx.enter_context(nc.semaphore("zeroed"))
        slots_named = ctx.enter_context(nc.semaphore("slots_named"))
        built = ctx.enter_context(nc.semaphore("built"))
        turned = ctx.enter_context(nc.semaphore("turned"))
        b1_rows = ctx.enter_context(nc.sbuf_tensor("b1_rows", [NX * KH, P], F32))
        ps = ctx.enter_context(nc.psum_tensor("const_ps", [P, 512], F32))
        sb2 = ctx.enter_context(nc.sbuf_tensor("sb2_rows", [P, D], F32))
        all_ones = ctx.enter_context(nc.sbuf_tensor("all_ones", [P, E, E], F32))
        block = ctx.enter_context(nc.Block())
        x_rows = dram["x"].rearrange("b n d -> (b n) d").rearrange("(t p) d -> p t d", p=P)

        @block.sync
        def _(sp):
            for g in range(4):
                if g == 1:
                    sp.wait_ge(small_in, 80)
                sp.dma_start(k.x[:, 8 * g:8 * g + 8, :], x_rows[:, 8 * g:8 * g + 8, :]).then_inc(k.x_in[g], 16)
            sp.wait_ge(slots_named, 1)

        @block.scalar
        def _(act):
            act.dma_start(b1_rows[0:KH, :], dram["sb1"].rearrange("(c p) -> c p", p=P)).then_inc(small_in, 16)
            act.dma_start(b1_rows[KH:NX * KH, :],
                          dram["rb1"].rearrange("e (c p) -> (e c) p", p=P)).then_inc(small_in, 16)
            act.dma_start(k.router_w[:, :, :], dram["router_w"].rearrange("(k p) e -> p k e", p=P)).then_inc(small_in, 16)
            act.dma_start(k.router_b[:, :], dram["router_b"].rearrange("(o e) -> o e", o=1).to_broadcast([P, E])
                          ).then_inc(small_in, 16)
            act.dma_start(sb2[:, :], dram["sb2"].rearrange("(o d) -> o d", o=1).to_broadcast([P, D])).then_inc(small_in, 16)
            act.wait_ge(small_in, 80)

        @block.gpsimd
        def _(pool):
            pool.memset(k.ident[:, :], 0.0).then_inc(zeroed, 1)
            pool.memset(k.neg_half[:, :], -0.5).then_inc(zeroed, 1)
            pool.memset(k.zero_rows[:, :, :], 0.0).then_inc(zeroed, 1)
            pool.wait_ge(zeroed, 3)
            pool.iota(k.zero_rows[:, :, D], pattern=[[1, SLOTS // P]], base=TOP * T, channel_multiplier=SLOTS // P,
                      allow_small_or_imprecise_dtypes=True).then_inc(slots_named, 1)
            pool.memset(all_ones[:, :, :], 1.0).then_inc(zeroed, 1)
            pool.memset(k.ones[:, :], 1.0).then_inc(zeroed, 1)
            pool.iota(k.job_starts[:, :], pattern=[[SLOTS, T // SLOTS]], base=0, channel_multiplier=0,
                      allow_small_or_imprecise_dtypes=True).then_inc(zeroed, 1)
            pool.iota(k.expert_numbers[:, :], pattern=[[1, E]], base=0, channel_multiplier=0,
                      allow_small_or_imprecise_dtypes=True).then_inc(zeroed, 1)
            pool.iota(k.job_numbers[:, :], pattern=[[1, JOBS]], base=0, channel_multiplier=0,
                      allow_small_or_imprecise_dtypes=True).then_inc(zeroed, 1)
            pool.iota(k.pair_rows[:, :, :], pattern=[[1, TOP], [TOP * P, TILES]], base=0, channel_multiplier=TOP,
                      allow_small_or_imprecise_dtypes=True).then_inc(zeroed, 1)
            pool.wait_ge(zeroed, 9)
            pool.affine_select(out=k.earlier[:, :], in_=k.ones[:, :], compare_op=ALU.is_ge, fill=0.0, base=-1,
                               pattern=[[1, P]], channel_multiplier=-1).then_inc(built, 1)
            pool.affine_select(out=k.lower[:, :, :], in_=all_ones[:, :, :], compare_op=ALU.is_ge, fill=0.0, base=-1,
                               pattern=[[1, E], [-1, E]], channel_multiplier=0).then_inc(built, 1)
            pool.affine_select(out=k.ident[:, :], in_=k.ident[:, :], compare_op=ALU.not_equal, fill=1.0,
                               base=0, pattern=[[-1, P]], channel_multiplier=1).then_inc(built, 1)

        @block.tensor
        def _(pe):
            pe.wait_ge(built, 3)
            pe.wait_ge(small_in, 80)
            pe.transpose(ps[:, 0:NX * KH], b1_rows[:, :], k.ident[0:NX * KH, 0:NX * KH]).then_inc(turned, 1)

        @block.vector
        def _(dve):
            dve.wait_ge(turned, 1)
            dve.tensor_copy(k.b1[:, :, :], ps[:, 0:NX * KH].rearrange("p (x c) -> p x c", x=NX)).then_inc(built, 1)
            dve.tensor_scalar(k.half_sb2[:, :], sb2[:, :], 0.5, None, ALU.mult).then_inc(built, 1)


class Weights:

    def __init__(self, nc, ctx, name):
        def sb(n, shape, dt=F32):
            return ctx.enter_context(nc.sbuf_tensor(f"{name}_{n}", shape, dt))

        def sem(n):
            return nc.alloc_semaphore(f"{name}_{n}")

        self.w1_in, self.w2_in = sb("w1_in", [P, KD, H]), sb("w2_in", [P, KH, D])
        self.w1_hi, self.w1_lo = sb("w1_hi", [P, KD, H], F32R), sb("w1_lo", [P, KD, H], F32R)
        self.w2_hi, self.w2_lo = sb("w2_hi", [P, KH, D], F32R), sb("w2_lo", [P, KH, D], F32R)
        self.w1_loaded, self.w2_loaded = sem("w1_loaded"), sem("w2_loaded")
        self.w1_hi_done, self.w1_split = sem("w1_hi_done"), sem("w1_split")
        self.w2_hi_done, self.w2_split = sem("w2_hi_done"), sem("w2_split")

    def w1_high(self, act, n):
        act.wait_ge(self.w1_loaded, 16 * n + 16)
        act.activation(self.w1_hi[:, :, :], self.w1_in[:, :, :], ACT.Copy).then_inc(self.w1_hi_done, 1)

    def w2_high(self, act, n):
        act.wait_ge(self.w2_loaded, 16 * n + 16)
        act.activation(self.w2_hi[:, :, :], self.w2_in[:, :, :], ACT.Copy).then_inc(self.w2_hi_done, 1)

    def w1_low(self, dve, n):
        dve.wait_ge(self.w1_hi_done, n + 1)
        dve.tensor_tensor(self.w1_lo[:, :, :], self.w1_in[:, :, :], self.w1_hi[:, :, :].bitcast(F32),
                          ALU.subtract).then_inc(self.w1_split, 1)

    def w2_low(self, dve, n):
        dve.wait_ge(self.w2_hi_done, n + 1)
        dve.tensor_tensor(self.w2_lo[:, :, :], self.w2_in[:, :, :], self.w2_hi[:, :, :].bitcast(F32),
                          ALU.subtract).then_inc(self.w2_split, 1)


def ffn(nc, k, dram, w, name):
    with ExitStack() as ctx:
        def sem(n):
            return nc.alloc_semaphore(f"{name}_{n}")

        def sb(n, shape, dt=F32):
            return ctx.enter_context(nc.sbuf_tensor(f"{name}_{n}", shape, dt))

        h32 = sb("h32", [P, KH, GN])
        h_hi = sb("h_hi", [P, KH, GN], F32R)
        with ExitStack() as early:
            early_bufs = [early.enter_context(nc.sbuf_tensor(f"{name}_early{n}", [P, width], F32))
                          for n, width in enumerate((GT * D, GT * D, GT * ROW, GT * D, E * TILES * E))]
        jobT_hi, jobT_lo = sb("jobT_hi", [P, KD, SLOTS], F32R), sb("jobT_lo", [P, KD, SLOTS], F32R)
        rows_in, rows_out = sb("rows_in", [P, GT, ROW]), sb("rows_out", [P, GT, D])
        h_lo = sb("h_lo", [P, KH, GN], F32R)
        b2_in = sb("b2_in", [P, D])
        out_rows = sb("out_rows", [P, JOBS, GT])
        out_ids = sb("out_ids", [P, GT], mybir.dt.uint32)
        HB = 4
        hid_ps = ctx.enter_context(nc.psum_tensor(f"{name}_hid_ps", [P, HB, GN], F32))
        turn_ps = ctx.enter_context(nc.psum_tensor(f"{name}_turn_ps", [P, KD, SLOTS], F32))
        def area(buf, at, *shape):
            n = int(np.prod(shape))
            flat = buf[:, at:at + n]
            if len(shape) == 1:
                return flat
            names = ["a", "b", "c"][:len(shape)]
            return flat.rearrange(f"p ({' '.join(names)}) -> p {' '.join(names)}", **dict(zip(names, shape)))

        xn = [area(b, 0, GT, D) for b in early_bufs[0:2]]
        xT32 = [area(b, 0, KD, GN) for b in early_bufs[2:4]]
        TE = TILES * E
        logits, chosen, best, next_best = (area(early_bufs[0], n * TE, TILES, E) for n in range(4))
        probs, rank, slot = (area(early_bufs[1], n * TE, TILES, E) for n in range(3))
        tiles_sum, picked = area(early_bufs[3], 0, 2, TE), area(early_bufs[3], 2 * TE, 2, TE)
        tiles_sum, picked = (b.rearrange("p a (t e) -> p a t e", e=E) for b in (tiles_sum, picked))
        owned_b1 = area(early_bufs[2], 0, JOBS, KH * E).rearrange("p j (c e) -> p j c e", e=E)
        beats = early_bufs[4][:, :].rearrange("p (j t e) -> p j t e", j=E, e=E)
        stats = sb("stats", [P, 2, GT, 6])
        mean_var = sb("mean_var", [P, 2, GT, 2])
        var_eps = sb("var_eps", [P, 2, GT])
        rstd = sb("rstd", [P, 2, GT])
        fills = sb("fills", [P, E, T // SLOTS])
        jobs = sb("jobs", [P, E])
        behind = sb("behind", [P, E, E])
        start = sb("start", [P, E])
        end = sb("end", [P, E])
        passed_by = sb("passed_by", [P, JOBS, E])
        owner = sb("owner", [P, JOBS])
        owned = sb("owned", [P, JOBS, E])
        slot_f = sb("slot_f", [P, TOP, TILES])
        top = sb("top", [P, TILES])
        total = sb("total", [P, TILES])
        out_ps = ctx.enter_context(nc.psum_tensor(f"{name}_out_ps", [P, GT // 2, 512], F32))

        scattered, rows_loaded, turned = sem("scattered"), sem("rows_loaded"), sem("turned")
        jobT_hi_done, job_split = sem("jobT_hi_done"), sem("job_split")
        hid_done, gelu_done, h_hi_done, h_split = sem("hid_done"), sem("gelu_done"), sem("h_hi_done"), sem("h_split")
        chunk_used, out_done, out_taken = sem("chunk_used"), sem("out_done"), sem("out_taken")
        rows_stored, b2_loaded, ids_done, rows_noted, based = (sem("rows_stored"), sem("b2_loaded"), sem("ids_done"),
                                                               sem("rows_noted"), sem("based"))
        first_half_in, first_rest_in, renamed = sem("first_half_in"), sem("first_rest_in"), sem("renamed")
        logit_ps = turn_ps[:, 0, 0:TE]
        count_ps = turn_ps[:, 1, 0:2 * TE].rearrange("p (n t e) -> p n t e", n=2, e=E)

        stats_done, agg_done, rstd_done, eps_done = sem("stats_done"), sem("agg_done"), sem("rstd_done"), sem("eps_done")
        xn_done, x_turned, copied, kept = sem("xn_done"), sem("x_turned"), sem("copied"), sem("kept")
        hi_done, lo_done, logits_done = sem("hi_done"), sem("lo_done"), sem("logits_done")
        chain, exp_in, exp_out, diag_zero = sem("chain"), sem("exp_in"), sem("exp_out"), sem("diag_zero")
        chosen_done, counted, slots_ready, tables_ready = (sem("chosen_done"), sem("counted"), sem("slots_ready"),
                                                           sem("tables_ready"))
        block = ctx.enter_context(nc.Block())
        w1_dram = dram["rw1"].rearrange("e (k p) h -> e p k h", p=P)
        w2_dram = dram["rw2"].rearrange("e (k p) d -> e p k d", p=P)
        x_dram = dram["slot_x"].rearrange("(j p t) d -> j p t d", t=GT, p=P)
        @block.gpsimd
        def _(pool):
            pool.memset(beats[:, :, :, :], 0.0).then_inc(diag_zero, 1)

            def rsqrt(g, p):
                wait_apart(pool, k, agg_done, g + 1)
                pool.tensor_scalar(var_eps[:, p, :], mean_var[:, p, :, 1], EPS, None, ALU.add).then_inc(eps_done, 1)
                pool.wait_ge(eps_done, g + 1)
                pool.tensor_tensor(rstd[:, p, :], var_eps[:, p, :], k.neg_half[:, 0:GT], ALU.pow).then_inc(rstd_done, 1)

            with pool.Fori(0, G // 2) as j:
                rsqrt(2 * j, 0)
                rsqrt(2 * j + 1, 1)
            w.w1_low(pool, 0)
            w.w2_low(pool, 0)

            pool.wait_ge(slots_ready, 1)
            pool.wait_ge(k.slots_zeroed, 16 * JOBS * k.ffns)

            def scatter(a, tiles, sem):
                for t in tiles:
                    pool.indirect_dma_start(dram["slot_x"], bass.IndirectOffsetOnAxis(ap=k.slot_ids[:, a, t:t + 1], axis=0),
                                            k.xn[:, t, :], None).then_inc(sem, 16)

            halves = (range(TILES // 2), range(TILES // 2, TILES))
            sems = (first_half_in, first_rest_in)
            for tiles, sem in zip(halves, sems):
                scatter(0, tiles, sem)
            for n, (tiles, sem) in enumerate(zip(halves, sems)):
                pool.wait_ge(sem, 16 * len(tiles))
                pool.tensor_copy(k.xn[:, tiles[0]:tiles[-1] + 1, D], k.pair_rows[:, 1, tiles[0]:tiles[-1] + 1]).then_inc(renamed, 1)
                pool.wait_ge(renamed, n + 1)
                scatter(1, tiles, scattered)

            def store(j):
                pool.wait_ge(ids_done, j + 1)
                for t in range(GT):
                    wait_apart(pool, k, out_taken, GT * (G + j) + 2 * (t // 2) + 2)
                    pool.indirect_dma_start(dram["slot_y"], bass.IndirectOffsetOnAxis(ap=out_ids[:, t:t + 1], axis=0),
                                            rows_out[:, t, :], None).then_inc(rows_stored, 16)

            with pool.Fori(0, JOBS) as j:
                store(j)
            pool.wait_ge(rows_stored, 16 * GT * JOBS)

        @block.sync
        def _(sp):
            sp.dma_start(w.w1_in[:, :, :], dram["sw1"].rearrange("(k p) h -> p k h", p=P)).then_inc(w.w1_loaded, 16)
            sp.dma_start(w.w2_in[:, :, :], dram["sw2"].rearrange("(k p) d -> p k d", p=P)).then_inc(w.w2_loaded, 16)
            if k.ffns == 1:
                zero_slots(sp, k, dram)

            def one(ap, i):
                return ap[bass.ds(i, 1)].rearrange("o p a b -> p (o a) b")

            def load_w1(j, e):
                sp.wait_ge(w.w1_split, j + 1)
                sp.dma_start(w.w1_in[:, :, :], one(w1_dram, e)).then_inc(w.w1_loaded, 16)

            def load_w2(j, e):
                sp.wait_ge(w.w2_split, j + 1)
                sp.dma_start(w.w2_in[:, :, :], one(w2_dram, e)).then_inc(w.w2_loaded, 16)

            def load_b2(j, e, reuse):
                if reuse:
                    sp.wait_ge(out_taken, GT * (G + j))
                sp.dma_start(b2_in[:, :], dram["rb2"][bass.ds(e, 1)].to_broadcast([P, D])).then_inc(b2_loaded, 16)

            def expert_of(j):
                return sp.value_load(k.job_expert[0:1, bass.ds(j, 1)], min_val=0, max_val=E - 1)

            sp.wait_ge(tables_ready, 1)
            load_w1(0, expert_of(0))
            load_w1(1, expert_of(1))
            e = expert_of(0)
            load_w2(0, e)
            load_b2(0, e, False)
            with sp.Fori(1, JOBS - 1) as j:
                load_w1(j + 1, expert_of(j + 1))
                e = expert_of(j)
                load_w2(j, e)
                load_b2(j, e, True)
            e = expert_of(JOBS - 1)
            load_w2(JOBS - 1, e)
            load_b2(JOBS - 1, e, True)

        @block.scalar
        def _(act):
            def copy(g, p, reuse):
                act.wait_ge(x_turned, g + 1)
                if reuse:
                    act.wait_ge(logits_done, g - 1)
                    act.wait_ge(lo_done, g - 1)
                for kd in range(KD):
                    last = act.activation(xT32[p][:, kd, :], hid_ps[:, 2 * p + kd, :], ACT.Copy)
                last.then_inc(copied, 1)
                act.wait_ge(copied, g + 1)
                act.activation(k.xT_hi[:, :, bass.ds(g * GN, GN)], xT32[p][:, :, :], ACT.Copy).then_inc(hi_done, 1)
                act.activation(k.xn[:, bass.ds(GT * g, GT), 0:D], xn[p][:, :, :], ACT.Copy).then_inc(kept, 1)

            copy(0, 0, False)
            copy(1, 1, False)
            w.w1_high(act, 0)
            w.w2_high(act, 0)
            with act.Fori(1, G // 2 - 1) as j:
                copy(2 * j, 0, True)
                copy(2 * j + 1, 1, True)
            copy(G - 2, 0, True)
            copy(G - 1, 1, True)
            act.wait_ge(exp_in, 1)
            act.activation(probs[:, :, :], probs[:, :, :], ACT.Exp).then_inc(exp_out, 1)

            def w1_high(n, i):
                act.wait_ge(hid_done, KH * i)
                w.w1_high(act, n)

            def w2_high(n, i):
                act.wait_ge(out_done, GT * i)
                w.w2_high(act, n)

            def hidden(bias, i, reuse):
                for c in range(KH):
                    if reuse:
                        act.wait_ge(h_split, KH * (i - 1) + c + 1)
                    wait_apart(act, k, hid_done, KH * i + c + 1)
                    act.activation(h32[:, c, :], hid_ps[:, c % HB, :], ACT.Gelu, bias=bias(c)).then_inc(gelu_done, 1)

            def high(i, reuse):
                for c in range(KH):
                    act.wait_ge(gelu_done, KH * i + c + 1)
                    if reuse and c < KH - 1:
                        act.wait_ge(chunk_used, (KH - 1) * (i - 1) + c + 1)
                    elif reuse:
                        act.wait_ge(out_done, GT * i)
                    act.activation(h_hi[:, c, :], h32[:, c, :], ACT.Copy).then_inc(h_hi_done, 1)

            def job_high(j, i):
                act.wait_ge(turned, j + 1)
                act.wait_ge(hid_done, KH * i)
                for kd in range(KD):
                    last = act.activation(jobT_hi[:, kd, :], turn_ps[:, kd, :], ACT.Copy)
                last.then_inc(jobT_hi_done, 1)

            def bias_of(j):
                return lambda c: k.job_b1[:, bass.ds(j, 1), c]

            def load_rows(j, reuse):
                if reuse:
                    act.wait_ge(turned, j)
                    act.wait_ge(rows_noted, j)
                act.dma_start(rows_in[:, :, :], x_dram[bass.ds(j, 1)].rearrange("o p t d -> p (o t) d")
                              ).then_inc(rows_loaded, 16)

            def shared_bias(c):
                return k.b1[:, 0, c:c + 1]

            def job(j, prefetch):
                hidden(bias_of(j), G + j, True)
                if prefetch:
                    job_high(j + 1, G + j + 1)
                    if prefetch > 1:
                        load_rows(j + 2, True)
                    w1_high(j + 2, G + j + 1)
                high(G + j, True)
                w2_high(j + 1, G + j)

            hidden(shared_bias, 0, False)
            high(0, False)
            with act.Fori(1, G) as g:
                hidden(shared_bias, g, True)
                high(g, True)
            act.wait_ge(scattered, 16 * TILES)
            act.wait_ge(tables_ready, 1)
            load_rows(0, False)
            job_high(0, G)
            load_rows(1, True)
            w1_high(1, G)
            with act.Fori(0, JOBS - 2) as j:
                job(j, 2)
            job(JOBS - 2, 1)
            job(JOBS - 1, 0)

        @block.vector
        def _(dve):
            def statistics(g, p):
                for t in range(GT):
                    last = dve.bn_stats(stats[:, p, t, :], k.x[:, GT * g + t, :])
                last.then_inc(stats_done, 1)

            def aggregate(g, p):
                wait_apart(dve, k, stats_done, g + 1)
                for t in range(GT):
                    last = dve.bn_aggr(mean_var[:, p, t, :], stats[:, p, t, :])
                last.then_inc(agg_done, 1)

            def scale(g, p, reuse):
                if reuse:
                    dve.wait_ge(x_turned, g - 1)
                    dve.wait_ge(kept, g - 1)
                dve.wait_ge(rstd_done, g + 1)
                for t in range(GT):
                    last = dve.tensor_scalar(xn[p][:, t, :], k.x[:, GT * g + t, :], mean_var[:, p, t, 0:1],
                                             rstd[:, p, t:t + 1], ALU.subtract, ALU.mult)
                last.then_inc(xn_done, 1)

            def x_low(g, p):
                dve.wait_ge(hi_done, g + 1)
                at = bass.ds(g * GN, GN)
                dve.tensor_tensor(k.xT_lo[:, :, at], xT32[p][:, :, :], k.xT_hi[:, :, at].bitcast(F32),
                                  ALU.subtract).then_inc(lo_done, 1)

            def step(g, p, reuse):
                scale(g, p, reuse)
                aggregate(g + 1, 1 - p)
                statistics(g + 2, p)

            def low(i):
                for c in range(KH):
                    dve.wait_ge(h_hi_done, KH * i + c + 1)
                    dve.tensor_tensor(h_lo[:, c, :], h32[:, c, :], h_hi[:, c, :].bitcast(F32),
                                      ALU.subtract).then_inc(h_split, 1)

            def job_low(j):
                dve.wait_ge(jobT_hi_done, j + 1)
                dve.tensor_tensor(jobT_lo[:, :, :], turn_ps[:, :, :], jobT_hi[:, :, :].bitcast(F32),
                                  ALU.subtract).then_inc(job_split, 1)

            def base(g):
                xg = k.x[:, bass.ds(GT * g, GT), :]
                dve.tensor_tensor(xg, xg, k.half_sb2[:, :].unsqueeze(1).to_broadcast([P, GT, D]), ALU.add).then_inc(based, 1)

            def add(g):
                dve.wait_ge(based, g + 1)
                for a in range(GT // 2):
                    dve.wait_ge(out_done, GT * g + 2 * a + 2)
                    xt = k.x[:, bass.ds(GT * g + 2 * a, 2), :]
                    dve.scalar_tensor_tensor(out=xt, in0=out_ps[:, a, :].rearrange("p (t d) -> p t d", t=2), scalar=0.5,
                                             in1=xt, op0=ALU.mult, op1=ALU.add).then_inc(out_taken, 2)

            def take(j, reuse):
                dve.wait_ge(b2_loaded, 16 * j + 16)
                if reuse:
                    dve.wait_ge(rows_stored, 16 * GT * j)
                dve.tensor_copy(out_ids[:, :], out_rows[:, bass.ds(j, 1), :].rearrange("p o t -> p (o t)")).then_inc(ids_done, 1)
                for a in range(GT // 2):
                    dve.wait_ge(out_done, GT * (G + j) + 2 * a + 2)
                    dve.tensor_tensor(rows_out[:, 2 * a:2 * a + 2, :], out_ps[:, a, :].rearrange("p (t d) -> p t d", t=2),
                                      b2_in[:, :].unsqueeze(1).to_broadcast([P, 2, D]), ALU.add).then_inc(out_taken, 2)

            def note(j):
                dve.wait_ge(rows_loaded, 16 * j + 16)
                dve.tensor_copy(out_rows[:, bass.ds(j, 1), :].rearrange("p o t -> p (o t)"), rows_in[:, :, D]).then_inc(rows_noted, 1)

            if k.ffns == 1:
                dve.wait_ge(k.x_in[0], 16)
            statistics(0, 0)
            statistics(1, 1)
            aggregate(0, 0)
            if k.ffns == 1:
                dve.wait_ge(k.x_in[1], 16)
            step(0, 0, False)
            step(1, 1, False)
            x_low(0, 0)
            if k.ffns == 1:
                dve.wait_ge(k.x_in[2], 16)
                dve.wait_ge(k.x_in[3], 16)
            with dve.Fori(1, G // 2 - 1) as j:
                step(2 * j, 0, True)
                x_low(2 * j - 1, 1)
                step(2 * j + 1, 1, True)
                x_low(2 * j, 0)
            scale(G - 2, 0, True)
            aggregate(G - 1, 1)
            x_low(G - 3, 1)
            scale(G - 1, 1, True)
            x_low(G - 2, 0)
            x_low(G - 1, 1)

            links = [0]

            def link(ins):
                links[0] += 1
                ins.then_inc(chain, 1)
                dve.wait_ge(chain, links[0])

            dve.wait_ge(logits_done, G)
            dve.wait_ge(kept, G)
            link(dve.tensor_tensor(logits[:, :, :], logit_ps.rearrange("p (t e) -> p t e", e=E),
                                   k.router_b[:, :].unsqueeze(1).to_broadcast([P, TILES, E]), ALU.add))
            link(dve.tensor_reduce(top[:, :], logits[:, :, :], AX_X, ALU.max))
            dve.tensor_tensor(probs[:, :, :], logits[:, :, :], top[:, :].unsqueeze(2).to_broadcast([P, TILES, E]),
                              ALU.subtract).then_inc(exp_in, 1)
            dve.wait_ge(diag_zero, 1)
            for j in range(E):
                rival = logits[:, :, j:j + 1]
                if j:
                    last = dve.tensor_tensor(beats[:, j, :, 0:j], rival.to_broadcast([P, TILES, j]),
                                             logits[:, :, 0:j], ALU.is_gt)
                if j < E - 1:
                    last = dve.tensor_tensor(beats[:, j, :, j + 1:E], rival.to_broadcast([P, TILES, E - 1 - j]),
                                             logits[:, :, j + 1:E], ALU.is_ge)
            link(last)
            link(dve.tensor_reduce(rank[:, :, :], beats[:, :, :, :].rearrange("p j t e -> p t e j"), AX_X, ALU.add))
            dve.tensor_scalar(chosen[:, :, :], rank[:, :, :], float(TOP), None, ALU.is_lt).then_inc(chosen_done, 1)
            dve.tensor_scalar(best[:, :, :], rank[:, :, :], 0.0, None, ALU.is_equal)
            link(dve.tensor_scalar(next_best[:, :, :], rank[:, :, :], 1.0, None, ALU.is_equal))
            dve.wait_ge(counted, 1)
            per_tile = count_ps[:, 1, :, :]
            link(dve.tensor_copy(tiles_sum[:, 0, :, :], per_tile))
            a, step = 0, 1
            while step < TILES:
                dve.tensor_copy(tiles_sum[:, 1 - a, 0:step, :], tiles_sum[:, a, 0:step, :])
                link(dve.tensor_tensor(tiles_sum[:, 1 - a, step:, :], tiles_sum[:, a, step:, :],
                                       tiles_sum[:, a, 0:TILES - step, :], ALU.add))
                a, step = 1 - a, 2 * step
            link(dve.tensor_tensor(fills[:, :, :], tiles_sum[:, a, TILES - 1, :].unsqueeze(2).to_broadcast([P, E, T // SLOTS]),
                                   k.job_starts[:, :].unsqueeze(1).to_broadcast([P, E, T // SLOTS]), ALU.is_gt))
            link(dve.tensor_reduce(jobs[:, :], fills[:, :, :], AX_X, ALU.add))
            link(dve.tensor_tensor(behind[:, :, :], jobs[:, :].unsqueeze(1).to_broadcast([P, E, E]), k.lower[:, :, :], ALU.mult))
            link(dve.tensor_reduce(start[:, :], behind[:, :, :], AX_X, ALU.add))
            dve.tensor_tensor(end[:, :], start[:, :], jobs[:, :], ALU.add)
            dve.tensor_tensor(slot[:, :, :], tiles_sum[:, a, :, :], per_tile, ALU.subtract)
            link(dve.tensor_scalar(start[:, :], start[:, :], float(SLOTS), None, ALU.mult))
            link(dve.tensor_tensor(slot[:, :, :], slot[:, :, :], count_ps[:, 0, :, :], ALU.add))
            link(dve.tensor_tensor(slot[:, :, :], slot[:, :, :], start[:, :].unsqueeze(1).to_broadcast([P, TILES, E]), ALU.add))
            dve.tensor_tensor(picked[:, 0, :, :], slot[:, :, :], best[:, :, :], ALU.mult)
            link(dve.tensor_tensor(picked[:, 1, :, :], slot[:, :, :], next_best[:, :, :], ALU.mult))
            link(dve.tensor_reduce(slot_f[:, :, :], picked[:, :, :, :], AX_X, ALU.add))
            dve.tensor_copy(k.xn[:, :, D], k.pair_rows[:, 0, :])
            dve.tensor_copy(k.slot_ids[:, :, :], slot_f[:, :, :]).then_inc(slots_ready, 1)
            base(0)
            low(0)
            dve.wait_ge(exp_out, 1)
            link(dve.tensor_reduce(total[:, :], probs[:, :, :], AX_X, ALU.add))
            link(dve.reciprocal(total[:, :], total[:, :]))
            link(dve.tensor_tensor(probs[:, :, :], probs[:, :, :], total[:, :].unsqueeze(2).to_broadcast([P, TILES, E]),
                                   ALU.mult))
            dve.wait_ge(chosen_done, 1)
            link(dve.scalar_tensor_tensor(out=k.gate[:, :, 1:NX], in0=probs[:, :, :], scalar=0.5, in1=chosen[:, :, :],
                                          op0=ALU.mult, op1=ALU.mult))
            link(dve.memset(k.gate[:, :, 0:1], 0.5))

            dve.tensor_tensor(picked[:, 0, :, :], k.gate[:, :, 1:NX], best[:, :, :], ALU.mult)
            link(dve.tensor_tensor(picked[:, 1, :, :], k.gate[:, :, 1:NX], next_best[:, :, :], ALU.mult))
            link(dve.tensor_reduce(k.pair_gate[:, :, :], picked[:, :, :, :], AX_X, ALU.add))
            link(dve.tensor_tensor(passed_by[:, :, :], k.job_numbers[:, :].unsqueeze(2).to_broadcast([P, JOBS, E]),
                                   end[:, :].unsqueeze(1).to_broadcast([P, JOBS, E]), ALU.is_ge))
            link(dve.tensor_reduce(owner[:, :], passed_by[:, :, :], AX_X, ALU.add))
            link(dve.tensor_scalar(owner[:, :], owner[:, :], float(E - 1), None, ALU.min))
            link(dve.tensor_copy(k.job_expert[:, :], owner[:, :]))

            link(dve.tensor_tensor(owned[:, :, :], owner[:, :].unsqueeze(2).to_broadcast([P, JOBS, E]),
                                   k.expert_numbers[:, :].unsqueeze(1).to_broadcast([P, JOBS, E]), ALU.is_equal))
            link(dve.tensor_tensor(owned_b1[:, :, :, :], owned[:, :, :].unsqueeze(2).to_broadcast([P, JOBS, KH, E]),
                                   k.b1[:, 1:NX, :].rearrange("p e c -> p c e").unsqueeze(1).to_broadcast([P, JOBS, KH, E]),
                                   ALU.mult))
            dve.tensor_reduce(k.job_b1[:, :, :], owned_b1[:, :, :, :], AX_X, ALU.add).then_inc(tables_ready, 1)
            with dve.Fori(1, G) as g:
                base(g)
                low(g)
                add(g - 1)
            note(0)
            job_low(0)
            w.w1_low(dve, 1)

            def job(j):
                note(j + 1)
                job_low(j + 1)
                w.w1_low(dve, j + 2)
                low(G + j)

            job(0)
            add(G - 1)
            w.w2_low(dve, 1)
            job(1)
            take(0, False)
            w.w2_low(dve, 2)
            with dve.Fori(2, JOBS - 1) as j:
                job(j)
                take(j - 1, True)
                w.w2_low(dve, j + 1)
            low(G + JOBS - 1)
            take(JOBS - 2, True)
            w.w2_low(dve, JOBS)
            take(JOBS - 1, True)

        @block.tensor
        def _(pe):
            def turn_x(g, p, reuse):
                pe.wait_ge(xn_done, g + 1)
                if reuse:
                    pe.wait_ge(copied, g - 1)
                for kd in range(KD):
                    for t in range(GT):
                        last = pe.transpose(hid_ps[:, 2 * p + kd, t * P:(t + 1) * P], xn[p][:, t, kd * P:(kd + 1) * P],
                                            k.ident[:, :])
                last.then_inc(x_turned, 1)

            def route(g, p):
                pe.wait_ge(copied, g + 1)
                for t in range(GT):
                    for kd in range(KD):
                        last = pe.matmul(turn_ps[:, 0, bass.ds((GT * g + t) * E, E)], xT32[p][:, kd, t * P:(t + 1) * P],
                                         k.router_w[:, kd, :], start=(kd == 0), stop=(kd == KD - 1))
                last.then_inc(logits_done, 1)

            turn_x(0, 0, False)
            turn_x(1, 1, False)
            route(0, 0)
            route(1, 1)
            with pe.Fori(1, G // 2) as j:
                turn_x(2 * j, 0, True)
                turn_x(2 * j + 1, 1, True)
                route(2 * j, 0)
                route(2 * j + 1, 1)

            def first(xs, i, start):
                for c in range(KH):
                    if not start:
                        pe.wait_ge(gelu_done, KH * i + c + 1 - HB)
                    passes = [(w1, xs(n, kd), kd) for kd in range(KD) for w1, n in ((w.w1_hi, 0), (w.w1_hi, 1), (w.w1_lo, 0))]
                    for n, (w1, x, kd) in enumerate(passes):
                        last = pe.matmul(hid_ps[:, c % HB, :], w1[:, kd, c * P:(c + 1) * P], x,
                                         start=(n == 0), stop=(n == len(passes) - 1))
                    last.then_inc(hid_done, 1)

            def second(i, reuse):
                for c in range(KH):
                    pe.wait_ge(h_split, KH * i + c + 1)
                    for t in range(GT):
                        if reuse and c == 0:
                            pe.wait_ge(out_taken, GT * (i - 1) + t + 1)
                        for n, (h, w2) in enumerate(((h_hi, w.w2_hi), (h_hi, w.w2_lo), (h_lo, w.w2_hi))):
                            last = pe.matmul(out_ps[:, t // 2, (t % 2) * D:(t % 2 + 1) * D], h[:, c, t * P:(t + 1) * P], w2[:, c, :],
                                             start=(c == 0 and n == 0 and t % 2 == 0), stop=(c == KH - 1 and n == 2), skip_group_check=True)
                        if c == KH - 1:
                            last.then_inc(out_done, 1)
                    if c < KH - 1:
                        last.then_inc(chunk_used, 1)

            def group(g):
                return lambda n, kd: (k.xT_hi, k.xT_lo)[n][:, kd, bass.ds(g * GN, GN)]

            def job_rows(n, kd):
                return (jobT_hi, jobT_lo)[n][:, kd, :]

            def turn(j, reuse):
                pe.wait_ge(rows_loaded, 16 * j + 16)
                if reuse:
                    pe.wait_ge(job_split, j)
                for kd in range(KD):
                    for t in range(GT):
                        last = pe.transpose(turn_ps[:, kd, t * P:(t + 1) * P], rows_in[:, t, kd * P:(kd + 1) * P], k.ident[:, :])
                last.then_inc(turned, 1)

            def job_first(j):
                pe.wait_ge(w.w1_split, j + 2)
                pe.wait_ge(job_split, j + 1)
                first(job_rows, G + j, False)

            pe.wait_ge(w.w1_split, 1)
            pe.wait_ge(lo_done, G)
            first(group(0), 0, True)
            pe.wait_ge(chosen_done, 1)
            for n, tri in enumerate((k.earlier, k.ones)):
                last = pe.matmul(turn_ps[:, 1, n * TILES * E:(n + 1) * TILES * E], tri[:, :],
                                 chosen[:, :, :].rearrange("p t e -> p (t e)"), start=True, stop=True)
            last.then_inc(counted, 1)

            pe.wait_ge(w.w2_split, 1)
            first(group(1), 1, False)
            second(0, False)
            with pe.Fori(2, G) as g:
                first(group(g), g, False)
                second(g - 1, True)
            turn(0, False)
            job_first(0)
            turn(1, True)
            second(G - 1, True)
            with pe.Fori(1, JOBS - 1) as j:
                job_first(j)
                turn(j + 1, True)
                pe.wait_ge(w.w2_split, j + 1)
                second(G + j - 1, True)
            job_first(JOBS - 1)
            pe.wait_ge(w.w2_split, JOBS)
            second(G + JOBS - 2, True)
            pe.wait_ge(w.w2_split, JOBS + 1)
            second(G + JOBS - 1, True)


def combine(nc, k, dram, name, stores):
    R = 4
    with ExitStack() as ctx:
        got = ctx.enter_context(nc.sbuf_tensor(f"{name}_got", [P, R, GT, TOP, D], F32))
        got_in = [nc.alloc_semaphore(f"{name}_got_in{r}") for r in range(R)]
        added = nc.alloc_semaphore(f"{name}_added")
        half_added = nc.alloc_semaphore(f"{name}_half_added")
        stored = nc.alloc_semaphore(f"{name}_stored")
        block = ctx.enter_context(nc.Block())
        y_rows = dram["slot_y"][0:TOP * T].rearrange("(g t p a) d -> g p t a d", t=GT, p=P, a=TOP)
        out_rows = dram["out"].rearrange("b n d -> (b n) d").rearrange("(g t p) d -> g p t d", t=GT, p=P)

        @block.sync
        def _(sp):
            def load(g, r, reuse):
                if reuse:
                    sp.wait_ge(added, GT * (g - R + 1))
                sp.dma_start(got[:, r, :, :, :], y_rows[bass.ds(g, 1)].rearrange("o p t a d -> p (o t) a d")
                             ).then_inc(got_in[r], 16)

            for r in range(R):
                load(r, r, False)
            with sp.Fori(1, G // R) as q:
                for r in range(R):
                    load(R * q + r, r, True)

        @block.scalar
        def _(act):
            if not stores:
                return
            with act.Fori(0, G) as g:
                act.wait_ge(added, GT * (g + 1))
                act.dma_start(out_rows[bass.ds(g, 1)].rearrange("o p t d -> p (o t) d"), k.x[:, bass.ds(GT * g, GT), :]
                              ).then_inc(stored, 16)
            act.wait_ge(stored, 16 * G)

        @block.vector
        def _(dve):
            with dve.Fori(0, G // R) as q:
                for r in range(R):
                    g = R * q + r
                    dve.wait_ge(got_in[r], 16 * (q + 1))
                    for a, done in ((0, half_added), (1, added)):
                        for t in range(GT):
                            if a:
                                dve.wait_ge(half_added, GT * g + t + 1)
                            xt = k.x[:, GT * g + t, :]
                            dve.scalar_tensor_tensor(out=xt, in0=got[:, r, t, a, :],
                                                     scalar=k.pair_gate[:, a, bass.ds(GT * g + t, 1)],
                                                     in1=xt, op0=ALU.mult, op1=ALU.add).then_inc(done, 1)


def attention(nc, k, dram):
    with ExitStack() as ctx:
        def sem(n):
            return ctx.enter_context(nc.semaphore(f"attn_{n}"))

        def sb(n, shape, dt=F32):
            return ctx.enter_context(nc.sbuf_tensor(f"attn_{n}", shape, dt))

        def bank(n):
            return ctx.enter_context(nc.psum_tensor(f"attn_{n}_ps", [P, 512], F32))

        w_in = sb("w_in", [P, KD, WALL])
        w_hi, w_lo = sb("w_hi", [P, KD, WALL], F32R), sb("w_lo", [P, KD, WALL], F32R)
        wo_in, wo_scaled = sb("wo_in", [P, NH, D]), sb("wo_scaled", [P, NH, D])
        wo_hi, wo_lo = sb("wo_hi", [P, NH, D], F32R), sb("wo_lo", [P, NH, D], F32R)
        gnorm = sb("gnorm", [P, 1])
        wgk = sb("wgk", [P, KD, NH])
        bgk = sb("bgk", [P, NH])
        upto = sb("upto", [P, P])
        causal = sb("causal", [P, P])
        expert_out = sb("expert_out", [P, GT, TOP, D])
        stats = sb("stats", [P, GT, 6])
        mean_var = sb("mean_var", [P, GT, 2])
        var_eps = sb("var_eps", [P, GT])
        rstd = sb("rstd", [P, GT])
        xn = sb("xn", [P, GT, D])
        xT32 = sb("xT32", [P, KD, GN])
        xT_hi, xT_lo = sb("xT_hi", [P, KD, GN], F32R), sb("xT_lo", [P, KD, GN], F32R)
        z = sb("z", [P, GT, NH])
        z_min = sb("z_min", [P, GT, NH])
        z_abs = sb("z_abs", [P, GT, NH])
        z_exp = sb("z_exp", [P, GT, NH])
        z_log = sb("z_log", [P, GT, NH])
        decay = sb("decay", [P, GT, NH])
        kT = sb("kT", [P, 2, GN])
        q_pad = sb("q_pad", [P, 2, 2, GN])
        steps_hi, steps_lo = sb("steps_hi", [P, 2, NH, P], F32R), sb("steps_lo", [P, 2, NH, P], F32R)
        decay_hi, decay_lo = sb("decay_hi", [P, GT, NH], F32R), sb("decay_lo", [P, GT, NH])
        ones_hi = sb("ones_hi", [P, P], F32R)
        cum = sb("cum", [P, NH, P])
        cum_exp = sb("cum_exp", [P, 2, NH, P])
        cum_col = sb("cum_col", [P, NH])
        gap = sb("gap", [P, NH, P])
        gap_exp = sb("gap_exp", [P, NH, P])
        k_gap = sb("k_gap", [P, NH])
        k_fac = sb("k_fac", [P, NH])
        q_dec = sb("q_dec", [P, 2, 2, P])
        k_dec = sb("k_dec", [P, 2, NH, DK])
        v32 = sb("v32", [P, 2, NH * DV])
        score = sb("score", [P, 2, NH, P])
        tanh_g = sb("tanh_g", [P, NH * DV])
        gate = sb("gate", [P, 2, NH * DV])
        state = sb("state", [P, 2, 2, DV])
        o32 = sb("o32", [P, NH * DV])
        o_sq = sb("o_sq", [P, NH, DV])
        o_sum = sb("o_sum", [P, NH])
        o_mean = sb("o_mean", [P, NH])
        o_rstd = sb("o_rstd", [P, NH])
        o_gated = sb("o_gated", [P, NH * DV])
        oT_hi, oT_lo = sb("oT_hi", [P, NH * P], F32R), sb("oT_lo", [P, NH * P], F32R)
        cum_ps, score_ps, v_ps, g_ps = bank("cum"), bank("score"), bank("v"), bank("g")
        o_ps, s_ps, y_ps, k_ps = bank("o"), bank("s"), bank("y"), bank("k")
        COL, GK = NH * DK, NH * DK + 16

        decay_made, decay_hi_done = sem("decay_made"), sem("decay_hi_done")
        expert_out_in, first_added, both_added = sem("expert_out_in"), sem("first_added"), sem("both_added")
        w_in_in = [sem("qk_w_in"), sem("vg_w_in")]
        ones_done, wo_hi_done, wo_ready, vg_w_ready = sem("ones_done"), sem("wo_hi_done"), sem("wo_ready"), sem("vg_w_ready")
        loaded, w_hi_done, w_ready = sem("loaded"), sem("w_hi_done"), sem("w_ready")
        const_made, const_ready, wo_scaled_done = sem("const_made"), sem("const_ready"), sem("wo_scaled_done")
        stats_done, agg_done, eps_done, rstd_done = sem("stats_done"), sem("agg_done"), sem("eps_done"), sem("rstd_done")
        xn_done, turned, copied, hi_done, split_done = (sem("xn_done"), sem("turned"), sem("copied"), sem("hi_done"),
                                                        sem("split_done"))
        gk_done, z_done, z_abs_done, z_exp_done, z_log_done, z_min_done, log_sig_done, decay_done = (
            sem("gk_done"), sem("z_done"), sem("z_abs_done"), sem("z_exp_done"), sem("z_log_done"), sem("z_min_done"),
            sem("log_sig_done"), sem("decay_done"))
        qk_done, qk_copied = sem("qk_done"), sem("qk_copied")
        steps_done, k_done, score_done, cum_done, v_done, g_done = (
            sem("steps_done"), sem("k_done"), sem("score_done"), sem("cum_done"), sem("v_done"), sem("g_done"))
        cum_copied, cum_exp_done, col_copied, gap_done, gap_exp_done = (
            sem("cum_copied"), sem("cum_exp_done"), sem("col_copied"), sem("gap_done"), sem("gap_exp_done"))
        k_gap_done, k_fac_done, v_copied, tanh_done = sem("k_gap_done"), sem("k_fac_done"), sem("v_copied"), sem("tanh_done")
        q_dec_done, k_dec_done, masked, gated = sem("q_dec_done"), sem("k_dec_done"), sem("masked"), sem("gated")
        s_done, o_done, state_done = sem("s_done"), sem("o_done"), sem("state_done")
        o_copied, sq_done, sum_done, mean_done, o_rstd_done, o_gated_done = (
            sem("o_copied"), sem("sq_done"), sem("sum_done"), sem("mean_done"), sem("o_rstd_done"), sem("o_gated_done"))
        oT_done, oT_hi_done, oT_split, y_done, y_added = (
            sem("oT_done"), sem("oT_hi_done"), sem("oT_split"), sem("y_done"), sem("y_added"))
        block = ctx.enter_context(nc.Block())

        def states(b, c):
            return (GT - 1) * b + min(c + 1, GT - 1)

        def schedule(eng, slot, drain):
            for c in range(GT):
                slot(0, c, 2)
            with eng.Fori(1, B - 2) as b:
                for c in range(GT):
                    slot(b, c, 2)
            for b in (B - 2, B - 1):
                for c in range(GT):
                    slot(b, c, B - 1 - b)
            drain()

        def before(b, c, back):
            if c >= back:
                return b, c - back
            if isinstance(b, int) and b == 0:
                return None
            return b - 1, c - back + GT

        @block.sync
        def _(sp):
            y_rows = dram["slot_y"][0:TOP * T].rearrange("(g t p a) d -> g p t a d", t=GT, p=P, a=TOP)

            def load_outputs(b, reuse):
                if reuse:
                    sp.wait_ge(both_added, b)
                sp.dma_start(expert_out[:, :, :, :], y_rows[bass.ds(b, 1)].rearrange("o p t a d -> p (o t) a d")
                             ).then_inc(expert_out_in, 16)

            load_outputs(0, False)
            for n, (name, width) in enumerate((("Wq", 256), ("Wk", 256), ("Wv", 512), ("Wg", 512))):
                at = (0, 256, 512, 1024)[n]
                sp.dma_start(w_in[:, :, at:at + width], dram[name].rearrange("(k p) n -> p k n", p=P)).then_inc(w_in_in[n // 2], 16)
            sp.dma_start(wo_in[:, :, :], dram["Wo"].rearrange("(h p) d -> p h d", p=P)).then_inc(loaded, 16)
            sp.dma_start(gnorm[:, :], dram["gnorm_w"].rearrange("(p o) -> p o", o=1)).then_inc(loaded, 16)
            sp.dma_start(wgk[:, :, :], dram["Wgk"].rearrange("(k p) h -> p k h", p=P)).then_inc(loaded, 16)
            sp.dma_start(bgk[:, :], dram["bgk"].rearrange("(o h) -> o h", o=1).to_broadcast([P, NH])).then_inc(loaded, 16)
            with sp.Fori(1, B) as b:
                load_outputs(b, True)
            zero_slots(sp, k, dram)
            sp.wait_ge(loaded, 64)

        @block.gpsimd
        def _(pool):
            pool.memset(causal[:, :], 0.0).then_inc(const_made, 1)
            pool.memset(q_pad[:, :, :, :], 0.0).then_inc(const_made, 1)
            pool.memset(state[:, :, :, :], 0.0).then_inc(const_made, 1)
            pool.wait_ge(const_made, 3)
            pool.affine_select(out=upto[:, :], in_=k.ones[:, :], compare_op=ALU.is_ge, fill=0.0, base=0,
                               pattern=[[1, P]], channel_multiplier=-1).then_inc(const_ready, 1)
            pool.affine_select(out=causal[:, :], in_=causal[:, :], compare_op=ALU.is_ge, fill=NEVER, base=0,
                               pattern=[[1, P]], channel_multiplier=-1).then_inc(const_ready, 1)
            pool.wait_ge(const_ready, 2)

            def norm_rsqrt(b):
                wait_apart(pool, k, agg_done, b + 1)
                pool.tensor_scalar(var_eps[:, :], mean_var[:, :, 1], EPS, None, ALU.add).then_inc(eps_done, 1)
                pool.wait_ge(eps_done, b + 1)
                pool.tensor_tensor(rstd[:, :], var_eps[:, :], k.neg_half[:, 0:GT], ALU.pow).then_inc(rstd_done, 1)

            def spread(b, c):
                n = GT * b + c
                if c == 0:
                    pool.wait_ge(decay_done, b + 1)
                if before(b, c, 2):
                    pool.wait_ge(cum_done, n - 1)
                for steps, part in ((steps_hi, decay_hi[:, c, :].bitcast(F32)), (steps_lo, decay_lo[:, c, :])):
                    last = pool.tensor_tensor(steps[:, c % 2, :, :], upto[:, :].unsqueeze(1).to_broadcast([P, NH, P]),
                                              part.unsqueeze(2).to_broadcast([P, NH, P]), ALU.mult)
                last.then_inc(steps_done, 1)

            def out_rsqrt(b, c):
                n = GT * b + c
                wait_apart(pool, k, sum_done, n + 1)
                pool.tensor_scalar(o_mean[:, :], o_sum[:, :], 1.0 / DV, EPS, ALU.mult, ALU.add).then_inc(mean_done, 1)
                pool.wait_ge(mean_done, n + 1)
                pool.tensor_tensor(o_rstd[:, :], o_mean[:, :], k.neg_half[:, 0:NH], ALU.pow).then_inc(o_rstd_done, 1)

            def slot(b, c, more):
                if before(b, c, 2):
                    out_rsqrt(*before(b, c, 2))
                if c == 0:
                    spread(b, 0)
                if c < GT - 1:
                    spread(b, c + 1)
                if c == 1 and more:
                    norm_rsqrt(b + 1)

            def drain():
                out_rsqrt(B - 1, GT - 2)
                out_rsqrt(B - 1, GT - 1)

            pool.tensor_copy(ones_hi[:, :], k.ones[:, :]).then_inc(ones_done, 1)
            norm_rsqrt(0)
            pool.wait_ge(w_hi_done, 2)
            pool.tensor_tensor(w_lo[:, :, 512:WALL], w_in[:, :, 512:WALL], w_hi[:, :, 512:WALL].bitcast(F32), ALU.subtract
                               ).then_inc(vg_w_ready, 1)
            pool.wait_ge(wo_scaled_done, 1)
            pool.tensor_copy(wo_hi[:, :, :], wo_scaled[:, :, :]).then_inc(wo_hi_done, 1)
            pool.wait_ge(wo_hi_done, 1)
            pool.tensor_tensor(wo_lo[:, :, :], wo_scaled[:, :, :], wo_hi[:, :, :].bitcast(F32), ALU.subtract).then_inc(wo_ready, 1)
            schedule(pool, slot, drain)

        @block.vector
        def _(dve):
            def add_outputs(b, part):
                dve.wait_ge(expert_out_in, 16 * b + 16)
                pairs = [(a, t) for a in range(TOP) for t in range(GT)]
                for a, t in pairs[part]:
                    if (a, t) == (1, 0):
                        dve.wait_ge(first_added, b + 1)
                    xt = k.x[:, GT * b + t, :]
                    last = dve.scalar_tensor_tensor(out=xt, in0=expert_out[:, t, a, :], scalar=k.pair_gate[:, a, bass.ds(GT * b + t, 1)],
                                                    in1=xt, op0=ALU.mult, op1=ALU.add)
                    if (a, t) in ((0, GT - 1), (1, GT - 1)):
                        last.then_inc((first_added, both_added)[a], 1)

            def statistics(b):
                wait_apart(dve, k, both_added, b + 1)
                for t in range(GT):
                    last = dve.bn_stats(stats[:, t, :], k.x[:, GT * b + t, :])
                last.then_inc(stats_done, 1)

            def aggregate(b):
                wait_apart(dve, k, stats_done, b + 1)
                for t in range(GT):
                    last = dve.bn_aggr(mean_var[:, t, :], stats[:, t, :])
                last.then_inc(agg_done, 1)

            def scale(b, reuse):
                if reuse:
                    dve.wait_ge(turned, b)
                dve.wait_ge(rstd_done, b + 1)
                for t in range(GT):
                    last = dve.tensor_scalar(xn[:, t, :], k.x[:, GT * b + t, :], mean_var[:, t, 0:1], rstd[:, t:t + 1],
                                             ALU.subtract, ALU.mult)
                last.then_inc(xn_done, 1)

            def split(b):
                dve.wait_ge(copied, b + 1)
                if before(b, 0, 1):
                    dve.wait_ge(g_done, GT * b)
                dve.tensor_copy(xT_hi[:, :, :], xT32[:, :, :]).then_inc(hi_done, 1)
                dve.wait_ge(hi_done, b + 1)
                dve.tensor_tensor(xT_lo[:, :, :], xT32[:, :, :], xT_hi[:, :, :].bitcast(F32), ALU.subtract).then_inc(split_done, 1)

            def logit(b):
                dve.wait_ge(gk_done, b + 1)
                dve.tensor_tensor(z[:, :, :], k_ps[:, GK:GK + GT * NH].rearrange("p (t h) -> p t h", h=NH),
                                  bgk[:, :].unsqueeze(1).to_broadcast([P, GT, NH]), ALU.add).then_inc(z_done, 1)
                dve.wait_ge(z_done, b + 1)
                dve.scalar_tensor_tensor(out=z_abs[:, :, :], in0=z[:, :, :], scalar=-1.0, in1=z[:, :, :],
                                         op0=ALU.mult, op1=ALU.min).then_inc(z_abs_done, 1)
                dve.tensor_scalar(z_min[:, :, :], z[:, :, :], 0.0, None, ALU.min).then_inc(z_min_done, 1)

            def log_sigmoid(b):
                dve.wait_ge(z_log_done, b + 1)
                dve.wait_ge(z_min_done, b + 1)
                if before(b, 0, 1):
                    dve.wait_ge(steps_done, GT * b)
                dve.tensor_tensor(z_min[:, :, :], z_min[:, :, :], z_log[:, :, :], ALU.subtract).then_inc(log_sig_done, 1)
                dve.wait_ge(log_sig_done, b + 1)
                dve.tensor_scalar(decay[:, :, :], z_min[:, :, :], 1.0 / GLN, None, ALU.mult).then_inc(decay_made, 1)
                dve.wait_ge(decay_made, b + 1)
                dve.tensor_copy(decay_hi[:, :, :], decay[:, :, :]).then_inc(decay_hi_done, 1)
                dve.wait_ge(decay_hi_done, b + 1)
                dve.tensor_tensor(decay_lo[:, :, :], decay[:, :, :], decay_hi[:, :, :].bitcast(F32), ALU.subtract
                                  ).then_inc(decay_done, 1)

            def gaps(b, c):
                n = GT * b + c
                dve.wait_ge(cum_done, n + 1)
                dve.tensor_copy(cum_col[:, :], k_ps[:, COL:COL + NH]).then_inc(col_copied, 1)
                dve.wait_ge(col_copied, n + 1)
                dve.wait_ge(cum_copied, n + 1)
                if before(b, c, 1):
                    dve.wait_ge(k_fac_done, n)
                    dve.wait_ge(gap_exp_done, n)
                dve.tensor_tensor(k_gap[:, :], cum[:, :, P - 1], cum_col[:, :], ALU.subtract).then_inc(k_gap_done, 1)
                for h in range(NH):
                    last = dve.scalar_tensor_tensor(out=gap[:, h, :], in0=cum[:, h, :], scalar=cum_col[:, h:h + 1],
                                                    in1=causal[:, :], op0=ALU.subtract, op1=ALU.min)
                last.then_inc(gap_done, 1)

            def decayed(b, c):
                n = GT * b + c
                dve.wait_ge(cum_exp_done, n + 1)
                if c == 0:
                    dve.wait_ge(qk_copied, 4 * (b + 1))
                if before(b, c, 2):
                    dve.wait_ge(o_done, n - 1)
                for i in range(2):
                    rows = slice(DK * i, DK * i + DK)
                    last = dve.tensor_tensor(q_dec[rows, c % 2, :, :], q_pad[rows, :, i, c * P:(c + 1) * P],
                                             cum_exp[rows, c % 2, i:NH:2, :], ALU.mult)
                last.then_inc(q_dec_done, 1)
                dve.wait_ge(k_done, n + 1)
                dve.wait_ge(k_fac_done, n + 1)
                dve.tensor_tensor(k_dec[:, c % 2, :, :], k_ps[:, 0:NH * DK].rearrange("p (h d) -> p h d", h=NH),
                                  k_fac[:, :].unsqueeze(2).to_broadcast([P, NH, DK]), ALU.mult).then_inc(k_dec_done, 1)

            def mask(b, c):
                n = GT * b + c
                dve.wait_ge(score_done, n + 1)
                dve.wait_ge(gap_exp_done, n + 1)
                dve.tensor_tensor(score[:, c % 2, :, :], score_ps[:, :].rearrange("p (h t) -> p h t", h=NH),
                                  gap_exp[:, :, :], ALU.mult).then_inc(masked, 1)

            def swish(b, c):
                n = GT * b + c
                dve.wait_ge(tanh_done, n + 1)
                if before(b, c, 2):
                    dve.wait_ge(o_gated_done, n - 1)
                dve.scalar_tensor_tensor(out=gate[:, c % 2, :], in0=tanh_g[:, :], scalar=1.0, in1=g_ps[:, :],
                                         op0=ALU.add, op1=ALU.mult).then_inc(gated, 1)

            def update(b, c):
                n = GT * b + c
                dve.wait_ge(o_done, n + 1)
                if before(b, c, 1):
                    dve.wait_ge(state_done, states(*before(b, c, 1)))
                new = s_ps[:, :].rearrange("p (a i d) -> p a i d", a=2, i=2)
                for i in range(2):
                    rows = slice(DK * i, DK * i + DK)
                    if c == 0:
                        last = dve.tensor_copy(state[rows, :, i, :], new[rows, :, i, :])
                        continue
                    for a in range(2):
                        last = dve.scalar_tensor_tensor(out=state[rows, a, i, :], in0=state[rows, a, i, :],
                                                        scalar=cum_exp[rows, c % 2, 2 * a + i, P - 1:P],
                                                        in1=new[rows, a, i, :], op0=ALU.mult, op1=ALU.add)
                last.then_inc(state_done, 1)

            def square_sum(b, c):
                n = GT * b + c
                dve.wait_ge(sq_done, n + 1)
                if before(b, c, 1):
                    dve.wait_ge(mean_done, n)
                dve.tensor_reduce(o_sum[:, :], o_sq[:, :, :], AX_X, ALU.add).then_inc(sum_done, 1)

            def gate_out(b, c):
                n = GT * b + c
                dve.wait_ge(o_rstd_done, n + 1)
                if before(b, c, 1):
                    dve.wait_ge(oT_done, n)
                for h in range(NH):
                    cols = slice(h * DV, (h + 1) * DV)
                    last = dve.scalar_tensor_tensor(out=o_gated[:, cols], in0=o32[:, cols], scalar=o_rstd[:, h:h + 1],
                                                    in1=gate[:, c % 2, cols], op0=ALU.mult, op1=ALU.mult)
                last.then_inc(o_gated_done, 1)

            def out_low(b, c):
                n = GT * b + c
                dve.wait_ge(oT_hi_done, n + 1)
                dve.tensor_tensor(oT_lo[:, :], y_ps[:, :], oT_hi[:, :].bitcast(F32), ALU.subtract).then_inc(oT_split, 1)

            def add_out(b, c):
                n = GT * b + c
                dve.wait_ge(y_done, n + 1)
                xt = k.x[:, n, :]
                dve.tensor_tensor(xt, y_ps[:, 0:D], xt, ALU.add).then_inc(y_added, 1)

            def slot(b, c, more):
                mid, tail = before(b, c, 1), before(b, c, 2)
                if tail:
                    square_sum(*tail)
                if c and more > 1:
                    add_outputs(b + 2, (slice(0, 3), slice(3, 6), slice(6, 8))[c - 1])
                if c == 0:
                    logit(b)
                if c == 3 and more:
                    scale(b + 1, True)
                if tail:
                    gate_out(*tail)
                if c == 0:
                    log_sigmoid(b)
                    if more:
                        statistics(b + 1)
                    if tail:
                        out_low(*tail)
                gaps(b, c)
                decayed(b, c)
                if tail and c:
                    out_low(*tail)
                mask(b, c)
                swish(b, c)
                if mid and c:
                    update(*mid)
                if tail:
                    add_out(*tail)
                if c == 0 and more:
                    aggregate(b + 1)
                if c == 3 and more:
                    split(b + 1)

            def drain():
                for c in (GT - 2, GT - 1):
                    square_sum(B - 1, c)
                    gate_out(B - 1, c)
                    out_low(B - 1, c)
                    add_out(B - 1, c)

            add_outputs(0, slice(0, 8))
            statistics(0)
            aggregate(0)
            scale(0, False)
            dve.wait_ge(w_hi_done, 1)
            dve.tensor_tensor(w_lo[:, :, 0:512], w_in[:, :, 0:512], w_hi[:, :, 0:512].bitcast(F32), ALU.subtract).then_inc(w_ready, 1)
            split(0)
            dve.wait_ge(loaded, 64)
            for h in range(NH):
                last = dve.tensor_scalar(wo_scaled[:, h, :], wo_in[:, h, :], gnorm[:, 0:1], 0.5, ALU.mult, ALU.mult)
            last.then_inc(wo_scaled_done, 1)
            add_outputs(1, slice(0, 8))
            dve.wait_ge(const_ready, 2)
            schedule(dve, slot, drain)

        @block.scalar
        def _(act):
            def copy(b):
                act.wait_ge(turned, b + 1)
                if before(b, 0, 1):
                    act.wait_ge(gk_done, b)
                    act.wait_ge(split_done, b)
                act.activation(xT32[:, 0, :], v_ps[:, :], ACT.Copy)
                act.activation(xT32[:, 1, :], g_ps[:, :], ACT.Copy).then_inc(copied, 1)

            def log1p_exp(b):
                act.wait_ge(z_abs_done, b + 1)
                act.activation(z_exp[:, :, :], z_abs[:, :, :], ACT.Exp).then_inc(z_exp_done, 1)
                act.wait_ge(z_exp_done, b + 1)
                act.activation(z_log[:, :, :], z_exp[:, :, :], ACT.Ln, bias=1.0).then_inc(z_log_done, 1)

            def qk_copy(b):
                if before(b, 0, 1):
                    act.wait_ge(score_done, GT * b)
                    act.wait_ge(q_dec_done, GT * b)
                else:
                    act.wait_ge(const_ready, 2)
                for a, ps in enumerate((cum_ps, score_ps)):
                    act.wait_ge(qk_done, 4 * b + a + 1)
                    act.activation(kT[:, a, :], ps[:, :], ACT.Copy).then_inc(qk_copied, 1)
                for a, ps in enumerate((v_ps, g_ps)):
                    act.wait_ge(qk_done, 4 * b + a + 3)
                    act.activation(q_pad[0:DK, a, 0, :], ps[0:DK, :], ACT.Copy, scale=DK ** -0.5)
                    act.activation(q_pad[DK:P, a, 1, :], ps[DK:P, :], ACT.Copy, scale=DK ** -0.5).then_inc(qk_copied, 1)

            def front(b, c, tail):
                n = GT * b + c
                act.wait_ge(v_done, n + 1)
                if before(b, c, 2):
                    act.wait_ge(o_done, n - 1)
                act.activation(v32[:, c % 2, :], v_ps[:, :], ACT.Copy).then_inc(v_copied, 1)
                act.wait_ge(cum_done, n + 1)
                if before(b, c, 1):
                    act.wait_ge(gap_done, n)
                act.activation(cum[:, :, :], cum_ps[:, :].rearrange("p (h t) -> p h t", h=NH), ACT.Copy).then_inc(cum_copied, 1)
                act.wait_ge(cum_copied, n + 1)
                if before(b, c, 2):
                    act.wait_ge(state_done, states(*before(b, c, 2)))
                    act.wait_ge(q_dec_done, n - 1)
                act.activation(cum_exp[:, c % 2, :, :], cum[:, :, :], ACT.Exp).then_inc(cum_exp_done, 1)
                act.wait_ge(k_gap_done, n + 1)
                if before(b, c, 1):
                    act.wait_ge(k_dec_done, n)
                act.activation(k_fac[:, :], k_gap[:, :], ACT.Exp).then_inc(k_fac_done, 1)
                if tail:
                    out_high(*tail)
                act.wait_ge(gap_done, n + 1)
                if before(b, c, 1):
                    act.wait_ge(masked, n)
                act.activation(gap_exp[:, :, :], gap[:, :, :], ACT.Exp).then_inc(gap_exp_done, 1)
                act.wait_ge(g_done, n + 1)
                if before(b, c, 1):
                    act.wait_ge(gated, n)
                act.activation(tanh_g[:, :], g_ps[:, :], ACT.Tanh, scale=0.5).then_inc(tanh_done, 1)

            def out_copy(b, c):
                n = GT * b + c
                act.wait_ge(o_done, n + 1)
                if before(b, c, 1):
                    act.wait_ge(o_gated_done, n)
                    act.wait_ge(sum_done, n)
                act.activation(o32[:, :], o_ps[:, :], ACT.Copy).then_inc(o_copied, 1)
                act.wait_ge(o_copied, n + 1)
                act.activation(o_sq[:, :, :].rearrange("p h d -> p (h d)"), o32[:, :], ACT.Square).then_inc(sq_done, 1)

            def out_high(b, c):
                n = GT * b + c
                act.wait_ge(oT_done, n + 1)
                if before(b, c, 1):
                    act.wait_ge(y_done, n)
                act.activation(oT_hi[:, :], y_ps[:, :], ACT.Copy).then_inc(oT_hi_done, 1)

            def slot(b, c, more):
                tail = before(b, c, 2)
                if tail:
                    out_copy(*tail)
                if c == 0:
                    copy(b)
                    log1p_exp(b)
                    qk_copy(b)
                    if tail:
                        out_high(*tail)
                front(b, c, tail if c else None)

            def drain():
                for c in (GT - 2, GT - 1):
                    out_copy(B - 1, c)
                    out_high(B - 1, c)

            act.wait_ge(w_in_in[0], 32)
            act.activation(w_hi[:, :, 0:512], w_in[:, :, 0:512], ACT.Copy).then_inc(w_hi_done, 1)
            act.wait_ge(w_in_in[1], 32)
            act.activation(w_hi[:, :, 512:WALL], w_in[:, :, 512:WALL], ACT.Copy).then_inc(w_hi_done, 1)
            schedule(act, slot, drain)

        @block.tensor
        def _(pe):
            def product(out, pairs):
                for i, (w, x) in enumerate(pairs):
                    last = pe.matmul(out, w, x, start=(i == 0), stop=(i == len(pairs) - 1))
                return last

            def turn(b):
                pe.wait_ge(xn_done, b + 1)
                if before(b, 0, 1):
                    pe.wait_ge(v_copied, GT * b)
                    pe.wait_ge(gated, GT * b)
                for kd, ps in enumerate((v_ps, g_ps)):
                    for t in range(GT):
                        last = pe.transpose(ps[:, t * P:(t + 1) * P], xn[:, t, kd * P:(kd + 1) * P], k.ident[:, :])
                last.then_inc(turned, 1)

            def decay_logits(b):
                pe.wait_ge(copied, b + 1)
                if before(b, 0, 1):
                    pe.wait_ge(k_dec_done, GT * b)
                for t in range(GT):
                    last = product(k_ps[:, GK + NH * t:GK + NH * (t + 1)],
                                   [(xT32[:, kd, t * P:(t + 1) * P], wgk[:, kd, :]) for kd in range(KD)])
                last.then_inc(gk_done, 1)

            def qk(b):
                pe.wait_ge(split_done, b + 1)
                if before(b, 0, 1):
                    pe.wait_ge(cum_copied, GT * b)
                    pe.wait_ge(masked, GT * b)
                for ps, at in ((cum_ps, 256), (score_ps, 384), (v_ps, 0), (g_ps, 128)):
                    product(ps[:, :], [(w[:, kd, at:at + P], x[:, kd, :]) for kd in range(KD)
                                       for w, x in ((w_hi, xT_hi), (w_hi, xT_lo), (w_lo, xT_hi))]).then_inc(qk_done, 1)

            def rows(out, b, c, at, width):
                toks = slice(c * P, (c + 1) * P)
                return product(out, [(x[:, kd, toks], w[:, kd, at:at + width]) for kd in range(KD)
                                     for x, w in ((xT_hi, w_hi), (xT_hi, w_lo), (xT_lo, w_hi))])

            def front(b, c):
                n = GT * b + c
                if c:
                    pe.wait_ge(v_copied, n)
                else:
                    pe.wait_ge(qk_copied, 4 * (b + 1))
                if not before(b, c, 1):
                    pe.wait_ge(vg_w_ready, 1)
                rows(v_ps[:, :], b, c, 512, 512).then_inc(v_done, 1)
                if before(b, c, 1):
                    pe.wait_ge(k_dec_done, n)
                if c == 0:
                    pe.wait_ge(z_done, b + 1)
                for a in range(2):
                    last = pe.transpose(k_ps[:, a * P:(a + 1) * P], kT[:, a, c * P:(c + 1) * P], k.ident[:, :])
                last.then_inc(k_done, 1)
                pe.wait_ge(steps_done, n + 1)
                product(k_ps[:, COL:COL + NH], [(upto[:, :], decay[:, c, :])])
                if c:
                    pe.wait_ge(cum_copied, n)
                product(cum_ps[:, :], [(ones_hi[:, :], steps[:, c % 2, :, :].rearrange("p h t -> p (h t)"))
                                       for steps in (steps_hi, steps_lo)]).then_inc(cum_done, 1)
                if c:
                    pe.wait_ge(masked, n)
                for a in range(2):
                    last = product(score_ps[:, 256 * a:256 * a + 256],
                                   [(kT[:, a, c * P:(c + 1) * P], q_pad[:, a, :, c * P:(c + 1) * P])])
                last.then_inc(score_done, 1)
                if c:
                    pe.wait_ge(gated, n)
                rows(g_ps[:, :], b, c, 1024, 512).then_inc(g_done, 1)

            def mid(b, c):
                n = GT * b + c
                pe.wait_ge(v_copied, n + 1)
                pe.wait_ge(k_dec_done, n + 1)
                pe.wait_ge(masked, n + 1)
                if before(b, c, 1):
                    pe.wait_ge(state_done, states(*before(b, c, 1)))
                    pe.wait_ge(o_copied, n)
                if c < GT - 1:
                    for a in range(2):
                        last = product(s_ps[:, 256 * a:256 * a + 256],
                                       [(k_dec[:, c % 2, 2 * a:2 * a + 2, :].rearrange("p h d -> p (h d)"),
                                         v32[:, c % 2, 256 * a:256 * a + 256])])
                    last.then_inc(s_done, 1)
                for a in range(2):
                    if c:
                        pe.matmul(o_ps[:, 256 * a:256 * a + 256], q_dec[:, c % 2, a, :],
                                  state[:, a, :, :].rearrange("p i d -> p (i d)"), start=True, stop=True,
                                  skip_group_check=True)
                    for h in (2 * a, 2 * a + 1):
                        cols = slice(h * DV, (h + 1) * DV)
                        last = pe.matmul(o_ps[:, cols], score[:, c % 2, h, :], v32[:, c % 2, cols],
                                         start=(c == 0), stop=True, skip_group_check=True)
                last.then_inc(o_done, 1)

            def turn_out(b, c):
                n = GT * b + c
                pe.wait_ge(o_gated_done, n + 1)
                if before(b, c, 1):
                    pe.wait_ge(y_added, n)
                for h in range(NH):
                    last = pe.transpose(y_ps[:, h * P:(h + 1) * P], o_gated[:, h * DV:(h + 1) * DV], k.ident[:, :])
                last.then_inc(oT_done, 1)

            def project(b, c):
                if not before(b, c, 1):
                    pe.wait_ge(wo_ready, 1)
                pe.wait_ge(oT_split, GT * b + c + 1)
                product(y_ps[:, 0:D], [(o[:, h * P:(h + 1) * P], w[:, h, :]) for h in range(NH)
                                       for o, w in ((oT_hi, wo_hi), (oT_hi, wo_lo), (oT_lo, wo_hi))]).then_inc(y_done, 1)

            def slot(b, c, more):
                m, tail = before(b, c, 1), before(b, c, 2)
                if c == 0:
                    if m:
                        mid(*m)
                    decay_logits(b)
                    qk(b)
                    if m:
                        turn_out(*tail)
                    front(b, 0)
                    if m:
                        project(*tail)
                    return
                front(b, c)
                if tail:
                    turn_out(*tail)
                mid(*m)
                if tail:
                    project(*tail)
                if c == 3 and more:
                    turn(b + 1)

            def drain():
                mid(B - 1, GT - 1)
                for c in (GT - 2, GT - 1):
                    turn_out(B - 1, c)
                    project(B - 1, c)

            turn(0)
            pe.wait_ge(w_ready, 1)
            pe.wait_ge(loaded, 64)
            pe.wait_ge(const_ready, 2)
            pe.wait_ge(ones_done, 1)
            schedule(pe, slot, drain)


def store(nc, k, dram):
    with ExitStack() as ctx:
        stored = ctx.enter_context(nc.semaphore("stored"))
        block = ctx.enter_context(nc.Block())
        rows = dram["out"].rearrange("b n d -> (b n) d").rearrange("(t p) d -> p t d", p=P)

        @block.sync
        def _(sp):
            for g in range(4):
                sp.dma_start(rows[:, 8 * g:8 * g + 8, :], k.x[:, 8 * g:8 * g + 8, :]).then_inc(stored, 16)
            sp.wait_ge(stored, 64)


def macaron(nc, dram, parts=("ffn1", "attn", "ffn2")):
    k = Core()
    with ExitStack() as ctx:
        def sb(n, shape, dt=F32):
            return ctx.enter_context(nc.sbuf_tensor(n, shape, dt))

        k.x = sb("x", [P, TILES, D])
        k.ident = sb("ident", [P, P])
        k.neg_half = sb("neg_half", [P, GT])
        k.router_w = sb("router_w", [P, KD, E])
        k.router_b = sb("router_b", [P, E])
        k.b1 = sb("b1", [P, NX, KH])
        k.half_sb2 = sb("half_sb2", [P, D])
        k.job_b1 = sb("job_b1", [P, JOBS, KH])
        k.pair_rows = sb("pair_rows", [P, TOP, TILES])
        k.gate = sb("gate", [P, TILES, NX])
        k.ones = sb("ones", [P, P])
        k.zero_rows = sb("zero_rows", [P, SLOTS // P, ROW])
        k.earlier = sb("earlier", [P, P])
        k.lower = sb("lower", [P, E, E])
        k.job_starts = sb("job_starts", [P, T // SLOTS])
        k.expert_numbers = sb("expert_numbers", [P, E])
        k.job_numbers = sb("job_numbers", [P, JOBS])
        k.slot_ids = sb("slot_ids", [P, TOP, TILES], mybir.dt.uint32)
        k.pair_gate = sb("pair_gate", [P, TOP, TILES])
        k.job_expert = sb("job_expert", [P, JOBS], mybir.dt.int32)
        k.slots_zeroed = ctx.enter_context(nc.semaphore("slots_zeroed"))
        dram["slot_x"] = nc.dram_tensor("slot_x", (JOBS * SLOTS, ROW), F32, kind="Internal").ap()
        dram["slot_y"] = nc.dram_tensor("slot_y", (TOP * T + SLOTS, D), F32, kind="Internal").ap()
        k.passed = ctx.enter_context(nc.semaphore("passed"))
        k.x_in = [ctx.enter_context(nc.semaphore(f"x_in{g}")) for g in range(4)]
        k.ffns = 0
        constants(nc, k, dram)
        for part in parts:
            if part == "attn":
                attention(nc, k, dram)
                continue
            with nc.cleanup_on_exit():
                with ExitStack() as phase:
                    k.xn = phase.enter_context(nc.sbuf_tensor(f"{part}_xn", [P, TILES, ROW], F32))
                    k.xT_hi = phase.enter_context(nc.sbuf_tensor(f"{part}_xT_hi", [P, KD, T], F32R))
                    k.xT_lo = phase.enter_context(nc.sbuf_tensor(f"{part}_xT_lo", [P, KD, T], F32R))
                    w = Weights(nc, phase, part)
                    k.ffns += 1
                    ffn(nc, k, dram, w, part)
                if part == parts[-1]:
                    combine(nc, k, dram, f"{part}_combine", True)
        if parts[-1] == "attn":
            store(nc, k, dram)


_INS = {"L0_attn_x": "x", "L0_attn_Wq": "Wq", "L0_attn_Wk": "Wk", "L0_attn_Wv": "Wv", "L0_attn_Wg": "Wg",
        "L0_attn_Wgk": "Wgk", "L0_attn_bgk": "bgk", "L0_attn_Wo": "Wo", "L0_attn_gnorm_w": "gnorm_w",
        "L0_ffn_router_w": "router_w", "L0_ffn_router_b": "router_b", "L0_ffn_sw1": "sw1", "L0_ffn_sb1": "sb1",
        "L0_ffn_sw2": "sw2", "L0_ffn_sb2": "sb2", "L0_ffn_rw1": "rw1", "L0_ffn_rb1": "rb1", "L0_ffn_rw2": "rw2",
        "L0_ffn_rb2": "rb2"}


def kernel(**inputs):
    import numpy as _np
    import concourse.bacc as _bacc
    from concourse import mybir as _mybir
    from concourse.bass_utils import run_bass_kernel_spmd as _run

    nc = _bacc.Bacc("TRN2", target_bir_lowering=False, num_devices=1)
    arrays, dram = {}, {}
    for name, short in _INS.items():
        a = _np.ascontiguousarray(inputs[name])
        arrays[f"in_{short}"] = a
        dram[short] = nc.dram_tensor(f"in_{short}", a.shape, _mybir.dt.from_np(a.dtype), kind="ExternalInput").ap()
    shape = inputs["L0_attn_x"].shape
    dram["out"] = nc.dram_tensor("out_x", shape, _mybir.dt.float32, kind="ExternalOutput").ap()
    macaron(nc, dram)
    r = _run(nc, [arrays], core_ids=[0])
    return r.results[0]["out_x"]
```
